# Optimizing a Trainium2 kernel written in Bass

```python
import numpy as np
import jax
import jax.numpy as jnp

def _softmax(x, axis=-1):
    return jax.nn.softmax(x, axis=axis)

def _gelu(x):
    return jax.nn.gelu(x, approximate=True)

def _silu(x):
    return jax.nn.silu(x)

def _sigmoid(x):
    return jax.nn.sigmoid(x)

def _layernorm(x, axis=-1, eps=1e-05):
    m = jnp.mean(x, axis=axis, keepdims=True)
    v = jnp.var(x, axis=axis, keepdims=True)
    return (x - m) / jnp.sqrt(v + eps)

def _scatter_add(tgt, idx, src, axis=0):
    return tgt.at[idx].add(src)

def _segment_sum(src, seg, n):
    return jax.ops.segment_sum(src, seg, n)
kernel_name = 'mk_flamingo_gated_d2_seqx_r4_af06a6'

def setup_inputs(seed: int=0):
    np.random.seed(seed)
    _w = jnp.asarray

    def _rec_inputs():
        import jax
        import jax.numpy as jnp
        _rk = jax.random.key(seed)
        x = -0.0003929 + 0.9999 * jax.random.normal(jax.random.fold_in(_rk, 1), (2, 1024, 256), jnp.float32)
        _lenS = 1024 - jax.random.randint(jax.random.fold_in(_rk, 7), (2,), 0, max(1, 1024 // 4) + 1, jnp.int32)
        _lenS2 = 77 - jax.random.randint(jax.random.fold_in(_rk, 8), (2,), 0, max(1, 77 // 4) + 1, jnp.int32)
        _ctx_2048P = jax.random.normal(jax.random.fold_in(_rk, 11), (2, 16, 512), jnp.float32)
        _ctx_2048c = jax.random.dirichlet(jax.random.fold_in(_rk, 511), 0.3 * jnp.ones((16,), jnp.float32), (2, 77))
        _ctx_2048t = jnp.einsum('bsk,bkd->bsd', _ctx_2048c, _ctx_2048P)
        _ctx_2048t = _ctx_2048t * jax.lax.rsqrt(jnp.mean(jnp.square(_ctx_2048t)) + 1e-12) * 0.953939
        ctx_2048 = 4.13588e-05 + 0.999923 * (_ctx_2048t + 0.3 * jax.random.normal(jax.random.fold_in(_rk, 611), (2, 77, 512), jnp.float32))
        _validS = jnp.arange(1024)[None, :] < _lenS[:, None]
        _validS2 = jnp.arange(77)[None, :] < _lenS2[:, None]
        _causal = jnp.tril(jnp.ones((1024, 1024), dtype=bool))
        mask_BxS2_if0 = jnp.where(jnp.ones((2, 77), dtype=bool), 4, 0).astype(jnp.int32)
        _g = jax.random.normal(jax.random.fold_in(_rk, 9001), (2, 2), jnp.float32)
        _g = jnp.sign(_g) * jnp.maximum(jnp.abs(_g), 1.0) + (_g == 0) * 1.0
        g_xattn = _g[0]
        g_ffn = _g[1]
        return (x, ctx_2048, mask_BxS2_if0, g_xattn, g_ffn)
    x, ctx_2048, mask_BxS2_if0, g_xattn, g_ffn = _rec_inputs()

    def _L0_xattn_setup():
        import jax, jax.numpy as jnp
        import numpy as np
        B, L, P = (4, 1024, 256)
        D_MODEL = 256
        D_GLOBAL = 512
        HEADDIM = 32
        EPSILON = 0.001
        RMS_EPS = 1e-05

        def rmsnorm(x, g, eps=RMS_EPS):
            var = jnp.mean(jnp.square(x), axis=-1, keepdims=True)
            return x * jax.lax.rsqrt(var + eps) * g

        def _hnet_depool(h, h_patch_full, patch_lens):
            h_patch = h_patch_full[..., :D_MODEL]
            bsz, plen = (h_patch.shape[0], h_patch.shape[1])
            seqlen = h.shape[1]
            logp = jnp.full((bsz, plen), -EPSILON, dtype=jnp.float32)
            bidx = jnp.cumsum(patch_lens, axis=1) - 1
            boundary_mask = jnp.zeros((bsz, seqlen), dtype=jnp.int32)
            boundary_mask = boundary_mask.at[jnp.arange(bsz)[:, None], bidx].set(1)
            dt = (-jnp.log(-jnp.expm1(logp))).astype(h_patch.dtype)
            x = h_patch / dt[..., None]
            n_heads = D_MODEL // HEADDIM
            A = -jnp.ones((n_heads,), dtype=jnp.float32)
            bcoef = jnp.exp(logp).astype(h_patch.dtype)
            x4 = x.reshape(bsz, plen, n_heads, HEADDIM)
            a = jnp.exp(dt[:, :, None] * A[None, None, :])
            u = (dt * bcoef)[:, :, None, None] * x4
            a_b = jnp.broadcast_to(a[..., None], u.shape)

            def comb(lft, rgt):
                aL, uL = lft
                aR, uR = rgt
                return (aL * aR, uL * aR + uR)
            _, s = jax.lax.associative_scan(comb, (a_b, u), axis=1)
            depool = s.reshape(bsz, plen, D_MODEL)
            plug = jnp.clip(jnp.cumsum(boundary_mask, axis=1) - 1, 0, plen - 1)
            depool_out = depool[jnp.arange(bsz)[:, None], plug]
            return depool_out + h
        key = jax.random.key(seed)
        k1, k2, k3, k4 = jax.random.split(key, 4)
        embeds = jax.random.normal(k1, (B, L, D_MODEL), dtype=jnp.float32)
        patch_embeds = jax.random.normal(k2, (B, P, D_GLOBAL), dtype=jnp.float32)
        patch_lens = jnp.full((B, P), L // P, dtype=jnp.int64)
        W_in = jax.random.normal(k3, (D_MODEL, D_MODEL), dtype=jnp.float32) * 0.02
        b_in = jnp.zeros((D_MODEL,), dtype=jnp.float32)
        g_res = jnp.ones((D_MODEL,), dtype=jnp.float32)
        g_init = jnp.ones((D_GLOBAL,), dtype=jnp.float32)
        return {'embeds': embeds, 'patch_embeds': patch_embeds, 'patch_lens': patch_lens, 'W_in': W_in, 'b_in': b_in, 'g_res': g_res, 'g_init': g_init}
    _L0_xattn_all = _L0_xattn_setup()
    _L0_xattn_in = {k: v for k, v in _L0_xattn_all.items() if k in ('W_in', 'b_in', 'g_res', 'g_init')}
    del _L0_xattn_all

    def _L0_ffn_setup():
        import jax, jax.numpy as jnp
        import numpy as np
        NEG_INF = jnp.float32(-1000000000.0)

        def _router(x, Wr, br, top_k=2):
            logits = jnp.einsum('bsd,de->bse', x, Wr) + br
            _, top_idx = jax.lax.top_k(logits, top_k)
            num_experts = logits.shape[-1]
            mask = jnp.any(top_idx[..., None] == jnp.arange(num_experts), axis=-2)
            sparse_logits = jnp.where(mask, logits, NEG_INF)
            weights = jax.nn.softmax(sparse_logits, axis=-1)
            return (weights, top_idx, mask)
        key = jax.random.key(seed)
        ks = jax.random.split(key, 8)
        B, S, D, E, H = (4, 512, 256, 8, 1024)
        sd = 1.0 / np.sqrt(D)
        sh = 1.0 / np.sqrt(H)
        x = jax.random.normal(ks[0], (B, S, D), dtype=jnp.float32)
        Wr = jax.random.normal(ks[1], (D, E), dtype=jnp.float32) * sd
        br = jnp.zeros((E,), dtype=jnp.float32)
        W1 = jax.random.normal(ks[2], (E, D, H), dtype=jnp.float32) * sd
        b1 = jnp.zeros((E, H), dtype=jnp.float32)
        W2 = jax.random.normal(ks[3], (E, H, D), dtype=jnp.float32) * sh
        b2 = jnp.zeros((E, D), dtype=jnp.float32)
        return {'x': x, 'Wr': Wr, 'br': br, 'W1': W1, 'b1': b1, 'W2': W2, 'b2': b2}
    _L0_ffn_all = _L0_ffn_setup()
    _L0_ffn_in = {k: v for k, v in _L0_ffn_all.items() if k in ('Wr', 'br', 'W1', 'b1', 'W2', 'b2')}
    del _L0_ffn_all

    def _L1_xattn_setup():
        import jax, jax.numpy as jnp
        import numpy as np
        NUM_HEADS = 16
        key = jax.random.key(seed)
        ks = jax.random.split(key, 5)
        dim = 256
        B, N, N_c = (4, 256, 64)
        x = jax.random.normal(ks[0], (B, N, dim), dtype=jnp.float32)
        context = jax.random.normal(ks[1], (B, N_c, 2 * dim), dtype=jnp.float32)
        w_qkv = jax.random.normal(ks[2], (3 * dim, dim), dtype=jnp.float32) * 0.02
        w_proj = jax.random.normal(ks[3], (dim, dim), dtype=jnp.float32) * 0.02
        b_proj = jax.random.normal(ks[4], (dim,), dtype=jnp.float32) * 0.02
        return {'x': x, 'context': context, 'w_qkv': w_qkv, 'w_proj': w_proj, 'b_proj': b_proj}
    _L1_xattn_all = _L1_xattn_setup()
    _L1_xattn_in = {k: v for k, v in _L1_xattn_all.items() if k in ('w_qkv', 'w_proj', 'b_proj')}
    del _L1_xattn_all

    def _L1_ffn_setup():
        import jax, jax.numpy as jnp
        import numpy as np
        E = 32
        K = 4
        H = 256
        I = 192
        ROUTED_SCALING_FACTOR = 1.0
        key = jax.random.key(seed)
        k0, k1, k2, k3, k4, k5 = jax.random.split(key, 6)
        return {'hidden_states': jax.random.normal(k0, (1, 512, H), jnp.float32), 'gate_w': jax.random.normal(k1, (E, H), jnp.float32) * 0.02, 'w1': jax.random.normal(k2, (E, H, I), jnp.float32) * 0.02, 'w3': jax.random.normal(k3, (E, H, I), jnp.float32) * 0.02, 'w2': jax.random.normal(k4, (E, I, H), jnp.float32) * 0.02, 'e_bias': jax.random.normal(k5, (E,), jnp.float32) * 0.02}
    _L1_ffn_all = _L1_ffn_setup()
    _L1_ffn_in = {k: v for k, v in _L1_ffn_all.items() if k in ('gate_w', 'w1', 'w3', 'w2', 'e_bias')}
    del _L1_ffn_all
    return {'x': x, 'ctx_2048': ctx_2048, 'mask_BxS2_if0': mask_BxS2_if0, 'g_xattn': g_xattn, 'g_ffn': g_ffn, 'L0_xattn_W_in': _L0_xattn_in['W_in'], 'L0_xattn_b_in': _L0_xattn_in['b_in'], 'L0_xattn_g_res': _L0_xattn_in['g_res'], 'L0_xattn_g_init': _L0_xattn_in['g_init'], 'L0_ffn_Wr': _L0_ffn_in['Wr'], 'L0_ffn_br': _L0_ffn_in['br'], 'L0_ffn_W1': _L0_ffn_in['W1'], 'L0_ffn_b1': _L0_ffn_in['b1'], 'L0_ffn_W2': _L0_ffn_in['W2'], 'L0_ffn_b2': _L0_ffn_in['b2'], 'L1_xattn_w_qkv': _L1_xattn_in['w_qkv'], 'L1_xattn_w_proj': _L1_xattn_in['w_proj'], 'L1_xattn_b_proj': _L1_xattn_in['b_proj'], 'L1_ffn_gate_w': _L1_ffn_in['gate_w'], 'L1_ffn_w1': _L1_ffn_in['w1'], 'L1_ffn_w3': _L1_ffn_in['w3'], 'L1_ffn_w2': _L1_ffn_in['w2'], 'L1_ffn_e_bias': _L1_ffn_in['e_bias']}

def reference(x, ctx_2048, mask_BxS2_if0, g_xattn, g_ffn, L0_xattn_W_in, L0_xattn_b_in, L0_xattn_g_res, L0_xattn_g_init, L0_ffn_Wr, L0_ffn_br, L0_ffn_W1, L0_ffn_b1, L0_ffn_W2, L0_ffn_b2, L1_xattn_w_qkv, L1_xattn_w_proj, L1_xattn_b_proj, L1_ffn_gate_w, L1_ffn_w1, L1_ffn_w3, L1_ffn_w2, L1_ffn_e_bias):
    import jax
    import jax.numpy as jnp

    def _L0_xattn_ref(embeds, patch_embeds, patch_lens, W_in, b_in, g_res, g_init):
        import jax, jax.numpy as jnp
        import numpy as np
        B, L, P = (4, 1024, 256)
        D_MODEL = 256
        D_GLOBAL = 512
        HEADDIM = 32
        EPSILON = 0.001
        RMS_EPS = 1e-05

        def rmsnorm(x, g, eps=RMS_EPS):
            var = jnp.mean(jnp.square(x), axis=-1, keepdims=True)
            return x * jax.lax.rsqrt(var + eps) * g

        def _hnet_depool(h, h_patch_full, patch_lens):
            h_patch = h_patch_full[..., :D_MODEL]
            bsz, plen = (h_patch.shape[0], h_patch.shape[1])
            seqlen = h.shape[1]
            logp = jnp.full((bsz, plen), -EPSILON, dtype=jnp.float32)
            bidx = jnp.cumsum(patch_lens, axis=1) - 1
            boundary_mask = jnp.zeros((bsz, seqlen), dtype=jnp.int32)
            boundary_mask = boundary_mask.at[jnp.arange(bsz)[:, None], bidx].set(1)
            dt = (-jnp.log(-jnp.expm1(logp))).astype(h_patch.dtype)
            x = h_patch / dt[..., None]
            n_heads = D_MODEL // HEADDIM
            A = -jnp.ones((n_heads,), dtype=jnp.float32)
            bcoef = jnp.exp(logp).astype(h_patch.dtype)
            x4 = x.reshape(bsz, plen, n_heads, HEADDIM)
            a = jnp.exp(dt[:, :, None] * A[None, None, :])
            u = (dt * bcoef)[:, :, None, None] * x4
            a_b = jnp.broadcast_to(a[..., None], u.shape)

            def comb(lft, rgt):
                aL, uL = lft
                aR, uR = rgt
                return (aL * aR, uL * aR + uR)
            _, s = jax.lax.associative_scan(comb, (a_b, u), axis=1)
            depool = s.reshape(bsz, plen, D_MODEL)
            plug = jnp.clip(jnp.cumsum(boundary_mask, axis=1) - 1, 0, plen - 1)
            depool_out = depool[jnp.arange(bsz)[:, None], plug]
            return depool_out + h
        h = rmsnorm(embeds, g_res)
        h = jnp.einsum('bld,ed->ble', h, W_in) + b_in
        h_patch = rmsnorm(patch_embeds, g_init)
        return _hnet_depool(h, h_patch, patch_lens)

    def _L0_ffn_ref(x, Wr, br, W1, b1, W2, b2):
        import jax, jax.numpy as jnp
        import numpy as np
        NEG_INF = jnp.float32(-1000000000.0)

        def _router(x, Wr, br, top_k=2):
            logits = jnp.einsum('bsd,de->bse', x, Wr) + br
            _, top_idx = jax.lax.top_k(logits, top_k)
            num_experts = logits.shape[-1]
            mask = jnp.any(top_idx[..., None] == jnp.arange(num_experts), axis=-2)
            sparse_logits = jnp.where(mask, logits, NEG_INF)
            weights = jax.nn.softmax(sparse_logits, axis=-1)
            return (weights, top_idx, mask)
        weights, top_idx, mask = _router(x, Wr, br, top_k=2)
        num_experts = W1.shape[0]
        out = jnp.zeros_like(x)
        for e in range(num_experts):
            h = jax.nn.relu(jnp.einsum('bsd,dh->bsh', x, W1[e]) + b1[e])
            y = jnp.einsum('bsh,hd->bsd', h, W2[e]) + b2[e]
            w = weights[:, :, e] * mask[:, :, e].astype(x.dtype)
            out = out + y * w[:, :, None]
        return out

    def _L1_xattn_ref(x, context, w_qkv, w_proj, b_proj):
        import jax, jax.numpy as jnp
        import numpy as np
        NUM_HEADS = 16
        B, N, C = x.shape
        H = NUM_HEADS
        D = C // H
        scale = D ** (-0.5)
        qkv = (x @ w_qkv.T).reshape(B, N, 3, H, D).transpose(2, 0, 3, 1, 4)
        q, k, v = (qkv[0], qkv[1], qkv[2])
        N_c = context.shape[1]
        kv = context.reshape(B, N_c, 2, H, D).transpose(2, 0, 3, 1, 4)
        extra_k, extra_v = (kv[0], kv[1])
        k = jnp.concatenate([extra_k, k], axis=2)
        v = jnp.concatenate([extra_v, v], axis=2)
        dtype = q.dtype
        attn = jnp.einsum('bhnd,bhmd->bhnm', q * scale, k).astype(jnp.float32)
        attn = jax.nn.softmax(attn, axis=-1).astype(dtype)
        out = jnp.einsum('bhnm,bhmd->bhnd', attn, v)
        out = out.transpose(0, 2, 1, 3).reshape(B, N, C)
        return out @ w_proj.T + b_proj

    def _L1_ffn_ref(hidden_states, gate_w, w1, w3, w2, e_bias):
        import jax, jax.numpy as jnp
        import numpy as np
        E = 32
        K = 4
        H = 256
        I = 192
        ROUTED_SCALING_FACTOR = 1.0
        orig_shape = hidden_states.shape
        x = hidden_states.reshape(-1, orig_shape[-1])
        T = x.shape[0]
        router_logits = x @ gate_w.T
        scores = jax.nn.sigmoid(router_logits.astype(jnp.float32))
        _, topk_ids = jax.lax.top_k(scores + e_bias[None, :], K)
        topk_w = jnp.take_along_axis(scores, topk_ids, axis=1)
        topk_w = topk_w / jnp.sum(topk_w, axis=1, keepdims=True)
        combine = jnp.zeros((T, E), jnp.float32).at[jnp.arange(T)[:, None], topk_ids].add(topk_w)
        g = jnp.einsum('th,ehi->tei', x, w1)
        u = jnp.einsum('th,ehi->tei', x, w3)
        a = jax.nn.silu(g) * u * combine[:, :, None].astype(x.dtype)
        out = jnp.einsum('tei,eih->th', a, w2)
        out = out * ROUTED_SCALING_FACTOR
        return out.reshape(orig_shape)
    x = x + jnp.tanh(g_xattn[0]) * _L0_xattn_ref(_layernorm(x, axis=-1), ctx_2048, mask_BxS2_if0, L0_xattn_W_in, L0_xattn_b_in, L0_xattn_g_res, L0_xattn_g_init)
    x = x + jnp.tanh(g_ffn[0]) * _L0_ffn_ref(_layernorm(x, axis=-1), L0_ffn_Wr, L0_ffn_br, L0_ffn_W1, L0_ffn_b1, L0_ffn_W2, L0_ffn_b2)
    x = x + jnp.tanh(g_xattn[1]) * _L1_xattn_ref(_layernorm(x, axis=-1), ctx_2048, L1_xattn_w_qkv, L1_xattn_w_proj, L1_xattn_b_proj)
    x = x + jnp.tanh(g_ffn[1]) * _L1_ffn_ref(_layernorm(x, axis=-1), L1_ffn_gate_w, L1_ffn_w1, L1_ffn_w3, L1_ffn_w2, L1_ffn_e_bias)
    return x

_drawn_inputs = setup_inputs


def setup_inputs(seed=0):
    import zlib

    import numpy as np

    out = dict(_drawn_inputs(seed))
    spreads = {'g_ffn': (-1.0, 0.6),
     'L0_xattn_b_in': (0.0, 0.1),
     'L0_xattn_g_res': (1.0, 0.2),
     'L0_xattn_g_init': (1.0, 0.2),
     'L0_ffn_br': (0.0, 0.1),
     'L0_ffn_b1': (0.0, 0.27),
     'L0_ffn_b2': (0.0, 0.1)}
    factors = {'L1_xattn_b_proj': 4.247,
     'L1_ffn_gate_w': 8.0,
     'L1_ffn_w1': 8.0,
     'L1_ffn_w3': 8.0,
     'L1_ffn_w2': 8.0,
     'L1_ffn_e_bias': 8.0}
    for name, (base, spread) in spreads.items():
        noise = np.random.default_rng([zlib.crc32(name.encode()), seed]).standard_normal(out[name].shape)
        drawn = base * np.exp(spread * noise) if base else spread * noise
        out[name] = jnp.asarray(drawn.astype(out[name].dtype))
    for name, factor in factors.items():
        out[name] = (out[name] * factor).astype(out[name].dtype)
    return out
```

```python
from contextlib import ExitStack, contextmanager

import numpy as np
import concourse.bass as bass
from concourse import mybir

F32 = mybir.dt.float32
BF16 = mybir.dt.bfloat16
U32 = mybir.dt.uint32
I32 = mybir.dt.int32
ALU = mybir.AluOpType
ACT = mybir.ActivationFunctionType
AX = mybir.AxisListType

P = 128
B, S, D = 2, 1024, 256
DK = D // P
NTOK = B * S
NTILE = NTOK // P
TPB = S // P
CL, CD = 77, 512
HB = 512

E0, K0, H0 = 8, 2, 1024
HK0 = H0 // P
E1, K1, I1 = 32, 4, 192
IH = I1 // 2
NT0 = (NTOK * K0 - E0) // P + E0
NT1 = (NTOK * K1 - E1) // P + E1
RING0, RING1 = 3, 4

HEADS, HD = 16, D // 16
GH = 4
NGRP = B * HEADS // GH
KEYS = CL + S
MT = 1 + TPB
QB = (0, 0, 1, 1, 0, 2)
KB = (0, 1, 0, 1, 2, 0)
QROWS = len(QB) * HD
AROWS = QROWS + 3

LN_EPS = 1e-5
RMS_EPS = 1e-5
PATCH_EPS = 1e-3

W1_0, W2_0 = 0, E0 * DK * H0 * 4
ARENA0_END = W2_0 + E0 * HK0 * D * 4
W13_BYTES = DK * 2 * I1 * 4
W2_1 = E1 * W13_BYTES
ARENA = W2_1 + E1 * 2 * D * 4
TOP = ARENA - (DK * D + D + DK * E1) * 4
EARLY = 26
ATT0 = EARLY * W13_BYTES


class Memory:
    pass


class Chain:

    def __init__(self, eng, sem):
        self.eng, self.sem, self.base, self.k, self.it, self.per = eng, sem, 0, 0, None, 0

    def __call__(self, ins):
        self.k += 1
        ins.then_inc(self.sem, 1)
        at = self.base + self.k
        self.eng.wait_ge(self.sem, at if self.it is None else self.it * self.per + at)

    @contextmanager
    def turns(self, it, per, times):
        self.base, self.k, self.it, self.per = self.base + self.k, 0, it, per
        yield
        assert self.k == per, (self.k, per)
        self.base, self.k, self.it = self.base + per * times, 0, None


def tile_loop(eng, n, ring, body):
    for j in range(ring + 1):
        body(j, j % ring, j // ring, j == 0, False)
    turns = (n - 2 - ring) // ring
    with eng.Fori(1, 1 + turns) as t:
        for u in range(ring):
            body(t * ring + (1 + u), (1 + u) % ring, t + (1 + u) // ring, False, False)
    for j in range(1 + ring + turns * ring, n):
        body(j, j % ring, j // ring, False, j == n - 1)


def moments(ch, nc, stats, n, mean, var, ve, tmp, eps):
    v = nc.vector
    v.tensor_tensor(tmp[0], stats[:, :, 1], stats[:, :, 4], ALU.add)
    v.tensor_tensor(tmp[1], stats[:, :, 1], stats[:, :, 4], ALU.subtract)
    ch(v.tensor_tensor(tmp[2], stats[:, :, 2], stats[:, :, 5], ALU.add))
    v.tensor_scalar(mean, tmp[0], 0.5, None, ALU.mult)
    ch(v.tensor_tensor(tmp[3], tmp[1], tmp[1], ALU.mult))
    ch(v.tensor_scalar(tmp[2], tmp[2], 1.0 / n, None, ALU.mult))
    ch(v.scalar_tensor_tensor(var, tmp[3], 0.25, tmp[2], ALU.mult, ALU.add))
    ch(v.tensor_scalar(ve, var, eps, None, ALU.add))


def make_env(nc, ctx, a, out):
    e = Memory()
    e.nc, e.a, e.out = nc, a, out

    def sb(name, shape, dt=F32):
        return ctx.enter_context(nc.sbuf_tensor(name, shape, dt))

    e.used = []

    def new_semaphore(name):
        e.used.append(nc.alloc_semaphore(name=name))
        return e.used[-1]

    e.sem = new_semaphore
    e.w0_in, e.w13_in, e.w2_in = (ctx.enter_context(nc.semaphore(n)) for n in ("w0_in", "w13_in", "w2_in"))
    e.x = sb("x_resident", [P, NTILE, D])
    e.arena = sb("arena", [P, ARENA // 4])
    e.scr = sb("scratch", [P, NTILE * D])
    e.ident = sb("ident", [P, P])
    e.identb = sb("identb", [P, P], BF16)
    e.earlier = sb("earlier", [P, P], BF16)
    e.onesb = sb("onesb", [P, P], BF16)
    e.iota = sb("iota", [P, P])
    e.iota_p = sb("iota_p", [P, 1])
    e.steps = sb("steps", [P, NTILE])
    e.stats = sb("stats", [P, NTILE, 6])
    e.mean = sb("mean", [P, NTILE])
    e.rstd = sb("rstd", [P, NTILE])
    e.var = sb("var", [P, NTILE])
    e.ve = sb("ve", [P, NTILE])
    e.std = sb("std", [P, NTILE])
    e.tmp = sb("ln_tmp", [P, 4, NTILE])
    e.tg = sb("tanh_gates", [P, 4])
    e.ebias = sb("ebias", [P, E1])
    e.expert = sb("expert", [1, P], I32)
    e.slot_u = sb("slot_u", [P, NTILE, K1], U32)
    e.token_u = sb("token_u", [P, NT1], U32)
    e.gate = sb("gate", [P, NTILE, K1])
    e.xg = sb("xg", [P, RING1, D])
    e.ysb = sb("ysb", [P, RING1, D])
    e.icol = sb("icol", [P, 4, K1], U32)
    e.ps = ctx.enter_context(nc.psum_tensor("ps", [P, 8, HB], F32))

    def dram(name, shape, dt=F32):
        return nc.dram_tensor(name, shape, dt, kind="Internal").ap()

    e.xn = [dram("xn0", [NTOK, D]), dram("xn1", [NTOK, D])]
    e.y = [dram("y0", [NT0 * P, D]), dram("y1", [NT1 * P, D])]
    e.qp = dram("q_parts", [3, D, NTOK], BF16)
    e.kp = dram("k_parts", [3, D, B, KEYS], BF16)

    def carve(off, shape, dt=F32, base=e.arena):
        n = int(np.prod(shape))
        words = n * (2 if dt == BF16 else 4) // 4
        v = base[:].rearrange("p a b -> p (a b)") if len(base.shape) == 3 else base[:]
        v = v[:, off // 4: off // 4 + words]
        if dt != F32:
            v = v.bitcast(dt)
        if len(shape) == 2:
            v = v.rearrange("p (a b) -> p a b", b=shape[1])
        if len(shape) == 3:
            v = v.rearrange("p (a b c) -> p a b c", b=shape[1], c=shape[2])
        if len(shape) == 4:
            v = v.rearrange("p (a b c d) -> p a b c d", b=shape[1], c=shape[2], d=shape[3])
        return v

    e.carve = carve
    e.w1 = carve(W1_0, [E0, DK, H0])
    e.w2 = carve(W2_0, [E0, HK0, D])
    e.w13 = carve(0, [E1, DK, 2 * I1])
    e.w2b = carve(W2_1, [E1, 2, D])
    o = ARENA0_END
    e.b2bc = carve(o, [E0, D]); o += E0 * D * 4
    e.wqkvT = carve(o, [DK, 3 * D]); o += DK * 3 * D * 4
    e.ctx = carve(o, [B, CD])[0:CL]; o += B * CD * 4
    e.b1T = carve(o, [E0 * HK0]); o += E0 * HK0 * 4
    e.wr = carve(o, [DK, E0]); o += DK * E0 * 4
    e.br = carve(o, [E0]); o += E0 * 4
    e.free0 = o
    e.dep = carve(o, [B, D]); o += B * D * 4
    e.plug = carve(o, [NTOK], BF16); o += NTOK * 2
    e.winT = carve(o, [DK, D]); o += DK * D * 4
    e.free1 = o
    o = TOP
    e.wprojT = carve(o, [DK, D]); o += DK * D * 4
    e.bproj = carve(o, [D]); o += D * 4
    e.gateT = carve(o, [DK, E1])
    return e


def prepare(e):
    nc, a, ps = e.nc, e.a, e.ps
    sem = e.sem
    x_in, small_in, consts = sem("x_in"), sem("small_in"), sem("consts")
    tr_raw, tr_done = sem("prep_tr_raw"), sem("prep_tr_done")
    pool_step, dve_step = sem("prep_pool_step"), sem("prep_dve_step")
    var_ready, std_ready = sem("prep_var"), sem("prep_std")
    u_ready, dep_raw, lens_ready, bidx_raw = sem("u_ready"), sem("dep_raw"), sem("lens_ready"), sem("bidx_raw")
    at_ready, cnt_raw, cnt_used = sem("at_ready"), sem("cnt_raw"), sem("cnt_used")

    wqkv = e.carve(0, [6, D], base=e.scr)
    wproj = e.carve(6 * D * 4, [DK, D], base=e.scr)
    gatew = e.carve(8 * D * 4, [D], base=e.scr)
    b1r = e.carve(9 * D * 4, [P], base=e.scr)
    ginit = e.carve(9 * D * 4 + P * 4, [D], base=e.scr)
    bin_ = e.carve(10 * D * 4 + P * 4, [D], base=e.scr)
    rest = 11 * D * 4 + P * 4
    tri = e.carve(rest, [CL], base=e.scr); rest += CL * 4
    tdec = e.carve(rest, [CL], base=e.scr); rest += CL * 4
    gres = e.carve(rest, [DK], base=e.scr); rest += DK * 4
    lens_i = e.carve(rest, [B], base=e.scr).bitcast(I32); rest += B * 4
    lens = e.carve(rest, [B], base=e.scr); rest += B * 4
    bidx = e.carve(rest, [B], base=e.scr); rest += B * 4
    wrap = e.carve(rest, [B], base=e.scr); rest += B * 4
    cs = e.carve(rest, [B, 6], base=e.scr); rest += B * 24
    cm = e.carve(rest, [8, B], base=e.scr); rest += 8 * B * 4
    g4 = e.carve(rest, [4], base=e.scr); rest += 16
    ones = e.carve(rest, [CL], base=e.scr); rest += CL * 4
    win = e.carve(rest, [DK, D], base=e.scr); rest += DK * D * 4
    assert rest <= NTILE * D * 4, rest
    u = e.carve(e.free1, [B, D])
    assert e.free1 + B * D * 4 <= TOP
    at = e.ysb[:].rearrange("p a b -> p (a b)")[:, 0:S]
    iota_t = e.xg[:].rearrange("p a b -> p (a b)")[:, 0:S]
    N_SMALL = 18

    turn = []
    for dk in range(DK):
        for et in range(DK):
            turn.append((win[:, et, dk * P:(dk + 1) * P], P, e.winT[:, dk, et * P:(et + 1) * P], gres[:, dk:dk + 1]))
        for et in range(6):
            turn.append((wqkv[:, et, dk * P:(dk + 1) * P], P, e.wqkvT[:, dk, et * P:(et + 1) * P], None))
        for et in range(DK):
            turn.append((wproj[:, et, dk * P:(dk + 1) * P], P, e.wprojT[:, dk, et * P:(et + 1) * P], None))
        turn.append((gatew[0:E1, dk * P:(dk + 1) * P], E1, e.gateT[:, dk, :], None))
    turn.append((b1r[0:E0 * HK0, :], E0 * HK0, e.b1T, None))

    dt = float(-np.log(-np.expm1(np.float32(-PATCH_EPS)).astype(np.float32)).astype(np.float32))
    bcoef = float(np.exp(np.float32(-PATCH_EPS)))
    decay = [bcoef * float(np.exp(-dt * k)) for k in range(CL)]
    decay = [w for w in decay if np.float32(w) > 0]

    with nc.Block() as block:
        @block.sync
        def _(sp):
            sp.dma_start(e.x[:], a["x"].rearrange("b (t p) d -> p (b t) d", p=P)).then_inc(x_in, 16)
            for dst, src in (
                (win, a["L0_xattn_W_in"].rearrange("(k p) d -> p k d", p=P)),
                (wqkv, a["L1_xattn_w_qkv"].rearrange("(k p) d -> p k d", p=P)),
                (wproj, a["L1_xattn_w_proj"].rearrange("(k p) d -> p k d", p=P)),
                (gatew[0:E1, :], a["L1_ffn_gate_w"]),
                (b1r[0:E0 * HK0, :], a["L0_ffn_b1"].rearrange("e (k p) -> (e k) p", p=P)),
                (ginit[0:CL, :], a["L0_xattn_g_init"][0:D].partition_broadcast(CL)),
                (bin_[0:CL, :], a["L0_xattn_b_in"].partition_broadcast(CL)),
                (gres, a["L0_xattn_g_res"].rearrange("(k p) -> p k", p=P)),
                (lens_i[0:CL, :], a["mask_BxS2_if0"].rearrange("b s -> s b")),
                (e.ctx, a["ctx_2048"].rearrange("b s d -> s b d")),
                (g4[:, 0:2], a["g_xattn"].partition_broadcast(P)),
                (g4[:, 2:4], a["g_ffn"].partition_broadcast(P)),
                (e.wr, a["L0_ffn_Wr"].rearrange("(k p) e -> p k e", p=P)),
                (e.br, a["L0_ffn_br"].partition_broadcast(P)),
                (e.ebias[:], a["L1_ffn_e_bias"].partition_broadcast(P)),
                (e.bproj, a["L1_xattn_b_proj"].partition_broadcast(P)),
                (e.b2bc, a["L0_ffn_b2"].rearrange("e d -> (e d)").partition_broadcast(P).rearrange("p (e d) -> p e d", d=D)),
            ):
                sp.dma_start(dst, src, allow_slow_non_contiguous=True).then_inc(small_in, 16)
            for ex in range(E0):
                sp.dma_start(e.w1[:, ex], a["L0_ffn_W1"][ex].rearrange("(k p) h -> p k h", p=P)).then_inc(e.w0_in, 16)
                sp.dma_start(e.w2[:, ex], a["L0_ffn_W2"][ex].rearrange("(k p) d -> p k d", p=P)).then_inc(e.w0_in, 16)

        @block.gpsimd
        def _(pool):
            ch = Chain(pool, pool_step)
            g = nc.gpsimd
            g.memset(e.ident[:], 0.0)
            g.memset(e.identb[:], 0.0)
            g.memset(e.earlier[:], 1.0)
            g.memset(e.onesb[:], 1.0)
            g.memset(ones[0:CL, :], 1.0)
            g.memset(tri[0:CL, :], 1.0)
            ch(g.memset(tdec[0:CL, :], 0.0))
            for m in (e.ident, e.identb):
                g.affine_select(out=m[:], in_=m[:], compare_op=ALU.not_equal, fill=1.0, base=0, pattern=[[-1, P]], channel_multiplier=1)
            g.affine_select(out=e.earlier[:], in_=e.earlier[:], compare_op=ALU.is_gt, fill=0.0, base=0, pattern=[[1, P]], channel_multiplier=-1)
            g.affine_select(out=tri[0:CL, :], in_=tri[0:CL, :], compare_op=ALU.is_ge, fill=0.0, base=0, pattern=[[1, CL]], channel_multiplier=-1)
            for k, w in enumerate(decay):
                ch(g.affine_select(out=tdec[0:CL, :], in_=tdec[0:CL, :], compare_op=ALU.not_equal, fill=w, base=-k, pattern=[[1, CL]], channel_multiplier=-1))
            g.iota(iota_t[0:CL, :], pattern=[[1, S]], base=0, channel_multiplier=0, allow_small_or_imprecise_dtypes=True)
            g.iota(e.iota[:], pattern=[[1, P]], base=0, channel_multiplier=0, allow_small_or_imprecise_dtypes=True)
            g.iota(e.iota_p[:], pattern=[[0, 1]], base=0, channel_multiplier=1, allow_small_or_imprecise_dtypes=True)
            ch(g.iota(e.steps[:], pattern=[[P, NTILE]], base=0, channel_multiplier=0, allow_small_or_imprecise_dtypes=True))
            g.drain().then_inc(consts, 1)

        @block.tensor
        def _(pe):
            pe.wait_ge(consts, 1)
            pe.wait_ge(small_in, 16 * (N_SMALL - 1))
            for n, (src, rows, dst, scale) in enumerate(turn):
                if n >= 4:
                    pe.wait_ge(tr_done, n - 3)
                nc.tensor.transpose(ps[:, n % 4, 0:rows], src, e.ident[0:rows, 0:rows]).then_inc(tr_raw, 1)
            pe.wait_ge(lens_ready, 1)
            nc.tensor.matmul(ps[0:CL, 4, 0:B], tri[0:CL, :], lens[0:CL, :], start=True, stop=True).then_inc(bidx_raw, 1)
            for b in range(B):
                pe.wait_ge(u_ready, b + 1)
                nc.tensor.matmul(ps[0:CL, 5 + b, 0:D], tdec[0:CL, :], u[0:CL, b, :], start=True, stop=True).then_inc(dep_raw, 1)
            for b in range(B):
                pe.wait_ge(at_ready, b + 1)
                for h in range(S // HB):
                    if b == 0:
                        pe.wait_ge(tr_done, len(turn))
                    else:
                        pe.wait_ge(cnt_used, b)
                    nc.tensor.matmul(ps[0:CL, h, :], ones[0:CL, 0:CL], at[0:CL, h * HB:(h + 1) * HB], start=True, stop=True).then_inc(cnt_raw, 1)

        @block.scalar
        def _(act):
            act.wait_ge(small_in, 16 * (N_SMALL - 1))
            nc.scalar.activation(e.tg[:], g4, ACT.Tanh)
            for n, (src, rows, dst, scale) in enumerate(turn):
                act.wait_ge(tr_raw, n + 1)
                if scale is None:
                    nc.scalar.activation(dst, ps[:, n % 4, 0:rows], ACT.Copy).then_inc(tr_done, 1)
                else:
                    nc.scalar.activation(dst, ps[:, n % 4, 0:rows], ACT.Copy, scale=scale).then_inc(tr_done, 1)
            act.wait_ge(var_ready, 1)
            nc.scalar.activation(e.std[:], e.ve[:], ACT.Sqrt).then_inc(std_ready, 1)
            act.wait_ge(var_ready, 2)
            nc.scalar.activation(e.std[:], e.ve[:], ACT.Sqrt).then_inc(std_ready, 1)
            act.wait_ge(var_ready, 3)
            nc.scalar.activation(cm[0:CL, 6, :], cm[0:CL, 5, :], ACT.Sqrt).then_inc(std_ready, 1)

        @block.vector
        def _(dve):
            ch = Chain(dve, dve_step)
            v = nc.vector
            dve.wait_ge(x_in, 16)
            with dve.Fori(0, NTILE) as i:
                v.bn_stats(e.stats[:, i, :], e.x[:, i, :])
            ch(v.memset(e.tmp[:, 0, :], 0.0))
            t = [e.tmp[:, n, :] for n in range(4)]
            moments(ch, nc, e.stats, D, e.mean[:], e.var[:], e.ve[:], t, LN_EPS)
            v.engine_nop().then_inc(var_ready, 1)
            dve.wait_ge(std_ready, 1)
            ch(v.reciprocal(e.rstd[:], e.std[:]))
            ch(v.tensor_tensor(e.tmp[:, 0, :], e.rstd[:], e.rstd[:], ALU.mult))
            ch(v.tensor_tensor(e.tmp[:, 1, :], e.tmp[:, 0, :], e.var[:], ALU.mult))
            v.tensor_scalar(e.ve[:], e.tmp[:, 1, :], RMS_EPS, None, ALU.add).then_inc(var_ready, 1)
            dve.wait_ge(std_ready, 2)
            ch(v.reciprocal(e.tmp[:, 2, :], e.std[:]))
            ch(v.tensor_tensor(e.rstd[:], e.rstd[:], e.tmp[:, 2, :], ALU.mult))

            dve.wait_ge(small_in, 16 * (N_SMALL - 1))
            for b in range(B):
                ch(v.bn_stats(cs[0:CL, b, :], e.ctx[:, b, :]))
            c = [cm[0:CL, n, :] for n in range(8)]
            moments(ch, nc, cs[0:CL], CD, c[4], c[5], c[6], c[0:4], RMS_EPS)
            ch(v.tensor_tensor(c[0], c[4], c[4], ALU.mult))
            v.tensor_tensor(c[5], c[0], c[6], ALU.add).then_inc(var_ready, 1)
            dve.wait_ge(std_ready, 3)
            ch(v.reciprocal(c[7], c[6]))
            for b in range(B):
                v.scalar_tensor_tensor(u[0:CL, b, :], e.ctx[:, b, 0:D], cm[0:CL, 7, b:b + 1], ginit[0:CL, :], ALU.mult, ALU.mult).then_inc(u_ready, 1)

            v.tensor_copy(lens[0:CL, :], lens_i[0:CL, :]).then_inc(lens_ready, 1)
            dve.wait_ge(bidx_raw, 1)
            ch(v.tensor_scalar(bidx[0:CL, :], ps[0:CL, 4, 0:B], -1.0, None, ALU.add))
            ch(v.tensor_scalar(wrap[0:CL, :], bidx[0:CL, :], 0.0, float(S), ALU.is_lt, ALU.mult))
            ch(v.tensor_tensor(bidx[0:CL, :], bidx[0:CL, :], wrap[0:CL, :], ALU.add))
            for b in range(B):
                dve.wait_ge(dep_raw, b + 1)
                ch(v.tensor_tensor(e.dep[0:CL, b, :], ps[0:CL, 5 + b, 0:D], bin_[0:CL, :], ALU.add))
            dve.wait_ge(consts, 1)
            for b in range(B):
                row = e.plug[0:CL, b * S:(b + 1) * S]
                v.tensor_scalar(at[0:CL, :], iota_t[0:CL, :], bidx[0:CL, b:b + 1], None, ALU.is_equal).then_inc(at_ready, 1)
                dve.wait_ge(cnt_raw, 2 * b + 2)
                ch(v.tensor_scalar(at[0:CL, :], ps[0:CL, 0:2, :].rearrange("p a b -> p (a b)"), 1.0, None, ALU.min))
                v.engine_nop().then_inc(cnt_used, 1)
                count = ps[0:CL, 2:4, :].rearrange("p a b -> p (a b)")
                ch(v.tensor_tensor_scan(count, at[0:CL, :], at[0:CL, :], 0.0, ALU.add, ALU.max))
                ch(v.tensor_scalar(at[0:CL, :], count, -1.0, 0.0, ALU.add, ALU.max))
                ch(v.tensor_scalar(row, at[0:CL, :], float(CL - 1), None, ALU.min))


def depool_mixer(e):
    nc, ps, sem = e.nc, e.ps, e.sem
    xn_ready, xT_raw, xT_ready = sem("mix_xn_ready"), sem("mix_xT_raw"), sem("mix_xT_ready")
    mixed_raw, x_new = sem("mix_raw"), sem("mix_x_new")
    U = 4
    xn = e.carve(0, [U, D], base=e.scr)
    oh = e.carve(U * D * 4, [U, P], base=e.scr)
    xT = e.carve(U * (D + P) * 4, [U, DK, P], base=e.scr)

    with nc.Block() as block:
        def loop(eng, body):
            with eng.Fori(0, B) as b, eng.Fori(0, TPB // U) as h:
                for u in range(U):
                    body[0](b, h, u, b * TPB + h * U + u, b * (TPB // U) + h)
                if len(body) > 1:
                    for u in range(U):
                        body[1](b, h, u, b * TPB + h * U + u, b * (TPB // U) + h)

        @block.vector
        def _(dve):
            v = nc.vector
            dve.sem_inc(x_new, U)

            def norm(b, h, u, i, t):
                v.tensor_scalar(xn[:, u, :], e.x[:, i, :], e.mean[:, bass.ds(i, 1)], e.rstd[:, bass.ds(i, 1)], ALU.subtract, ALU.mult)
                v.tensor_scalar(oh[0:CL, u, :], e.plug[0:CL, bass.ds(i * P, P)], e.iota_p[0:CL, :], None, ALU.is_equal).then_inc(xn_ready, 1)

            def mix(b, h, u, i, t):
                dve.wait_ge(mixed_raw, i + 1)
                v.scalar_tensor_tensor(e.x[:, i, :], ps[:, 4 + u, 0:D], e.tg[:, 0:1], e.x[:, i, :], ALU.mult, ALU.add).then_inc(x_new, 1)
                dve.wait_ge(x_new, i + (U + 1))
                v.bn_stats(e.stats[:, i, :], e.x[:, i, :])

            loop(dve, (norm, mix))

        @block.tensor
        def _(pe):
            def turn(b, h, u, i, t):
                pe.wait_ge(xn_ready, i + 1)
                for k in range(DK):
                    last = nc.tensor.transpose(ps[:, u, k * P:(k + 1) * P], xn[:, u, k * P:(k + 1) * P], e.ident[:])
                last.then_inc(xT_raw, 1)

            def mix(b, h, u, i, t):
                pe.wait_ge(xT_ready, i + 1)
                pe.wait_ge(x_new, i + 1)
                for k in range(DK):
                    nc.tensor.matmul(ps[:, 4 + u, 0:D], xT[:, u, k, :], e.winT[:, k, :], start=(k == 0), stop=False)
                nc.tensor.matmul(ps[:, 4 + u, 0:D], oh[0:CL, u, :], e.dep[0:CL, b, :], start=False, stop=True).then_inc(mixed_raw, 1)

            loop(pe, (turn, mix))

        @block.scalar
        def _(act):
            def copy(b, h, u, i, t):
                act.wait_ge(xT_raw, i + 1)
                nc.scalar.activation(xT[:, u, :, :].rearrange("p k t -> p (k t)"), ps[:, u, 0:D], ACT.Copy).then_inc(xT_ready, 1)

            loop(act, (copy,))


def router(e, layer):
    nc, ps, sem = e.nc, e.ps, e.sem
    ne = (E0, E1)[layer]
    wr = (e.wr, e.gateT)[layer]
    nm = f"rt{layer}_"
    xn_ready, xT_raw, xT_ready = sem(nm + "xn_ready"), sem(nm + "xT_raw"), sem(nm + "xT_ready")
    lg_raw, lg_done, step = sem(nm + "lg_raw"), sem(nm + "lg_done"), sem(nm + "step")
    var_ready, std_ready = sem(nm + "var"), sem(nm + "std")
    U = 4
    stored = [sem(nm + f"xn_stored{u}") for u in range(U)]
    xn = e.carve(0, [U, D], base=e.scr)
    xT = e.carve(U * D * 4, [U, DK, P], base=e.scr)
    e.logits = e.carve(2 * U * D * 4, [NTILE, ne], base=e.scr)
    TURNS = NTILE // U

    with nc.Block() as block:
        @block.vector
        def _(dve):
            v = nc.vector
            ch = Chain(dve, step)
            moments(ch, nc, e.stats, D, e.mean[:], e.var[:], e.ve[:], [e.tmp[:, n, :] for n in range(4)], LN_EPS)
            v.engine_nop().then_inc(var_ready, 1)
            dve.wait_ge(std_ready, 1)
            ch(v.reciprocal(e.rstd[:], e.std[:]))
            dve.sem_inc(lg_done, U)

            def norm(t, u, wait):
                if wait:
                    dve.wait_ge(stored[u], t * 16)
                i = t * U + u
                v.tensor_scalar(xn[:, u, :], e.x[:, i, :], e.mean[:, bass.ds(i, 1)], e.rstd[:, bass.ds(i, 1)], ALU.subtract, ALU.mult).then_inc(xn_ready, 1)

            def logit(t, u):
                i = t * U + u
                dve.wait_ge(lg_raw, i + 1)
                if layer == 0:
                    v.tensor_tensor(e.logits[:, i, :], ps[:, 4 + u, 0:ne], e.br, ALU.add).then_inc(lg_done, 1)
                else:
                    v.tensor_copy(e.logits[:, i, :], ps[:, 4 + u, 0:ne]).then_inc(lg_done, 1)

            for u in range(U):
                norm(0, u, False)
            for u in range(U):
                logit(0, u)
            with dve.Fori(1, TURNS) as t:
                for u in range(U):
                    norm(t, u, True)
                for u in range(U):
                    logit(t, u)

        @block.scalar
        def _(act):
            act.wait_ge(var_ready, 1)
            nc.scalar.activation(e.std[:], e.ve[:], ACT.Sqrt).then_inc(std_ready, 1)
            with act.Fori(0, TURNS) as t:
                for u in range(U):
                    act.wait_ge(xT_raw, t * U + u + 1)
                    nc.scalar.activation(xT[:, u, :, :].rearrange("p k t -> p (k t)"), ps[:, u, 0:D], ACT.Copy).then_inc(xT_ready, 1)

        @block.sync
        def _(sp):
            with sp.Fori(0, TURNS) as t:
                for u in range(U):
                    i = t * U + u
                    sp.wait_ge(xn_ready, i + 1)
                    sp.dma_start(e.xn[layer][bass.ds(i * P, P), :], xn[:, u, :]).then_inc(stored[u], 16)
            for u in range(U):
                sp.wait_ge(stored[u], 16 * TURNS)

        @block.tensor
        def _(pe):
            with pe.Fori(0, TURNS) as t:
                for u in range(U):
                    pe.wait_ge(xn_ready, t * U + u + 1)
                    for k in range(DK):
                        last = nc.tensor.transpose(ps[:, u, k * P:(k + 1) * P], xn[:, u, k * P:(k + 1) * P], e.ident[:])
                    last.then_inc(xT_raw, 1)
                for u in range(U):
                    pe.wait_ge(xT_ready, t * U + u + 1)
                    pe.wait_ge(lg_done, t * U + u + 1)
                    for k in range(DK):
                        last = nc.tensor.matmul(ps[:, 4 + u, 0:ne], xT[:, u, k, :], wr[:, k, :], start=(k == 0), stop=(k == DK - 1))
                    last.then_inc(lg_raw, 1)


def route(e, layer):
    nc, ps, sem = e.nc, e.ps, e.sem
    ne, kk, nt = ((E0, K0, NT0), (E1, K1, NT1))[layer]
    nm = f"ro{layer}_"
    step, act_in, act_out = sem(nm + "step"), sem(nm + "act_in"), sem(nm + "act_out")
    mask_ready, rank_raw, first_ready, first_raw = sem(nm + "mask"), sem(nm + "rank_raw"), sem(nm + "first"), sem(nm + "first_raw")
    pick_ready, pick_used, token_raw = sem(nm + "pick_ready"), sem(nm + "pick_used"), sem(nm + "token_raw")
    pool_step = sem(nm + "pool_step")
    o = [e.free0 if layer == 0 else ATT0 + (E1 - EARLY) * W13_BYTES]

    def buf(shape, dt=F32):
        got = e.carve(o[0], shape, dt)
        o[0] += int(np.prod(shape)) * (2 if dt == BF16 else 4)
        assert o[0] <= TOP, o[0]
        return got

    N = NTILE * ne
    top = buf([NTILE, 8]); topi = buf([NTILE, 8]).bitcast(U32); topf = buf([NTILE, 8])
    chosen = buf([kk, NTILE, ne])
    mask = buf([NTILE, ne]); maskb = buf([NTILE, ne], BF16)
    place = buf([NTILE, ne]); work = buf([NTILE, ne])
    offs = buf([NTILE + 1, ne])
    many = buf([ne, NTILE]); tiles = buf([ne]); upto = buf([ne]); start = buf([ne]); below = buf([ne])
    first = buf([1])
    slot = buf([NTILE, kk]); slot_i = buf([NTILE, kk]).bitcast(I32)
    part_i = buf([NTILE, kk]).bitcast(I32); part = buf([NTILE, kk]); tile_i = buf([NTILE, kk]).bitcast(I32); tile_f = buf([NTILE, kk])
    token = buf([NTILE, kk])
    W = 4
    row_is = buf([W, P]); col_is = buf([W, nt])
    sel = e.logits
    ex = buf([NTILE, K0]); tot = buf([NTILE])
    if layer == 1:
        sel = buf([NTILE, ne]); sig = buf([NTILE, ne])
    NQ = NTILE * kk

    def bc(ap, n):
        return ap.unsqueeze(2).broadcast_to([P, ap.shape[1], n])

    with nc.Block() as block:
        @block.gpsimd
        def _(pool):
            nc.gpsimd.iota(token, pattern=[[P, NTILE], [0, kk]], base=0, channel_multiplier=1, allow_small_or_imprecise_dtypes=True).then_inc(pool_step, 1)

        @block.scalar
        def _(act):
            act.wait_ge(act_in, 1)
            if layer == 0:
                nc.scalar.activation(ex, ex, ACT.Exp).then_inc(act_out, 1)
            else:
                nc.scalar.activation(sig, e.logits, ACT.Exp, scale=-1.0).then_inc(act_out, 1)

        @block.vector
        def _(dve):
            v = nc.vector
            ch = Chain(dve, step)
            if layer == 1:
                v.engine_nop().then_inc(act_in, 1)
                dve.wait_ge(act_out, 1)
                ch(v.tensor_scalar(sig, sig, 1.0, None, ALU.add))
                ch(v.reciprocal(sig, sig))
                ch(v.tensor_tensor(sel, sig, e.ebias[:].unsqueeze(1).broadcast_to([P, NTILE, ne]), ALU.add))
            for i in range(NTILE):
                v.max(top[:, i, :], sel[:, i, :])
            ch(v.memset(tot, 0.0))
            for i in range(NTILE):
                v.max_index(topi[:, i, :], top[:, i, :], sel[:, i, :])
            ch(v.memset(offs[:, 0, :], 0.0))
            ch(v.tensor_copy(topf, topi))
            for k in range(kk):
                v.tensor_tensor(chosen[:, k], e.iota[:, 0:ne].unsqueeze(1).broadcast_to([P, NTILE, ne]), bc(topf[:, :, k], ne), ALU.is_equal)
            ch(v.memset(tot, 0.0))
            ch(v.tensor_tensor(mask, chosen[:, 0], chosen[:, 1], ALU.add))
            for k in range(2, kk):
                ch(v.tensor_tensor(mask, mask, chosen[:, k], ALU.add))
            v.tensor_copy(maskb, mask).then_inc(mask_ready, 1)

            if layer == 0:
                v.tensor_tensor(ex, top[:, :, 0:kk], bc(top[:, :, 0], kk), ALU.subtract).then_inc(act_in, 1)
                dve.wait_ge(act_out, 1)
                w = ex
            else:
                for k in range(kk):
                    ch(v.tensor_tensor(work, chosen[:, k], sig, ALU.mult))
                    ch(v.tensor_reduce(slot[:, :, k], work, AX.X, ALU.add))
                w = slot
            ch(v.tensor_reduce(tot, w, AX.X, ALU.add))
            ch(v.reciprocal(tot, tot))
            ch(v.tensor_tensor(e.gate[:, :, 0:kk], w, bc(tot, kk), ALU.mult))

            dve.wait_ge(rank_raw, 2)
            for i in range(NTILE):
                ch(v.tensor_tensor(offs[:, i + 1, :], offs[:, i, :], ps[:, 1, i * ne:(i + 1) * ne], ALU.add))
            ch(v.tensor_tensor(many, bc(offs[:, NTILE, :], NTILE), e.steps[:].unsqueeze(1).broadcast_to([P, ne, NTILE]), ALU.is_gt))
            ch(v.tensor_reduce(tiles, many, AX.X, ALU.add))
            ch(v.memset(below, 1.0))
            ch(v.tensor_tensor_scan(upto, below, tiles, 0.0, ALU.mult, ALU.add))
            ch(v.tensor_tensor(start, upto, tiles, ALU.subtract))
            ch(v.tensor_scalar(below, upto, e.iota_p[:], None, ALU.is_le))
            ch(v.tensor_reduce(first, below, AX.X, ALU.add))
            v.tensor_scalar(first, first, float(ne - 1), None, ALU.min).then_inc(first_ready, 1)

            ch(v.tensor_tensor(place, ps[:, 0, 0:N].rearrange("p (i e) -> p i e", e=ne), offs[:, 0:NTILE, :], ALU.add))
            ch(v.scalar_tensor_tensor(place, start.unsqueeze(1).broadcast_to([P, NTILE, ne]), float(P), place, ALU.mult, ALU.add))
            for k in range(kk):
                ch(v.tensor_tensor(work, chosen[:, k], place, ALU.mult))
                ch(v.tensor_reduce(slot[:, :, k], work, AX.X, ALU.add))
            v.tensor_copy(e.slot_u[:, :, 0:kk], slot)
            ch(v.tensor_copy(slot_i, slot))
            ch(v.tensor_scalar(part_i, slot_i, P - 1, None, ALU.bitwise_and))
            ch(v.tensor_scalar(tile_i, slot_i, 7, None, ALU.logical_shift_right))
            ch(v.tensor_copy(part, part_i))
            ch(v.tensor_copy(tile_f, tile_i))
            dve.wait_ge(first_raw, 1)
            ch(v.tensor_copy(e.expert[0:1, :], ps[0:1, 2, 0:P]))

            dve.wait_ge(pool_step, 1)
            pf, tf, kf = (z.rearrange("p i k -> p (i k)") for z in (part, tile_f, token))

            def pick(t, u, wait):
                q = t * W + u
                if wait:
                    dve.wait_ge(pick_used, q - (W - 1))
                v.tensor_scalar(row_is[:, u, :], e.iota[:], pf[:, bass.ds(q, 1)], None, ALU.is_equal)
                v.tensor_scalar(col_is[:, u, :], e.iota[:, 0:nt], tf[:, bass.ds(q, 1)], kf[:, bass.ds(q, 1)], ALU.is_equal, ALU.mult).then_inc(pick_ready, 1)

            for u in range(W):
                pick(0, u, False)
            with dve.Fori(1, NQ // W) as t:
                for u in range(W):
                    pick(t, u, True)
            dve.wait_ge(token_raw, 1)
            v.tensor_copy(e.token_u[:, 0:nt], ps[:, 3, 0:nt])

        @block.tensor
        def _(pe):
            pe.wait_ge(mask_ready, 1)
            m = maskb.rearrange("p i e -> p (i e)")
            nc.tensor.matmul(ps[:, 0, 0:N], e.earlier[:], m, start=True, stop=True).then_inc(rank_raw, 1)
            nc.tensor.matmul(ps[:, 1, 0:N], e.onesb[:], m, start=True, stop=True).then_inc(rank_raw, 1)
            pe.wait_ge(first_ready, 1)
            nc.tensor.transpose(ps[0:1, 2, 0:P], first, e.ident[:]).then_inc(first_raw, 1)

            def pick(q, u, begin, end):
                pe.wait_ge(pick_ready, q + 1)
                ins = nc.tensor.matmul(ps[:, 3, 0:nt], row_is[:, u, :], col_is[:, u, :], start=begin, stop=end)
                ins.then_inc(token_raw if end else pick_used, 1)

            for u in range(W):
                pick(u, u, u == 0, False)
            with pe.Fori(1, NQ // W - 1) as t:
                for u in range(W):
                    pick(t * W + u, u, False, False)
            for q in range(NQ - W, NQ):
                pick(q, q % W, False, q == NQ - 1)


def gather_tiles(e, layer, block, gathered, x_turned):
    nc = e.nc
    nt, ring = ((NT0, RING0), (NT1, RING1))[layer]
    icol_ready, carrier = e.sem(f"ga{layer}_icol_ready"), e.sem(f"ga{layer}_carrier")

    @block.gpsimd
    def _(pool):
        icol = e.icol[:].rearrange("p a b -> p (a b)")

        def body(j, r, turn, first, last):
            if not (isinstance(j, int) and j < ring):
                pool.wait_ge(x_turned, j + (1 - ring))
            nc.gpsimd.tensor_copy(icol[:, r:r + 1], e.token_u[:, bass.ds(j, 1)]).then_inc(icol_ready, 1)
            pool.wait_ge(icol_ready, j + 1)
            pool.sem_inc(carrier, 1)
            pool.indirect_dma_start(out=e.xg[:, r, :], out_offset=None, in_=e.xn[layer],
                                    in_offset=bass.IndirectOffsetOnAxis(ap=icol[:, r:r + 1], axis=0)).then_inc(gathered[r], 16)

        for j in range(ring):
            body(j, j, 0, j == 0, False)
        turns = (nt - ring) // ring
        with pool.Fori(1, 1 + turns) as t:
            for u in range(ring):
                body(t * ring + u, u, t, False, False)
        for j in range(ring * (1 + turns), nt):
            body(j, j % ring, j // ring, False, False)


def experts0(e):
    nc, ps, sem = e.nc, e.ps, e.sem
    gathered = [sem(f"e0_gathered{r}") for r in range(RING0)]
    x_turned, xT_ready = sem("e0_x_turned"), sem("e0_xT_ready")
    h_raw, h_copied, h_turned, hT_ready = sem("e0_h_raw"), sem("e0_h_copied"), sem("e0_h_turned"), sem("e0_hT_ready")
    y_raw, y_ready = sem("e0_y_raw"), sem("e0_y_ready")
    y_stored = [sem(f"e0_y_stored{r}") for r in range(RING0)]
    xT = e.carve(0, [DK, P], base=e.scr)
    h = e.carve(DK * P * 4, [H0], base=e.scr)
    hT = e.carve(DK * P * 4 + H0 * 4, [HK0, P], base=e.scr)
    HH = H0 // HB
    HALF = HK0 // HH
    XB, HB0, TB, YB = 0, 1, 3, 5

    with nc.Block() as block:
        gather_tiles(e, 0, block, gathered, x_turned)

        @block.tensor
        def _(pe):
            pe.wait_ge(e.w0_in, 16 * 2 * E0)

            def turn_x(j, r, turn):
                pe.wait_ge(gathered[r], turn * 16 + 16)
                for k in range(DK):
                    last = nc.tensor.transpose(ps[:, XB, k * P:(k + 1) * P], e.xg[:, r, k * P:(k + 1) * P], e.ident[:])
                last.then_inc(x_turned, 1)

            def down(j):
                ex = pe.value_load(e.expert[0:1, bass.ds(j, 1)], min_val=0, max_val=E0 - 1)
                if not (isinstance(j, int) and j == 0):
                    pe.wait_ge(y_ready, j)
                for k in range(HK0):
                    pe.wait_ge(hT_ready, j * HK0 + k + 1)
                    last = nc.tensor.matmul(ps[:, YB, 0:D], hT[:, k, :], e.w2[:, ex, k, :], start=(k == 0), stop=(k == HK0 - 1))
                last.then_inc(y_raw, 1)

            def body(j, r, turn, first, last):
                ex = pe.value_load(e.expert[0:1, bass.ds(j, 1)], min_val=0, max_val=E0 - 1)
                pe.wait_ge(xT_ready, j + 1)
                for n in range(HH):
                    for k in range(DK):
                        ins = nc.tensor.matmul(ps[:, HB0 + n, :], xT[:, k, :], e.w1[:, ex, k, n * HB:(n + 1) * HB], start=(k == 0), stop=(k == DK - 1))
                    ins.then_inc(h_raw, 1)
                if not last:
                    turn_x(j + 1, (r + 1) % RING0, turn + (r + 1) // RING0)
                if not first:
                    down(j - 1)
                for n in range(HH):
                    pe.wait_ge(h_copied, j * HH + n + 1)
                    for k in range(n * HALF, (n + 1) * HALF):
                        ins = nc.tensor.transpose(ps[:, TB + n, (k % HALF) * P:(k % HALF + 1) * P], h[:, k * P:(k + 1) * P], e.ident[:])
                    ins.then_inc(h_turned, 1)

            turn_x(0, 0, 0)
            tile_loop(pe, NT0, RING0, body)
            down(NT0 - 1)

        @block.scalar
        def _(act):
            def copy_x(j):
                act.wait_ge(x_turned, j + 1)
                nc.scalar.activation(xT.rearrange("p k t -> p (k t)"), ps[:, XB, 0:D], ACT.Copy).then_inc(xT_ready, 1)

            def body(j, r, turn, first, last):
                for n in range(HH):
                    act.wait_ge(h_raw, j * HH + n + 1)
                    nc.scalar.activation(h[:, n * HB:(n + 1) * HB], ps[:, HB0 + n, :], ACT.Copy).then_inc(h_copied, 1)
                if not last:
                    copy_x(j + 1)

            copy_x(0)
            tile_loop(act, NT0, RING0, body)

        @block.vector
        def _(dve):
            v = nc.vector

            def out(j, r, turn, fresh):
                ex = dve.value_load(e.expert[0:1, bass.ds(j, 1)], min_val=0, max_val=E0 - 1)
                if not fresh:
                    dve.wait_ge(y_stored[r], turn * 16)
                dve.wait_ge(y_raw, j + 1)
                v.tensor_tensor(e.ysb[:, r, :], ps[:, YB, 0:D], e.b2bc[:, ex, :], ALU.add).then_inc(y_ready, 1)

            def body(j, r, turn, first, last):
                if not first:
                    out(j - 1, (r - 1) % RING0, turn if r else turn - 1, isinstance(j, int) and j <= RING0)
                ex = dve.value_load(e.expert[0:1, bass.ds(j, 1)], min_val=0, max_val=E0 - 1)
                for k in range(HK0):
                    if k % HALF == 0:
                        dve.wait_ge(h_turned, j * HH + k // HALF + 1)
                    v.tensor_scalar(hT[:, k, :], ps[:, TB + k // HALF, (k % HALF) * P:(k % HALF + 1) * P],
                                    e.b1T[:, bass.ds(ex * HK0 + k, 1)], 0.0, ALU.add, ALU.max).then_inc(hT_ready, 1)

            tile_loop(dve, NT0, RING0, body)
            out(NT0 - 1, (NT0 - 1) % RING0, (NT0 - 1) // RING0, False)

        @block.sync
        def _(sp):
            def body(j, r, turn, first, last):
                sp.wait_ge(y_ready, j + 1)
                sp.dma_start(e.y[0][bass.ds(j * P, P), :], e.ysb[:, r, :]).then_inc(y_stored[r], 16)

            tile_loop(sp, NT0, RING0, body)
            for r in range(RING0):
                sp.wait_ge(y_stored[r], 16 * ((NT0 - 1 - r) // RING0 + 1))


def experts1(e):
    nc, ps, sem = e.nc, e.ps, e.sem
    gathered = [sem(f"e1_gathered{r}") for r in range(RING1)]
    x_turned, xT_ready = sem("e1_x_turned"), sem("e1_xT_ready")
    gu_raw, silu_ready, a_ready, a_turned, aT_ready = (sem("e1_" + n) for n in ("gu_raw", "silu_ready", "a_ready", "a_turned", "aT_ready"))
    y_raw, y_ready = sem("e1_y_raw"), sem("e1_y_ready")
    y_stored = [sem(f"e1_y_stored{r}") for r in range(RING1)]
    xT = e.carve(0, [DK, P], base=e.scr)
    silu = e.carve(DK * P * 4, [I1], base=e.scr)
    act_in = e.carve(DK * P * 4 + I1 * 4, [I1], base=e.scr)
    aT = e.carve(DK * P * 4 + 2 * I1 * 4, [2, P], base=e.scr)
    XB, GB, TB, YB = 0, 1, 2, 3

    with nc.Block() as block:
        gather_tiles(e, 1, block, gathered, x_turned)

        @block.tensor
        def _(pe):
            pe.wait_ge(e.w13_in, 32 * E1)
            pe.wait_ge(e.w2_in, 16 * E1)

            def turn_x(j, r, turn):
                pe.wait_ge(gathered[r], turn * 16 + 16)
                for k in range(DK):
                    last = nc.tensor.transpose(ps[:, XB, k * P:(k + 1) * P], e.xg[:, r, k * P:(k + 1) * P], e.ident[:])
                last.then_inc(x_turned, 1)

            def down(j):
                ex = pe.value_load(e.expert[0:1, bass.ds(j, 1)], min_val=0, max_val=E1 - 1)
                if not (isinstance(j, int) and j == 0):
                    pe.wait_ge(y_ready, j)
                pe.wait_ge(aT_ready, j + 1)
                for k in range(2):
                    last = nc.tensor.matmul(ps[:, YB, 0:D], aT[0:IH, k, :], e.w2b[0:IH, ex, k, :], start=(k == 0), stop=(k == 1))
                last.then_inc(y_raw, 1)

            def body(j, r, turn, first, last):
                ex = pe.value_load(e.expert[0:1, bass.ds(j, 1)], min_val=0, max_val=E1 - 1)
                pe.wait_ge(xT_ready, j + 1)
                for k in range(DK):
                    ins = nc.tensor.matmul(ps[:, GB, 0:2 * I1], xT[:, k, :], e.w13[:, ex, k, :], start=(k == 0), stop=(k == DK - 1))
                ins.then_inc(gu_raw, 1)
                if not last:
                    turn_x(j + 1, (r + 1) % RING1, turn + (r + 1) // RING1)
                if not first:
                    down(j - 1)
                pe.wait_ge(a_ready, j + 1)
                for k in range(2):
                    ins = nc.tensor.transpose(ps[0:IH, TB, k * P:(k + 1) * P], act_in[:, k * IH:(k + 1) * IH], e.ident[:])
                ins.then_inc(a_turned, 1)

            turn_x(0, 0, 0)
            tile_loop(pe, NT1, RING1, body)
            down(NT1 - 1)

        @block.scalar
        def _(act):
            def copy_x(j):
                act.wait_ge(x_turned, j + 1)
                nc.scalar.activation(xT.rearrange("p k t -> p (k t)"), ps[:, XB, 0:D], ACT.Copy).then_inc(xT_ready, 1)

            def body(j, r, turn, first, last):
                act.wait_ge(gu_raw, j + 1)
                if not first:
                    act.wait_ge(a_ready, j)
                nc.scalar.activation(silu, ps[:, GB, 0:I1], ACT.Silu).then_inc(silu_ready, 1)
                if not last:
                    copy_x(j + 1)
                act.wait_ge(a_turned, j + 1)
                nc.scalar.activation(aT[0:IH].rearrange("p k t -> p (k t)"), ps[0:IH, TB, 0:2 * P], ACT.Copy).then_inc(aT_ready, 1)

            copy_x(0)
            tile_loop(act, NT1, RING1, body)

        @block.vector
        def _(dve):
            v = nc.vector

            def out(j, r, turn, fresh):
                if not fresh:
                    dve.wait_ge(y_stored[r], turn * 16)
                dve.wait_ge(y_raw, j + 1)
                v.tensor_copy(e.ysb[:, r, :], ps[:, YB, 0:D]).then_inc(y_ready, 1)

            def body(j, r, turn, first, last):
                dve.wait_ge(silu_ready, j + 1)
                v.tensor_tensor(act_in, ps[:, GB, I1:2 * I1], silu, ALU.mult).then_inc(a_ready, 1)
                if not first:
                    out(j - 1, (r - 1) % RING1, turn if r else turn - 1, isinstance(j, int) and j <= RING1)

            tile_loop(dve, NT1, RING1, body)
            out(NT1 - 1, (NT1 - 1) % RING1, (NT1 - 1) // RING1, False)

        @block.sync
        def _(sp):
            def body(j, r, turn, first, last):
                sp.wait_ge(y_ready, j + 1)
                sp.dma_start(e.y[1][bass.ds(j * P, P), :], e.ysb[:, r, :]).then_inc(y_stored[r], 16)

            tile_loop(sp, NT1, RING1, body)
            for r in range(RING1):
                sp.wait_ge(y_stored[r], 16 * ((NT1 - 1 - r) // RING1 + 1))


def combine(e, layer):
    nc, sem = e.nc, e.sem
    kk = (K0, K1)[layer]
    nm = f"co{layer}_"
    U = 4
    got = [sem(nm + f"got{u}") for u in range(U)]
    icol_ready, carrier, added, step = sem(nm + "icol_ready"), sem(nm + "carrier"), sem(nm + "added"), sem(nm + "step")
    stored = sem(nm + "stored")
    yg = e.carve(0, [U, kk, D], base=e.scr)
    TURNS = NTILE // U
    last_layer = layer == 1

    with nc.Block() as block:
        @block.gpsimd
        def _(pool):
            def body(t, u, wait):
                i = t * U + u
                if wait:
                    pool.wait_ge(added, i - (U - 1))
                nc.gpsimd.tensor_copy(e.icol[:, u, 0:kk], e.slot_u[:, i, 0:kk]).then_inc(icol_ready, 1)
                pool.wait_ge(icol_ready, i + 1)
                pool.sem_inc(carrier, 1)
                for k in range(kk):
                    pool.indirect_dma_start(out=yg[:, u, k, :], out_offset=None, in_=e.y[layer],
                                            in_offset=bass.IndirectOffsetOnAxis(ap=e.icol[:, u, k:k + 1], axis=0)).then_inc(got[u], 16)

            for u in range(U):
                body(0, u, False)
            with pool.Fori(1, TURNS) as t:
                for u in range(U):
                    body(t, u, True)

        @block.vector
        def _(dve):
            v = nc.vector
            ch = Chain(dve, step)
            with dve.Fori(0, TURNS) as t:
                with ch.turns(t, U * kk, TURNS):
                    for u in range(U):
                        i = t * U + u
                        dve.wait_ge(got[u], t * (16 * kk) + 16 * kk)
                        ch(v.tensor_scalar(yg[:, u, 0, :], yg[:, u, 0, :], e.gate[:, i, 0:1], None, ALU.mult))
                        for k in range(1, kk):
                            ch(v.scalar_tensor_tensor(yg[:, u, 0, :], yg[:, u, k, :], e.gate[:, i, k:k + 1], yg[:, u, 0, :], ALU.mult, ALU.add))
                        v.scalar_tensor_tensor(e.x[:, i, :], yg[:, u, 0, :], e.tg[:, 2 + layer:3 + layer], e.x[:, i, :], ALU.mult, ALU.add).then_inc(added, 1)
                        if not last_layer:
                            dve.wait_ge(added, i + 1)
                            v.bn_stats(e.stats[:, i, :], e.x[:, i, :])

        @block.sync
        def _(sp):
            if last_layer:
                o = e.out.rearrange("b (t p) d -> p (b t) d", p=P)
                with sp.Fori(0, NTILE) as i:
                    sp.wait_ge(added, i + 1)
                    sp.dma_start(o[:, i, :], e.x[:, i, :]).then_inc(stored, 16)
                sp.wait_ge(stored, 16 * NTILE)


def attention_buffers(e):
    o = [ATT0]

    def buf(shape, dt=F32):
        got = e.carve(o[0], shape, dt)
        o[0] += int(np.prod(shape)) * (2 if dt == BF16 else 4)
        assert o[0] <= TOP, o[0]
        return got

    e.v_all = buf([B, MT, D])
    mark = o[0]
    e.xn_a = buf([4, D]); e.xT_a = buf([DK, HB]); e.parts = buf([4, 3, HB], BF16); e.left = buf([4, HB])
    o[0] = mark
    e.q_aug = [buf([GH, S], BF16) for _ in range(2)]
    e.k_aug = [buf([GH, KEYS + 1], BF16) for _ in range(2)]
    e.v_g = [buf([MT, GH, HD + 1]) for _ in range(2)]
    e.prob = [buf([GH, HB]) for _ in range(2)]
    e.oT = buf([HB])
    e.mx = buf([GH, TPB]); e.mxc = buf([GH, TPB]); e.neg = buf([GH, 3, TPB], BF16); e.rest = buf([GH, TPB]); e.negT = buf([P], BF16)
    e.rec = buf([4, GH])
    e.att = e.carve(0, [NTILE, D], base=e.scr)


def project_qkv(e):
    nc, ps, sem, a = e.nc, e.ps, e.sem, e.a
    step, var_ready, std_ready = sem("qkv_step"), sem("qkv_var"), sem("qkv_std")
    xn_ready, xT_raw, xT_ready, v_raw, v_done = (sem("qkv_" + n) for n in ("xn_ready", "xT_raw", "xT_ready", "v_raw", "v_done"))
    unit_raw, part0, left1, part1, unit_done = (sem("qkv_" + n) for n in ("unit_raw", "part0", "left1", "part1", "unit_done"))
    c_raw, stored = sem("qkv_c_raw"), [sem(f"qkv_stored{n}") for n in range(4)]
    U = 4
    CH = NTOK // HB
    qp = e.qp.rearrange("c (k p) t -> k p c t", p=P)
    kp = e.kp.rearrange("c (k p) b t -> k p b c t", p=P)
    SCALE = (float(HD) ** -0.5, 1.0)
    UB = 4

    with nc.Block() as block:
        def chunks(eng, body):
            with eng.Fori(0, B) as b, eng.Fori(0, CH // B) as h:
                body(b, h, b * (CH // B) + h)

        @block.sync
        def _(sp):
            for ex in range(EARLY):
                load_w13(e, sp, ex)
            for n in range(4):
                sp.wait_ge(unit_done, n + 1)
                sp.dma_start(kp[n % DK, :, n // DK, :, 0:CL], e.parts[:, n, :, 0:CL]).then_inc(stored[n], 16)

            def body(b, h, c):
                for n in range(4):
                    sp.wait_ge(unit_done, c * 4 + (5 + n))
                    if n < 2:
                        dst = qp[n, :, :, bass.ds(c * HB, HB)]
                    else:
                        dst = kp[n - 2, :, b, :, bass.ds(h * HB + CL, HB)]
                    sp.dma_start(dst, e.parts[:, n, :, :]).then_inc(stored[n], 16)

            chunks(sp, body)
            for n in range(4):
                sp.wait_ge(stored[n], 16 * (CH + 1))

        @block.tensor
        def _(pe):
            for n in range(4):
                nc.tensor.transpose(ps[:, UB + n, 0:CL], e.ctx[:, n // DK, (n % DK) * P:(n % DK + 1) * P], e.ident[0:CL, 0:CL]).then_inc(unit_raw, 1)

            def body(b, h, c):
                for u in range(U):
                    pe.wait_ge(xn_ready, c * U + u + 1)
                    for k in range(DK):
                        last = nc.tensor.transpose(ps[:, u % 2, k * P:(k + 1) * P], e.xn_a[:, u, k * P:(k + 1) * P], e.ident[:])
                    last.then_inc(xT_raw, 1)
                    pe.wait_ge(xT_ready, c * U + u + 1)
                    pe.wait_ge(v_done, c * U + u + 1)
                    for k in range(DK):
                        last = nc.tensor.matmul(ps[:, 2 + u % 2, 0:D], e.xT_a[:, k, u * P:(u + 1) * P], e.wqkvT[:, k, 2 * D:3 * D], start=(k == 0), stop=(k == DK - 1))
                    last.then_inc(v_raw, 1)
                for n in range(4):
                    pe.wait_ge(left1, c * 4 + (n + 1))
                    for k in range(DK):
                        last = nc.tensor.matmul(ps[:, UB + n, :], e.wqkvT[:, k, n * P:(n + 1) * P], e.xT_a[:, k, :], start=(k == 0), stop=(k == DK - 1))
                    last.then_inc(unit_raw, 1)

            chunks(pe, body)

        @block.scalar
        def _(act):
            act.wait_ge(var_ready, 1)
            nc.scalar.activation(e.std[:], e.ve[:], ACT.Sqrt).then_inc(std_ready, 1)

            def first_part(n, w, scale):
                nc.scalar.activation(e.parts[:, n, 0, 0:w], ps[:, UB + n, 0:w], ACT.Copy, scale=scale).then_inc(part0, 1)

            def second_part(n, w):
                nc.scalar.activation(e.parts[:, n, 1, 0:w], e.left[:, n, 0:w], ACT.Copy).then_inc(part1, 1)

            for n in range(4):
                act.wait_ge(unit_raw, n + 1)
                first_part(n, CL, 1.0)
            for n in range(4):
                act.wait_ge(left1, n + 1)
                second_part(n, CL)

            def body(b, h, c):
                for u in range(U):
                    act.wait_ge(xT_raw, c * U + u + 1)
                    nc.scalar.activation(e.xT_a[:, :, u * P:(u + 1) * P], ps[:, u % 2, 0:D].rearrange("p (k t) -> p k t", k=DK), ACT.Copy).then_inc(xT_ready, 1)
                for n in range(4):
                    act.wait_ge(unit_raw, c * 4 + (5 + n))
                    act.wait_ge(stored[n], c * 16 + 16)
                    first_part(n, HB, SCALE[n // 2])
                for n in range(4):
                    act.wait_ge(left1, c * 4 + (5 + n))
                    second_part(n, HB)

            chunks(act, body)

        @block.vector
        def _(dve):
            v = nc.vector
            ch = Chain(dve, step)
            moments(ch, nc, e.stats, D, e.mean[:], e.var[:], e.ve[:], [e.tmp[:, n, :] for n in range(4)], LN_EPS)
            v.engine_nop().then_inc(var_ready, 1)
            dve.wait_ge(std_ready, 1)
            ch(v.reciprocal(e.rstd[:], e.std[:]))
            for b in range(B):
                v.tensor_copy(e.v_all[0:CL, b, 0, :], e.ctx[:, b, D:2 * D])
            dve.sem_inc(v_done, 2)

            def split(n, at, w, scale):
                dve.wait_ge(part0, at)
                v.scalar_tensor_tensor(e.left[:, n, 0:w], ps[:, UB + n, 0:w], scale, e.parts[:, n, 0, 0:w], ALU.mult, ALU.subtract).then_inc(left1, 1)

            def third(n, at, w):
                dve.wait_ge(part1, at)
                v.tensor_tensor(e.parts[:, n, 2, 0:w], e.left[:, n, 0:w], e.parts[:, n, 1, 0:w], ALU.subtract).then_inc(unit_done, 1)

            for n in range(4):
                split(n, n + 1, CL, 1.0)
            for n in range(4):
                third(n, n + 1, CL)

            def body(b, h, c):
                for u in range(U):
                    i = c * U + u
                    v.tensor_scalar(e.xn_a[:, u, :], e.x[:, i, :], e.mean[:, bass.ds(i, 1)], e.rstd[:, bass.ds(i, 1)], ALU.subtract, ALU.mult).then_inc(xn_ready, 1)
                for u in range(U):
                    dve.wait_ge(v_raw, c * U + u + 1)
                    v.tensor_copy(e.v_all[:, b, h * U + (1 + u), :], ps[:, 2 + u % 2, 0:D]).then_inc(v_done, 1)
                for n in range(4):
                    split(n, c * 4 + (5 + n), HB, SCALE[n // 2])
                for n in range(4):
                    third(n, c * 4 + (5 + n), HB)

            chunks(dve, body)


def load_w13(e, eng, ex):
    eng.dma_start(e.w13[:, ex, :, 0:I1], e.a["L1_ffn_w1"][ex].rearrange("(k p) i -> p k i", p=P)).then_inc(e.w13_in, 16)
    eng.dma_start(e.w13[:, ex, :, I1:2 * I1], e.a["L1_ffn_w3"][ex].rearrange("(k p) i -> p k i", p=P)).then_inc(e.w13_in, 16)


STEPS = 2 * MT
UNITS = GH * TPB
MAX_FROM, MAX_TO = 2, 15
NEG_AT, TURN_AT = 15, 16
HALF_AT, PREV_AT = MT + 1, 1


def units_at(s):
    span = MAX_TO - MAX_FROM
    lo, hi = (min(max(z - MAX_FROM, 0), span) * UNITS // span for z in (s, s + 1))
    return range(lo, hi)


def attend(e):
    nc, ps, sem = e.nc, e.ps, e.sem
    loaded = [sem(f"at_loaded{u}") for u in range(2)]
    max_in = [sem(f"at_max_in{u}") for u in range(2)]
    v_ready, ones_set, psum_set = sem("at_v_ready"), sem("at_ones_set"), sem("at_psum_set")
    max_raw, max_done, misc_raw, misc_done = (sem("at_" + n) for n in ("max_raw", "max_done", "misc_raw", "misc_done"))
    neg_ready, negT_ready, step = sem("at_neg_ready"), sem("at_negT_ready"), sem("at_step")
    s_raw, p_ready, pv_done, half_raw, half_out = (sem("at_" + n) for n in ("s_raw", "p_ready", "pv_done", "half_raw", "half_out"))
    MAXB, SB, AB, MB = 0, 4, 6, 7
    LOADS = 2 * len(QB)
    PER_NEXT, PER_GROUP = TPB + 1, TPB + 3
    REDUCE = UNITS + 1

    def misc_base(g):
        if isinstance(g, int) and g == 0:
            return PER_NEXT
        return g * PER_GROUP + (PER_NEXT - 1)

    def groups(eng, body):
        body(0, 0, True, False)
        with eng.Fori(0, (NGRP - 2) // 2) as t:
            for u in range(2):
                body(t * 2 + (1 + u), (1 + u) % 2, False, False)
        body(NGRP - 1, (NGRP - 1) % 2, False, True)

    def batch_of(g):
        return g // (NGRP // B), g % (NGRP // B)

    def key_rows(mt):
        return (0, CL) if mt == 0 else (CL + (mt - 1) * P, P)

    def extras(g, s, first, last):
        if s == PREV_AT and not first:
            yield "half", 1
        if s == HALF_AT:
            yield "half", 0
        if not last:
            for n in units_at(s):
                yield "max", n
                if n % GH == GH - 1:
                    yield "ctx", n // GH
            if s == NEG_AT:
                yield "neg", 0
            if s == TURN_AT:
                yield "turn", 0

    class Odds:

        def __init__(self):
            self.base, self.n = 0, 0

        def at(self, base):
            self.base, self.n = base, 0

        def next(self):
            self.n += 1
            return self.base + (self.n - 1)

    with nc.Block() as block:
        @block.sync
        def _(sp):
            qv = e.qp.rearrange("c (g h r) t -> c g r h t", h=GH, r=HD)
            kv = e.kp.rearrange("c (g h r) b t -> c g r h b t", h=GH, r=HD)

            def load(g, u):
                b, gg = batch_of(g)
                for n, (cq, ck) in enumerate(zip(QB, KB)):
                    rows = slice(n * HD, (n + 1) * HD)
                    sp.dma_start(e.q_aug[u][rows, :, :], qv[cq, gg, :, :, bass.ds(b * S, S)]).then_inc(loaded[u], 16)
                    sp.dma_start(e.k_aug[u][rows, :, 0:KEYS], kv[ck, gg, :, :, b, :]).then_inc(loaded[u], 16)

            def maxima(g, u):
                sp.wait_ge(negT_ready, g + 1)
                for h in range(GH):
                    for c in range(3):
                        lo = (h * 3 + c) * TPB
                        sp.dma_start(e.q_aug[u][QROWS + c:QROWS + c + 1, h, :].rearrange("o (t n) -> o t n", n=P),
                                     e.negT[lo:lo + TPB, :]).then_inc(max_in[u], 16)

            load(0, 0)
            maxima(0, 0)

            def body(g, u, first, last):
                if last:
                    return
                if not first:
                    sp.wait_ge(pv_done, g * STEPS)
                load(g + 1, 1 - u)
                maxima(g + 1, 1 - u)

            groups(sp, body)

        @block.gpsimd
        def _(pool):
            g_ = nc.gpsimd
            for u in range(2):
                g_.memset(e.k_aug[u][QROWS:AROWS, :, :], 1.0).then_inc(ones_set, 1)
                pool.wait_ge(ones_set, 2 * u + 1)
                g_.memset(e.v_g[u][:, :, :, HD:HD + 1], 1.0).then_inc(ones_set, 1)
                pool.wait_ge(ones_set, 2 * u + 2)

            def values(g, u):
                b, gg = batch_of(g)
                cols = e.v_all[:, b, :, bass.ds(gg * (GH * HD), GH * HD)]
                g_.tensor_copy(e.v_g[u][0:CL, 0, :, 0:HD], cols[0:CL, 0, :].rearrange("p (h r) -> p h r", h=GH)).then_inc(v_ready, 1)
                for mt in range(1, MT):
                    pool.wait_ge(v_ready, g * MT + mt)
                    pool.sem_inc(ones_set, 1)
                    g_.tensor_copy(e.v_g[u][:, mt, :, 0:HD], cols[:, mt, :].rearrange("p (h r) -> p h r", h=GH)).then_inc(v_ready, 1)

            values(0, 0)

            def body(g, u, first, last):
                if last:
                    return
                if not first:
                    pool.wait_ge(pv_done, g * STEPS)
                    pool.sem_inc(ones_set, 1)
                values(g + 1, 1 - u)

            groups(pool, body)

        @block.tensor
        def _(pe):
            odds = Odds()

            def odd():
                n = odds.next()
                if not (isinstance(n, int) and n == 0):
                    pe.wait_ge(misc_done, n)

            def maximum(g, u, n):
                nt, h = divmod(n, GH)
                if not (isinstance(g, int) and g == 0 and n < 2):
                    pe.wait_ge(max_done, g * REDUCE + (n - 1))
                for c in range(2):
                    ins = nc.tensor.matmul(ps[:, MAXB + 2 * (n % 2) + c, :], e.q_aug[u][0:QROWS, h, nt * P:(nt + 1) * P],
                                           e.k_aug[u][0:QROWS, h, CL + c * HB:CL + (c + 1) * HB], start=True, stop=True)
                ins.then_inc(max_raw, 1)

            def context_max(g, u, nt):
                odd()
                for h in range(GH):
                    ins = nc.tensor.matmul(ps[:, MB, h * CL:(h + 1) * CL], e.q_aug[u][0:QROWS, h, nt * P:(nt + 1) * P],
                                           e.k_aug[u][0:QROWS, h, 0:CL], start=True, stop=True)
                ins.then_inc(misc_raw, 1)

            def turn_maxima(g):
                pe.wait_ge(neg_ready, g + 1)
                odd()
                nc.tensor.transpose(ps[0:QROWS, MB, 0:P // 2].bitcast(BF16), e.neg.rearrange("p h c t -> p (h c t)"), e.identb[:]).then_inc(misc_raw, 1)

            def turn_half(count):
                pe.wait_ge(half_out, count)
                odd()
                for t in range(4):
                    ins = nc.tensor.transpose(ps[:, MB, t * P:(t + 1) * P], e.oT[:, t * P:(t + 1) * P], e.ident[:])
                ins.then_inc(misc_raw, 1)

            def weigh(g, u, s):
                mt = s % MT
                k0, rows = key_rows(mt)
                pe.wait_ge(p_ready, g * (GH * STEPS) + GH * (s + 1))
                if mt == 0 and not (isinstance(g, int) and g == 0 and s == 0):
                    pe.wait_ge(half_out, g * 2 + s // MT)
                for h in range(GH):
                    ins = nc.tensor.matmul(ps[h * 32:h * 32 + HD + 1, AB, :], e.v_g[u][0:rows, mt, h, :], e.prob[s % 2][0:rows, h, :],
                                           start=(mt == 0), stop=(mt == MT - 1))
                ins.then_inc(pv_done, 1)

            def score(g, u, s, h):
                nh, mt = divmod(s, MT)
                k0, rows = key_rows(mt)
                n = s * GH + h
                if not (isinstance(g, int) and g == 0 and n < 2):
                    pe.wait_ge(p_ready, g * (GH * STEPS) + (n - 1))
                nc.tensor.matmul(ps[0:rows, SB + h % 2, :], e.k_aug[u][0:AROWS, h, k0:k0 + rows],
                                 e.q_aug[u][0:AROWS, h, nh * HB:(nh + 1) * HB], start=True, stop=True).then_inc(s_raw, 1)

            def extra(g, u, what, n):
                if what == "max":
                    maximum(g, u, n)
                if what == "ctx":
                    context_max(g, u, n)
                if what == "turn":
                    turn_maxima(g)

            pe.wait_ge(ones_set, 4)
            pe.wait_ge(psum_set, 1)
            pe.wait_ge(loaded[0], 16 * LOADS)
            odds.at(0)
            for n in range(UNITS):
                maximum(0, 0, n)
                if n % GH == GH - 1:
                    context_max(0, 0, n // GH)
            turn_maxima(0)

            def body(g, u, first, last):
                odds.at(misc_base(g))
                pe.wait_ge(max_in[u], (g // 2) * (16 * 3 * GH) + 16 * 3 * GH if isinstance(g, int) else half_of(g, u) * (16 * 3 * GH) + 16 * 3 * GH)
                pe.wait_ge(v_ready, g * MT + MT)
                for s in range(STEPS):
                    if s == MAX_FROM and not last:
                        pe.wait_ge(loaded[1 - u], next_of(g, u) * (16 * LOADS) + 16 * LOADS)
                    score(g, u, s, 0)
                    score(g, u, s, 1)
                    if s > 0:
                        weigh(g, u, s - 1)
                    score(g, u, s, 2)
                    score(g, u, s, 3)
                    for what, n in extras(g, s, first, last):
                        if what == "half":
                            turn_half(g * 2 + 1 - n)
                        else:
                            extra(g + 1, 1 - u, what, n)
                weigh(g, u, STEPS - 1)

            groups(pe, body)
            odds.at(NGRP * PER_GROUP - 1)
            turn_half(NGRP * 2)

        @block.scalar
        def _(act):
            def body(g, u, first, last):
                for s in range(STEPS):
                    mt = s % MT
                    rows = key_rows(mt)[1]
                    for h in range(GH):
                        act.wait_ge(s_raw, g * (GH * STEPS) + (s * GH + h + 1))
                        if h == 0 and not (isinstance(g, int) and g == 0 and s < 2):
                            act.wait_ge(pv_done, g * STEPS + (s - 1))
                        nc.scalar.activation(e.prob[s % 2][0:rows, h, :], ps[0:rows, SB + h % 2, :], ACT.Exp).then_inc(p_ready, 1)
                    if s == MT:
                        out(g, 0)
                out(g, 1)

            def out(g, n):
                act.wait_ge(pv_done, g * STEPS + (n + 1) * MT)
                if not (isinstance(g, int) and g == 0 and n == 0):
                    act.wait_ge(half_raw, g * 2 + n)
                nc.scalar.activation(e.oT, ps[:, AB, :], ACT.Copy).then_inc(half_out, 1)

            groups(act, body)

        @block.vector
        def _(dve):
            v = nc.vector
            ch = Chain(dve, step)
            odds = Odds()
            v.memset(ps[:, AB, :], 0.0).then_inc(psum_set, 1)

            def maximum(g, n):
                nt, h = divmod(n, GH)
                dve.wait_ge(max_raw, g * UNITS + (n + 1))
                v.tensor_reduce(e.mx[:, h, nt:nt + 1], ps[:, MAXB + 2 * (n % 2):MAXB + 2 * (n % 2) + 2, :].rearrange("p a b -> p (a b)"), AX.X, ALU.max).then_inc(max_done, 1)

            def context_max(g, nt):
                dve.wait_ge(misc_raw, odds.next() + 1)
                v.tensor_reduce(e.mxc[:, :, nt], ps[:, MB, 0:GH * CL].rearrange("p (h c) -> p h c", h=GH), AX.X, ALU.max).then_inc(misc_done, 1)

            def negate(g):
                v.engine_nop().then_inc(max_done, 1)
                dve.wait_ge(max_done, g * REDUCE + REDUCE)
                ch(v.tensor_tensor(e.mx, e.mx, e.mxc, ALU.max))
                ch(v.tensor_scalar(e.neg[:, :, 0, :], e.mx, -1.0, None, ALU.mult))
                ch(v.scalar_tensor_tensor(e.rest, e.mx, -1.0, e.neg[:, :, 0, :], ALU.mult, ALU.subtract))
                ch(v.tensor_copy(e.neg[:, :, 1, :], e.rest))
                v.tensor_tensor(e.neg[:, :, 2, :], e.rest, e.neg[:, :, 1, :], ALU.subtract).then_inc(neg_ready, 1)

            def turned(g, u):
                dve.wait_ge(misc_raw, odds.next() + 1)
                if not (isinstance(g, int) and g == 0):
                    dve.wait_ge(max_in[1 - u], last_of(g, u) * (16 * 3 * GH) + 16 * 3 * GH)
                v.tensor_copy(e.negT[0:QROWS, :], ps[0:QROWS, MB, 0:P // 2].bitcast(BF16)).then_inc(negT_ready, 1)
                v.engine_nop().then_inc(misc_done, 1)

            def finish_half(b, gg, n):
                dve.wait_ge(misc_raw, odds.next() + 1)
                o = ps[:, MB, :].rearrange("p (t h c) -> p t h c", t=4, h=GH)
                ch(v.reciprocal(e.rec, o[:, :, :, HD]))
                for t in range(4):
                    ins = v.tensor_tensor(e.att[:, b * TPB + (n * 4 + t), bass.ds(gg * (GH * HD), GH * HD)].rearrange("p (h r) -> p h r", h=GH),
                                          o[:, t, :, 0:HD], e.rec[:, t, :].unsqueeze(2).broadcast_to([P, GH, HD]), ALU.mult)
                ins.then_inc(half_raw, 1)
                v.engine_nop().then_inc(misc_done, 1)

            def prologue():
                odds.at(0)
                for n in range(UNITS):
                    maximum(0, n)
                    if n % GH == GH - 1:
                        context_max(0, n // GH)
                negate(0)
                turned(0, 0)

            def body(g, u, first, last):
                odds.at(misc_base(g))
                for s in range(STEPS):
                    for what, n in extras(g, s, first, last):
                        if what == "half":
                            finish_half(*batch_of(g - n), n)
                        if what == "max":
                            maximum(g + 1, n)
                        if what == "ctx":
                            context_max(g + 1, n)
                        if what == "neg":
                            negate(g + 1)
                        if what == "turn":
                            turned(g + 1, 1 - u)

            prologue()
            per = {False: 4 + 2, True: 4 + 1}
            body(0, 0, True, False)
            with dve.Fori(0, (NGRP - 2) // 2) as t:
                with ch.turns(t, 2 * per[False], (NGRP - 2) // 2):
                    for u in range(2):
                        body(t * 2 + (1 + u), (1 + u) % 2, False, False)
            body(NGRP - 1, (NGRP - 1) % 2, False, True)
            odds.at(NGRP * PER_GROUP - 1)
            finish_half(*batch_of(NGRP - 1), 1)


def half_of(g, u):
    return (g - u) // 2


def next_of(g, u):
    return (g + 1 - (1 - u)) // 2


def last_of(g, u):
    return (g - 1 - (1 - u)) // 2


def project_out(e):
    nc, ps, sem, a = e.nc, e.ps, e.sem, e.a
    in_ready, aT_raw, aT_ready, o_raw, biased, x_new = (sem("pj_" + n) for n in ("in_ready", "aT_raw", "aT_ready", "o_raw", "biased", "x_new"))
    U = 4
    at = ATT0 + (E1 - EARLY) * W13_BYTES
    rows = e.carve(at, [U, D])
    aT = e.carve(at + U * D * 4, [U, DK, P])
    sums = e.carve(at + 2 * U * D * 4, [U, D])
    TURNS = NTILE // U

    with nc.Block() as block:
        @block.sync
        def _(sp):
            for ex in range(EARLY, E1):
                load_w13(e, sp, ex)

        @block.gpsimd
        def _(pool):
            with pool.Fori(0, TURNS) as t:
                for u in range(U):
                    i = t * U + u
                    pool.wait_ge(x_new, i + 1)
                    pool.sem_inc(biased, 1)
                    nc.gpsimd.tensor_copy(rows[:, u, :], e.att[:, i, :]).then_inc(in_ready, 1)

        @block.tensor
        def _(pe):
            with pe.Fori(0, TURNS) as t:
                for u in range(U):
                    pe.wait_ge(in_ready, t * U + u + 1)
                    for k in range(DK):
                        last = nc.tensor.transpose(ps[:, u, k * P:(k + 1) * P], rows[:, u, k * P:(k + 1) * P], e.ident[:])
                    last.then_inc(aT_raw, 1)
                for u in range(U):
                    pe.wait_ge(aT_ready, t * U + u + 1)
                    for k in range(DK):
                        last = nc.tensor.matmul(ps[:, 4 + u, 0:D], aT[:, u, k, :], e.wprojT[:, k, :], start=(k == 0), stop=(k == DK - 1))
                    last.then_inc(o_raw, 1)

        @block.scalar
        def _(act):
            with act.Fori(0, TURNS) as t:
                for u in range(U):
                    act.wait_ge(aT_raw, t * U + u + 1)
                    nc.scalar.activation(aT[:, u, :, :].rearrange("p k t -> p (k t)"), ps[:, u, 0:D], ACT.Copy).then_inc(aT_ready, 1)

        @block.vector
        def _(dve):
            v = nc.vector
            step = sem("pj_step")
            ch = Chain(dve, step)
            dve.sem_inc(x_new, U)
            with dve.Fori(0, TURNS) as t:
                with ch.turns(t, U, TURNS):
                    for u in range(U):
                        i = t * U + u
                        dve.wait_ge(o_raw, i + 1)
                        ch(v.tensor_tensor(sums[:, u, :], ps[:, 4 + u, 0:D], e.bproj, ALU.add))
                        v.scalar_tensor_tensor(e.x[:, i, :], sums[:, u, :], e.tg[:, 1:2], e.x[:, i, :], ALU.mult, ALU.add).then_inc(x_new, 1)
                        dve.wait_ge(x_new, i + (U + 1))
                        v.bn_stats(e.stats[:, i, :], e.x[:, i, :])


def load_w2(e):
    nc, a = e.nc, e.a
    with nc.Block() as block:
        @block.sync
        def _(sp):
            for ex in range(E1):
                sp.dma_start(e.w2b[0:IH, ex, :, :], a["L1_ffn_w2"][ex].rearrange("(k p) d -> p k d", p=IH)).then_inc(e.w2_in, 16)


def flamingo_block(nc, out, **inputs):
    with ExitStack() as ctx:
        e = make_env(nc, ctx, inputs, out)
        attention_buffers(e)
        for stage, *args in ((prepare,), (depool_mixer,), (router, 0), (route, 0), (experts0,), (combine, 0)):
            stage(e, *args)
        nc.clear_and_free_semaphores(e.used)
        nc.all_engine_barrier()
        e.used = []
        for stage, *args in ((project_qkv,), (attend,), (project_out,), (router, 1), (route, 1), (load_w2,), (experts1,), (combine, 1)):
            stage(e, *args)


NAMES = ("x", "ctx_2048", "mask_BxS2_if0", "g_xattn", "g_ffn", "L0_xattn_W_in", "L0_xattn_b_in", "L0_xattn_g_res", "L0_xattn_g_init",
         "L0_ffn_Wr", "L0_ffn_br", "L0_ffn_W1", "L0_ffn_b1", "L0_ffn_W2", "L0_ffn_b2", "L1_xattn_w_qkv", "L1_xattn_w_proj",
         "L1_xattn_b_proj", "L1_ffn_gate_w", "L1_ffn_w1", "L1_ffn_w3", "L1_ffn_w2", "L1_ffn_e_bias")


def kernel(**inputs):
    import concourse.bacc as bacc
    from concourse.bass_utils import run_bass_kernel_spmd

    nc = bacc.Bacc("TRN2", target_bir_lowering=False, num_devices=1)
    arrays = {"in_" + n: np.ascontiguousarray(inputs[n]) for n in NAMES}
    aps = {n: nc.dram_tensor("in_" + n, arrays["in_" + n].shape, mybir.dt.from_np(arrays["in_" + n].dtype), kind="ExternalInput").ap() for n in NAMES}
    out = nc.dram_tensor("out", (B, S, D), F32, kind="ExternalOutput").ap()
    flamingo_block(nc, out, **aps)
    return run_bass_kernel_spmd(nc, [arrays], core_ids=[0]).results[0]["out"]
```

```python
from contextlib import ExitStack, contextmanager

import numpy as np
import concourse.bass as bass
from concourse import mybir

F32 = mybir.dt.float32
BF16 = mybir.dt.bfloat16
U32 = mybir.dt.uint32
I32 = mybir.dt.int32
ALU = mybir.AluOpType
ACT = mybir.ActivationFunctionType
AX = mybir.AxisListType

P = 128
B, S, D = 2, 1024, 256
DK = D // P
NTOK = B * S
NTILE = NTOK // P
TPB = S // P
CL, CD = 77, 512
HB = 512

E0, K0, H0 = 8, 2, 1024
HK0 = H0 // P
E1, K1, I1 = 32, 4, 192
IH = I1 // 2
NT0 = (NTOK * K0 - E0) // P + E0
NT1 = (NTOK * K1 - E1) // P + E1
RING0, RING1 = 3, 4

HEADS, HD = 16, D // 16
GH = 4
NGRP = B * HEADS // GH
KEYS = CL + S
MT = 1 + TPB
QB = (0, 0, 1, 1, 0, 2)
KB = (0, 1, 0, 1, 2, 0)
QROWS = len(QB) * HD
AROWS = QROWS + 3

LN_EPS = 1e-5
RMS_EPS = 1e-5
PATCH_EPS = 1e-3

W1_0, W2_0 = 0, E0 * DK * H0 * 4
ARENA0_END = W2_0 + E0 * HK0 * D * 4
W13_BYTES = DK * 2 * I1 * 4
W2_1 = E1 * W13_BYTES
ARENA = W2_1 + E1 * 2 * D * 4
TOP = ARENA - (DK * D + D + DK * E1) * 4
EARLY = 26
ATT0 = EARLY * W13_BYTES


class Memory:
    pass


class Chain:

    def __init__(self, eng, sem, carrier=None):
        self.eng, self.sem, self.base, self.k, self.it, self.per, self.carrier = eng, sem, 0, 0, None, 0, carrier

    def __call__(self, ins):
        self.k += 1
        ins.then_inc(self.sem, 1)
        at = self.base + self.k
        self.eng.wait_ge(self.sem, at if self.it is None else self.it * self.per + at)
        if self.carrier is not None:
            self.eng.sem_inc(self.carrier, 1)

    @contextmanager
    def turns(self, it, per, times):
        self.base, self.k, self.it, self.per = self.base + self.k, 0, it, per
        yield
        assert self.k == per, (self.k, per)
        self.base, self.k, self.it = self.base + per * times, 0, None


def tile_loop(eng, n, ring, body):
    for j in range(ring + 1):
        body(j, j % ring, j // ring, j == 0, False)
    turns = (n - 2 - ring) // ring
    with eng.Fori(1, 1 + turns) as t:
        for u in range(ring):
            body(t * ring + (1 + u), (1 + u) % ring, t + (1 + u) // ring, False, False)
    for j in range(1 + ring + turns * ring, n):
        body(j, j % ring, j // ring, False, j == n - 1)


def moments(ch, nc, stats, n, mean, var, ve, tmp, eps):
    v = nc.vector
    v.tensor_tensor(tmp[0], stats[:, :, 1], stats[:, :, 4], ALU.add)
    v.tensor_tensor(tmp[1], stats[:, :, 1], stats[:, :, 4], ALU.subtract)
    ch(v.tensor_tensor(tmp[2], stats[:, :, 2], stats[:, :, 5], ALU.add))
    v.tensor_scalar(mean, tmp[0], 0.5, None, ALU.mult)
    ch(v.tensor_tensor(tmp[3], tmp[1], tmp[1], ALU.mult))
    ch(v.tensor_scalar(tmp[2], tmp[2], 1.0 / n, None, ALU.mult))
    ch(v.scalar_tensor_tensor(var, tmp[3], 0.25, tmp[2], ALU.mult, ALU.add))
    ch(v.tensor_scalar(ve, var, eps, None, ALU.add))


def make_env(nc, ctx, a, out):
    e = Memory()
    e.nc, e.a, e.out = nc, a, out

    def sb(name, shape, dt=F32):
        return ctx.enter_context(nc.sbuf_tensor(name, shape, dt))

    e.used = []

    def new_semaphore(name):
        e.used.append(nc.alloc_semaphore(name=name))
        return e.used[-1]

    e.sem = new_semaphore
    e.w0_in, e.w13_in, e.w2_in = (ctx.enter_context(nc.semaphore(n)) for n in ("w0_in", "w13_in", "w2_in"))
    e.x = sb("x_resident", [P, NTILE, D])
    e.arena = sb("arena", [P, ARENA // 4])
    e.scr = sb("scratch", [P, NTILE * D])
    e.ident = sb("ident", [P, P])
    e.identb = sb("identb", [P, P], BF16)
    e.earlier = sb("earlier", [P, P], BF16)
    e.onesb = sb("onesb", [P, P], BF16)
    e.iota = sb("iota", [P, P])
    e.iota_p = sb("iota_p", [P, 1])
    e.steps = sb("steps", [P, NTILE])
    e.stats = sb("stats", [P, NTILE, 6])
    e.mean = sb("mean", [P, NTILE])
    e.rstd = sb("rstd", [P, NTILE])
    e.var = sb("var", [P, NTILE])
    e.ve = sb("ve", [P, NTILE])
    e.std = sb("std", [P, NTILE])
    e.tmp = sb("ln_tmp", [P, 4, NTILE])
    e.tg = sb("tanh_gates", [P, 4])
    e.ebias = sb("ebias", [P, E1])
    e.expert = sb("expert", [1, P], I32)
    e.slot_u = sb("slot_u", [P, NTILE, K1], U32)
    e.token_u = sb("token_u", [P, NT1], U32)
    e.gate = sb("gate", [P, NTILE, K1])
    e.xg = sb("xg", [P, RING1, D])
    e.ysb = sb("ysb", [P, RING1, D])
    e.icol = sb("icol", [P, 4, K1], U32)
    e.ps = ctx.enter_context(nc.psum_tensor("ps", [P, 8, HB], F32))

    def dram(name, shape, dt=F32):
        return nc.dram_tensor(name, shape, dt, kind="Internal").ap()

    e.xn = [dram("xn0", [NTOK, D]), dram("xn1", [NTOK, D])]
    e.y = [dram("y0", [NT0 * P, D]), dram("y1", [NT1 * P, D])]
    e.qp = dram("q_parts", [3, D, NTOK], BF16)
    e.kp = dram("k_parts", [3, D, B, KEYS], BF16)

    def carve(off, shape, dt=F32, base=e.arena):
        n = int(np.prod(shape))
        words = n * (2 if dt == BF16 else 4) // 4
        v = base[:].rearrange("p a b -> p (a b)") if len(base.shape) == 3 else base[:]
        v = v[:, off // 4: off // 4 + words]
        if dt != F32:
            v = v.bitcast(dt)
        if len(shape) == 2:
            v = v.rearrange("p (a b) -> p a b", b=shape[1])
        if len(shape) == 3:
            v = v.rearrange("p (a b c) -> p a b c", b=shape[1], c=shape[2])
        if len(shape) == 4:
            v = v.rearrange("p (a b c d) -> p a b c d", b=shape[1], c=shape[2], d=shape[3])
        return v

    e.carve = carve
    e.w1 = carve(W1_0, [E0, DK, H0])
    e.w2 = carve(W2_0, [E0, HK0, D])
    e.w13 = carve(0, [E1, DK, 2 * I1])
    e.w2b = carve(W2_1, [E1, 2, D])
    o = ARENA0_END
    e.b2bc = carve(o, [E0, D]); o += E0 * D * 4
    e.wqkvT = carve(o, [DK, 3 * D]); o += DK * 3 * D * 4
    e.ctx = carve(o, [B, CD])[0:CL]; o += B * CD * 4
    e.b1T = carve(o, [E0 * HK0]); o += E0 * HK0 * 4
    e.wr = carve(o, [DK, E0]); o += DK * E0 * 4
    e.br = carve(o, [E0]); o += E0 * 4
    e.free0 = o
    e.dep = carve(o, [B, D]); o += B * D * 4
    e.plug = carve(o, [NTOK], BF16); o += NTOK * 2
    e.winT = carve(o, [DK, D]); o += DK * D * 4
    e.free1 = o
    o = TOP
    e.wprojT = carve(o, [DK, D]); o += DK * D * 4
    e.bproj = carve(o, [D]); o += D * 4
    e.gateT = carve(o, [DK, E1])
    return e


def prepare(e):
    nc, a, ps = e.nc, e.a, e.ps
    sem = e.sem
    x_in, small_in, consts = sem("x_in"), sem("small_in"), sem("consts")
    tr_raw, tr_done = sem("prep_tr_raw"), sem("prep_tr_done")
    pool_step, dve_step = sem("prep_pool_step"), sem("prep_dve_step")
    var_ready, std_ready = sem("prep_var"), sem("prep_std")
    u_ready, dep_raw, lens_ready, bidx_raw = sem("u_ready"), sem("dep_raw"), sem("lens_ready"), sem("bidx_raw")
    at_ready, cnt_raw, cnt_used = sem("at_ready"), sem("cnt_raw"), sem("cnt_used")

    wqkv = e.carve(0, [6, D], base=e.scr)
    wproj = e.carve(6 * D * 4, [DK, D], base=e.scr)
    gatew = e.carve(8 * D * 4, [D], base=e.scr)
    b1r = e.carve(9 * D * 4, [P], base=e.scr)
    ginit = e.carve(9 * D * 4 + P * 4, [D], base=e.scr)
    bin_ = e.carve(10 * D * 4 + P * 4, [D], base=e.scr)
    rest = 11 * D * 4 + P * 4
    tri = e.carve(rest, [CL], base=e.scr); rest += CL * 4
    tdec = e.carve(rest, [CL], base=e.scr); rest += CL * 4
    gres = e.carve(rest, [DK], base=e.scr); rest += DK * 4
    lens_i = e.carve(rest, [B], base=e.scr).bitcast(I32); rest += B * 4
    lens = e.carve(rest, [B], base=e.scr); rest += B * 4
    bidx = e.carve(rest, [B], base=e.scr); rest += B * 4
    wrap = e.carve(rest, [B], base=e.scr); rest += B * 4
    cs = e.carve(rest, [B, 6], base=e.scr); rest += B * 24
    cm = e.carve(rest, [8, B], base=e.scr); rest += 8 * B * 4
    g4 = e.carve(rest, [4], base=e.scr); rest += 16
    ones = e.carve(rest, [CL], base=e.scr); rest += CL * 4
    win = e.carve(rest, [DK, D], base=e.scr); rest += DK * D * 4
    assert rest <= NTILE * D * 4, rest
    u = e.carve(e.free1, [B, D])
    assert e.free1 + B * D * 4 <= TOP
    at = e.ysb[:].rearrange("p a b -> p (a b)")[:, 0:S]
    iota_t = e.xg[:].rearrange("p a b -> p (a b)")[:, 0:S]
    N_SMALL = 18

    turn = []
    for dk in range(DK):
        for et in range(DK):
            turn.append((win[:, et, dk * P:(dk + 1) * P], P, e.winT[:, dk, et * P:(et + 1) * P], gres[:, dk:dk + 1]))
        for et in range(6):
            turn.append((wqkv[:, et, dk * P:(dk + 1) * P], P, e.wqkvT[:, dk, et * P:(et + 1) * P], None))
        for et in range(DK):
            turn.append((wproj[:, et, dk * P:(dk + 1) * P], P, e.wprojT[:, dk, et * P:(et + 1) * P], None))
        turn.append((gatew[0:E1, dk * P:(dk + 1) * P], E1, e.gateT[:, dk, :], None))
    turn.append((b1r[0:E0 * HK0, :], E0 * HK0, e.b1T, None))

    dt = float(-np.log(-np.expm1(np.float32(-PATCH_EPS)).astype(np.float32)).astype(np.float32))
    bcoef = float(np.exp(np.float32(-PATCH_EPS)))
    decay = [bcoef * float(np.exp(-dt * k)) for k in range(CL)]
    decay = [w for w in decay if np.float32(w) > 0]

    with nc.Block() as block:
        @block.sync
        def _(sp):
            sp.dma_start(e.x[:], a["x"].rearrange("b (t p) d -> p (b t) d", p=P)).then_inc(x_in, 16)
            for dst, src in (
                (win, a["L0_xattn_W_in"].rearrange("(k p) d -> p k d", p=P)),
                (wqkv, a["L1_xattn_w_qkv"].rearrange("(k p) d -> p k d", p=P)),
                (wproj, a["L1_xattn_w_proj"].rearrange("(k p) d -> p k d", p=P)),
                (gatew[0:E1, :], a["L1_ffn_gate_w"]),
                (b1r[0:E0 * HK0, :], a["L0_ffn_b1"].rearrange("e (k p) -> (e k) p", p=P)),
                (ginit[0:CL, :], a["L0_xattn_g_init"][0:D].partition_broadcast(CL)),
                (bin_[0:CL, :], a["L0_xattn_b_in"].partition_broadcast(CL)),
                (gres, a["L0_xattn_g_res"].rearrange("(k p) -> p k", p=P)),
                (lens_i[0:CL, :], a["mask_BxS2_if0"].rearrange("b s -> s b")),
                (e.ctx, a["ctx_2048"].rearrange("b s d -> s b d")),
                (g4[:, 0:2], a["g_xattn"].partition_broadcast(P)),
                (g4[:, 2:4], a["g_ffn"].partition_broadcast(P)),
                (e.wr, a["L0_ffn_Wr"].rearrange("(k p) e -> p k e", p=P)),
                (e.br, a["L0_ffn_br"].partition_broadcast(P)),
                (e.ebias[:], a["L1_ffn_e_bias"].partition_broadcast(P)),
                (e.bproj, a["L1_xattn_b_proj"].partition_broadcast(P)),
                (e.b2bc, a["L0_ffn_b2"].rearrange("e d -> (e d)").partition_broadcast(P).rearrange("p (e d) -> p e d", d=D)),
            ):
                sp.dma_start(dst, src, allow_slow_non_contiguous=True).then_inc(small_in, 16)
            for ex in range(E0):
                sp.dma_start(e.w1[:, ex], a["L0_ffn_W1"][ex].rearrange("(k p) h -> p k h", p=P)).then_inc(e.w0_in, 16)
                sp.dma_start(e.w2[:, ex], a["L0_ffn_W2"][ex].rearrange("(k p) d -> p k d", p=P)).then_inc(e.w0_in, 16)

        @block.gpsimd
        def _(pool):
            ch = Chain(pool, pool_step)
            g = nc.gpsimd
            g.memset(e.ident[:], 0.0)
            g.memset(e.identb[:], 0.0)
            g.memset(e.earlier[:], 1.0)
            g.memset(e.onesb[:], 1.0)
            g.memset(ones[0:CL, :], 1.0)
            g.memset(tri[0:CL, :], 1.0)
            ch(g.memset(tdec[0:CL, :], 0.0))
            for m in (e.ident, e.identb):
                g.affine_select(out=m[:], in_=m[:], compare_op=ALU.not_equal, fill=1.0, base=0, pattern=[[-1, P]], channel_multiplier=1)
            g.affine_select(out=e.earlier[:], in_=e.earlier[:], compare_op=ALU.is_gt, fill=0.0, base=0, pattern=[[1, P]], channel_multiplier=-1)
            g.affine_select(out=tri[0:CL, :], in_=tri[0:CL, :], compare_op=ALU.is_ge, fill=0.0, base=0, pattern=[[1, CL]], channel_multiplier=-1)
            for k, w in enumerate(decay):
                ch(g.affine_select(out=tdec[0:CL, :], in_=tdec[0:CL, :], compare_op=ALU.not_equal, fill=w, base=-k, pattern=[[1, CL]], channel_multiplier=-1))
            g.iota(iota_t[0:CL, :], pattern=[[1, S]], base=0, channel_multiplier=0, allow_small_or_imprecise_dtypes=True)
            g.iota(e.iota[:], pattern=[[1, P]], base=0, channel_multiplier=0, allow_small_or_imprecise_dtypes=True)
            g.iota(e.iota_p[:], pattern=[[0, 1]], base=0, channel_multiplier=1, allow_small_or_imprecise_dtypes=True)
            ch(g.iota(e.steps[:], pattern=[[P, NTILE]], base=0, channel_multiplier=0, allow_small_or_imprecise_dtypes=True))
            g.drain().then_inc(consts, 1)

        @block.tensor
        def _(pe):
            pe.wait_ge(consts, 1)
            pe.wait_ge(small_in, 16 * (N_SMALL - 1))
            for n, (src, rows, dst, scale) in enumerate(turn):
                if n >= 4:
                    pe.wait_ge(tr_done, n - 3)
                nc.tensor.transpose(ps[:, n % 4, 0:rows], src, e.ident[0:rows, 0:rows]).then_inc(tr_raw, 1)
            pe.wait_ge(lens_ready, 1)
            nc.tensor.matmul(ps[0:CL, 4, 0:B], tri[0:CL, :], lens[0:CL, :], start=True, stop=True).then_inc(bidx_raw, 1)
            for b in range(B):
                pe.wait_ge(u_ready, b + 1)
                nc.tensor.matmul(ps[0:CL, 5 + b, 0:D], tdec[0:CL, :], u[0:CL, b, :], start=True, stop=True).then_inc(dep_raw, 1)
            for b in range(B):
                pe.wait_ge(at_ready, b + 1)
                for h in range(S // HB):
                    if b == 0:
                        pe.wait_ge(tr_done, len(turn))
                    else:
                        pe.wait_ge(cnt_used, b)
                    nc.tensor.matmul(ps[0:CL, h, :], ones[0:CL, 0:CL], at[0:CL, h * HB:(h + 1) * HB], start=True, stop=True).then_inc(cnt_raw, 1)

        @block.scalar
        def _(act):
            act.wait_ge(small_in, 16 * (N_SMALL - 1))
            nc.scalar.activation(e.tg[:], g4, ACT.Tanh)
            for n, (src, rows, dst, scale) in enumerate(turn):
                act.wait_ge(tr_raw, n + 1)
                if scale is None:
                    nc.scalar.activation(dst, ps[:, n % 4, 0:rows], ACT.Copy).then_inc(tr_done, 1)
                else:
                    nc.scalar.activation(dst, ps[:, n % 4, 0:rows], ACT.Copy, scale=scale).then_inc(tr_done, 1)
            act.wait_ge(var_ready, 1)
            nc.scalar.activation(e.std[:], e.ve[:], ACT.Sqrt).then_inc(std_ready, 1)
            act.wait_ge(var_ready, 2)
            nc.scalar.activation(e.std[:], e.ve[:], ACT.Sqrt).then_inc(std_ready, 1)
            act.wait_ge(var_ready, 3)
            nc.scalar.activation(cm[0:CL, 6, :], cm[0:CL, 5, :], ACT.Sqrt).then_inc(std_ready, 1)

        @block.vector
        def _(dve):
            ch = Chain(dve, dve_step)
            v = nc.vector
            dve.wait_ge(x_in, 16)
            with dve.Fori(0, NTILE) as i:
                v.bn_stats(e.stats[:, i, :], e.x[:, i, :])
            ch(v.memset(e.tmp[:, 0, :], 0.0))
            t = [e.tmp[:, n, :] for n in range(4)]
            moments(ch, nc, e.stats, D, e.mean[:], e.var[:], e.ve[:], t, LN_EPS)
            v.engine_nop().then_inc(var_ready, 1)
            dve.wait_ge(std_ready, 1)
            ch(v.reciprocal(e.rstd[:], e.std[:]))
            ch(v.tensor_tensor(e.tmp[:, 0, :], e.rstd[:], e.rstd[:], ALU.mult))
            ch(v.tensor_tensor(e.tmp[:, 1, :], e.tmp[:, 0, :], e.var[:], ALU.mult))
            v.tensor_scalar(e.ve[:], e.tmp[:, 1, :], RMS_EPS, None, ALU.add).then_inc(var_ready, 1)
            dve.wait_ge(std_ready, 2)
            ch(v.reciprocal(e.tmp[:, 2, :], e.std[:]))
            ch(v.tensor_tensor(e.rstd[:], e.rstd[:], e.tmp[:, 2, :], ALU.mult))

            dve.wait_ge(small_in, 16 * (N_SMALL - 1))
            for b in range(B):
                ch(v.bn_stats(cs[0:CL, b, :], e.ctx[:, b, :]))
            c = [cm[0:CL, n, :] for n in range(8)]
            moments(ch, nc, cs[0:CL], CD, c[4], c[5], c[6], c[0:4], RMS_EPS)
            ch(v.tensor_tensor(c[0], c[4], c[4], ALU.mult))
            v.tensor_tensor(c[5], c[0], c[6], ALU.add).then_inc(var_ready, 1)
            dve.wait_ge(std_ready, 3)
            ch(v.reciprocal(c[7], c[6]))
            for b in range(B):
                v.scalar_tensor_tensor(u[0:CL, b, :], e.ctx[:, b, 0:D], cm[0:CL, 7, b:b + 1], ginit[0:CL, :], ALU.mult, ALU.mult).then_inc(u_ready, 1)

            v.tensor_copy(lens[0:CL, :], lens_i[0:CL, :]).then_inc(lens_ready, 1)
            dve.wait_ge(bidx_raw, 1)
            ch(v.tensor_scalar(bidx[0:CL, :], ps[0:CL, 4, 0:B], -1.0, None, ALU.add))
            ch(v.tensor_scalar(wrap[0:CL, :], bidx[0:CL, :], 0.0, float(S), ALU.is_lt, ALU.mult))
            ch(v.tensor_tensor(bidx[0:CL, :], bidx[0:CL, :], wrap[0:CL, :], ALU.add))
            for b in range(B):
                dve.wait_ge(dep_raw, b + 1)
                ch(v.tensor_tensor(e.dep[0:CL, b, :], ps[0:CL, 5 + b, 0:D], bin_[0:CL, :], ALU.add))
            dve.wait_ge(consts, 1)
            for b in range(B):
                row = e.plug[0:CL, b * S:(b + 1) * S]
                v.tensor_scalar(at[0:CL, :], iota_t[0:CL, :], bidx[0:CL, b:b + 1], None, ALU.is_equal).then_inc(at_ready, 1)
                dve.wait_ge(cnt_raw, 2 * b + 2)
                ch(v.tensor_scalar(at[0:CL, :], ps[0:CL, 0:2, :].rearrange("p a b -> p (a b)"), 1.0, None, ALU.min))
                v.engine_nop().then_inc(cnt_used, 1)
                count = ps[0:CL, 2:4, :].rearrange("p a b -> p (a b)")
                ch(v.tensor_tensor_scan(count, at[0:CL, :], at[0:CL, :], 0.0, ALU.add, ALU.max))
                ch(v.tensor_scalar(at[0:CL, :], count, -1.0, 0.0, ALU.add, ALU.max))
                ch(v.tensor_scalar(row, at[0:CL, :], float(CL - 1), None, ALU.min))


def depool_mixer(e):
    nc, ps, sem = e.nc, e.ps, e.sem
    xn_ready, xT_raw, xT_ready = sem("mix_xn_ready"), sem("mix_xT_raw"), sem("mix_xT_ready")
    mixed_raw, x_new = sem("mix_raw"), sem("mix_x_new")
    U = 4
    xn = e.carve(0, [U, D], base=e.scr)
    oh = e.carve(U * D * 4, [U, P], base=e.scr)
    xT = e.carve(U * (D + P) * 4, [U, DK, P], base=e.scr)

    with nc.Block() as block:
        def loop(eng, body):
            with eng.Fori(0, B) as b, eng.Fori(0, TPB // U) as h:
                for u in range(U):
                    body[0](b, h, u, b * TPB + h * U + u, b * (TPB // U) + h)
                if len(body) > 1:
                    for u in range(U):
                        body[1](b, h, u, b * TPB + h * U + u, b * (TPB // U) + h)

        @block.vector
        def _(dve):
            v = nc.vector
            dve.sem_inc(x_new, U)

            def norm(b, h, u, i, t):
                v.tensor_scalar(xn[:, u, :], e.x[:, i, :], e.mean[:, bass.ds(i, 1)], e.rstd[:, bass.ds(i, 1)], ALU.subtract, ALU.mult)
                v.tensor_scalar(oh[0:CL, u, :], e.plug[0:CL, bass.ds(i * P, P)], e.iota_p[0:CL, :], None, ALU.is_equal).then_inc(xn_ready, 1)

            def mix(b, h, u, i, t):
                dve.wait_ge(mixed_raw, i + 1)
                v.scalar_tensor_tensor(e.x[:, i, :], ps[:, 4 + u, 0:D], e.tg[:, 0:1], e.x[:, i, :], ALU.mult, ALU.add).then_inc(x_new, 1)
                dve.wait_ge(x_new, i + (U + 1))
                v.bn_stats(e.stats[:, i, :], e.x[:, i, :])

            loop(dve, (norm, mix))

        @block.tensor
        def _(pe):
            def turn(b, h, u, i, t):
                pe.wait_ge(xn_ready, i + 1)
                for k in range(DK):
                    last = nc.tensor.transpose(ps[:, u, k * P:(k + 1) * P], xn[:, u, k * P:(k + 1) * P], e.ident[:])
                last.then_inc(xT_raw, 1)

            def mix(b, h, u, i, t):
                pe.wait_ge(xT_ready, i + 1)
                pe.wait_ge(x_new, i + 1)
                for k in range(DK):
                    nc.tensor.matmul(ps[:, 4 + u, 0:D], xT[:, u, k, :], e.winT[:, k, :], start=(k == 0), stop=False)
                nc.tensor.matmul(ps[:, 4 + u, 0:D], oh[0:CL, u, :], e.dep[0:CL, b, :], start=False, stop=True).then_inc(mixed_raw, 1)

            loop(pe, (turn, mix))

        @block.scalar
        def _(act):
            def copy(b, h, u, i, t):
                act.wait_ge(xT_raw, i + 1)
                nc.scalar.activation(xT[:, u, :, :].rearrange("p k t -> p (k t)"), ps[:, u, 0:D], ACT.Copy).then_inc(xT_ready, 1)

            loop(act, (copy,))


def router(e, layer):
    nc, ps, sem = e.nc, e.ps, e.sem
    ne = (E0, E1)[layer]
    wr = (e.wr, e.gateT)[layer]
    nm = f"rt{layer}_"
    xn_ready, xT_raw, xT_ready = sem(nm + "xn_ready"), sem(nm + "xT_raw"), sem(nm + "xT_ready")
    lg_raw, lg_done, step = sem(nm + "lg_raw"), sem(nm + "lg_done"), sem(nm + "step")
    var_ready, std_ready = sem(nm + "var"), sem(nm + "std")
    U = 4
    stored = [sem(nm + f"xn_stored{u}") for u in range(U)]
    xn = e.carve(0, [U, D], base=e.scr)
    xT = e.carve(U * D * 4, [U, DK, P], base=e.scr)
    e.logits = e.carve(2 * U * D * 4, [NTILE, ne], base=e.scr)
    TURNS = NTILE // U

    with nc.Block() as block:
        @block.vector
        def _(dve):
            v = nc.vector
            ch = Chain(dve, step)
            moments(ch, nc, e.stats, D, e.mean[:], e.var[:], e.ve[:], [e.tmp[:, n, :] for n in range(4)], LN_EPS)
            v.engine_nop().then_inc(var_ready, 1)
            dve.wait_ge(std_ready, 1)
            ch(v.reciprocal(e.rstd[:], e.std[:]))
            dve.sem_inc(lg_done, U)

            def norm(t, u, wait):
                if wait:
                    dve.wait_ge(stored[u], t * 16)
                i = t * U + u
                v.tensor_scalar(xn[:, u, :], e.x[:, i, :], e.mean[:, bass.ds(i, 1)], e.rstd[:, bass.ds(i, 1)], ALU.subtract, ALU.mult).then_inc(xn_ready, 1)

            def logit(t, u):
                i = t * U + u
                dve.wait_ge(lg_raw, i + 1)
                if layer == 0:
                    v.tensor_tensor(e.logits[:, i, :], ps[:, 4 + u, 0:ne], e.br, ALU.add).then_inc(lg_done, 1)
                else:
                    v.tensor_copy(e.logits[:, i, :], ps[:, 4 + u, 0:ne]).then_inc(lg_done, 1)

            for u in range(U):
                norm(0, u, False)
            for u in range(U):
                logit(0, u)
            with dve.Fori(1, TURNS) as t:
                for u in range(U):
                    norm(t, u, True)
                for u in range(U):
                    logit(t, u)

        @block.scalar
        def _(act):
            act.wait_ge(var_ready, 1)
            nc.scalar.activation(e.std[:], e.ve[:], ACT.Sqrt).then_inc(std_ready, 1)
            with act.Fori(0, TURNS) as t:
                for u in range(U):
                    act.wait_ge(xT_raw, t * U + u + 1)
                    nc.scalar.activation(xT[:, u, :, :].rearrange("p k t -> p (k t)"), ps[:, u, 0:D], ACT.Copy).then_inc(xT_ready, 1)

        @block.sync
        def _(sp):
            with sp.Fori(0, TURNS) as t:
                for u in range(U):
                    i = t * U + u
                    sp.wait_ge(xn_ready, i + 1)
                    sp.dma_start(e.xn[layer][bass.ds(i * P, P), :], xn[:, u, :]).then_inc(stored[u], 16)
            for u in range(U):
                sp.wait_ge(stored[u], 16 * TURNS)

        @block.tensor
        def _(pe):
            with pe.Fori(0, TURNS) as t:
                for u in range(U):
                    pe.wait_ge(xn_ready, t * U + u + 1)
                    for k in range(DK):
                        last = nc.tensor.transpose(ps[:, u, k * P:(k + 1) * P], xn[:, u, k * P:(k + 1) * P], e.ident[:])
                    last.then_inc(xT_raw, 1)
                for u in range(U):
                    pe.wait_ge(xT_ready, t * U + u + 1)
                    pe.wait_ge(lg_done, t * U + u + 1)
                    for k in range(DK):
                        last = nc.tensor.matmul(ps[:, 4 + u, 0:ne], xT[:, u, k, :], wr[:, k, :], start=(k == 0), stop=(k == DK - 1))
                    last.then_inc(lg_raw, 1)


def route(e, layer):
    nc, ps, sem = e.nc, e.ps, e.sem
    ne, kk, nt = ((E0, K0, NT0), (E1, K1, NT1))[layer]
    nm = f"ro{layer}_"
    step, act_in, act_out = sem(nm + "step"), sem(nm + "act_in"), sem(nm + "act_out")
    mask_ready, rank_raw, first_ready, first_raw = sem(nm + "mask"), sem(nm + "rank_raw"), sem(nm + "first"), sem(nm + "first_raw")
    pick_ready, pick_used, token_raw = sem(nm + "pick_ready"), sem(nm + "pick_used"), sem(nm + "token_raw")
    pool_step = sem(nm + "pool_step")
    o = [e.free0 if layer == 0 else ATT0 + (E1 - EARLY) * W13_BYTES]

    def buf(shape, dt=F32):
        got = e.carve(o[0], shape, dt)
        o[0] += int(np.prod(shape)) * (2 if dt == BF16 else 4)
        assert o[0] <= TOP, o[0]
        return got

    N = NTILE * ne
    top = buf([NTILE, 8]); topi = buf([NTILE, 8]).bitcast(U32); topf = buf([NTILE, 8])
    chosen = buf([kk, NTILE, ne])
    mask = buf([NTILE, ne]); maskb = buf([NTILE, ne], BF16)
    place = buf([NTILE, ne]); work = buf([NTILE, ne])
    offs = buf([NTILE + 1, ne])
    many = buf([ne, NTILE]); tiles = buf([ne]); upto = buf([ne]); start = buf([ne]); below = buf([ne])
    first = buf([1])
    slot = buf([NTILE, kk]); slot_i = buf([NTILE, kk]).bitcast(I32)
    part_i = buf([NTILE, kk]).bitcast(I32); part = buf([NTILE, kk]); tile_i = buf([NTILE, kk]).bitcast(I32); tile_f = buf([NTILE, kk])
    token = buf([NTILE, kk])
    W = 4
    row_is = buf([W, P]); col_is = buf([W, nt])
    sel = e.logits
    ex = buf([NTILE, K0]); tot = buf([NTILE])
    if layer == 1:
        sel = buf([NTILE, ne]); sig = buf([NTILE, ne])
    NQ = NTILE * kk

    def bc(ap, n):
        return ap.unsqueeze(2).broadcast_to([P, ap.shape[1], n])

    with nc.Block() as block:
        @block.gpsimd
        def _(pool):
            nc.gpsimd.iota(token, pattern=[[P, NTILE], [0, kk]], base=0, channel_multiplier=1, allow_small_or_imprecise_dtypes=True).then_inc(pool_step, 1)

        @block.scalar
        def _(act):
            act.wait_ge(act_in, 1)
            if layer == 0:
                nc.scalar.activation(ex, ex, ACT.Exp).then_inc(act_out, 1)
            else:
                nc.scalar.activation(sig, e.logits, ACT.Exp, scale=-1.0).then_inc(act_out, 1)

        @block.vector
        def _(dve):
            v = nc.vector
            ch = Chain(dve, step)
            if layer == 1:
                v.engine_nop().then_inc(act_in, 1)
                dve.wait_ge(act_out, 1)
                ch(v.tensor_scalar(sig, sig, 1.0, None, ALU.add))
                ch(v.reciprocal(sig, sig))
                ch(v.tensor_tensor(sel, sig, e.ebias[:].unsqueeze(1).broadcast_to([P, NTILE, ne]), ALU.add))
            for i in range(NTILE):
                v.max(top[:, i, :], sel[:, i, :])
            ch(v.memset(tot, 0.0))
            for i in range(NTILE):
                v.max_index(topi[:, i, :], top[:, i, :], sel[:, i, :])
            ch(v.memset(offs[:, 0, :], 0.0))
            ch(v.tensor_copy(topf, topi))
            for k in range(kk):
                v.tensor_tensor(chosen[:, k], e.iota[:, 0:ne].unsqueeze(1).broadcast_to([P, NTILE, ne]), bc(topf[:, :, k], ne), ALU.is_equal)
            ch(v.memset(tot, 0.0))
            ch(v.tensor_tensor(mask, chosen[:, 0], chosen[:, 1], ALU.add))
            for k in range(2, kk):
                ch(v.tensor_tensor(mask, mask, chosen[:, k], ALU.add))
            v.tensor_copy(maskb, mask).then_inc(mask_ready, 1)

            if layer == 0:
                v.tensor_tensor(ex, top[:, :, 0:kk], bc(top[:, :, 0], kk), ALU.subtract).then_inc(act_in, 1)
                dve.wait_ge(act_out, 1)
                w = ex
            else:
                for k in range(kk):
                    ch(v.tensor_tensor(work, chosen[:, k], sig, ALU.mult))
                    ch(v.tensor_reduce(slot[:, :, k], work, AX.X, ALU.add))
                w = slot
            ch(v.tensor_reduce(tot, w, AX.X, ALU.add))
            ch(v.reciprocal(tot, tot))
            ch(v.tensor_tensor(e.gate[:, :, 0:kk], w, bc(tot, kk), ALU.mult))

            dve.wait_ge(rank_raw, 2)
            for i in range(NTILE):
                ch(v.tensor_tensor(offs[:, i + 1, :], offs[:, i, :], ps[:, 1, i * ne:(i + 1) * ne], ALU.add))
            ch(v.tensor_tensor(many, bc(offs[:, NTILE, :], NTILE), e.steps[:].unsqueeze(1).broadcast_to([P, ne, NTILE]), ALU.is_gt))
            ch(v.tensor_reduce(tiles, many, AX.X, ALU.add))
            ch(v.memset(below, 1.0))
            ch(v.tensor_tensor_scan(upto, below, tiles, 0.0, ALU.mult, ALU.add))
            ch(v.tensor_tensor(start, upto, tiles, ALU.subtract))
            ch(v.tensor_scalar(below, upto, e.iota_p[:], None, ALU.is_le))
            ch(v.tensor_reduce(first, below, AX.X, ALU.add))
            v.tensor_scalar(first, first, float(ne - 1), None, ALU.min).then_inc(first_ready, 1)

            ch(v.tensor_tensor(place, ps[:, 0, 0:N].rearrange("p (i e) -> p i e", e=ne), offs[:, 0:NTILE, :], ALU.add))
            ch(v.scalar_tensor_tensor(place, start.unsqueeze(1).broadcast_to([P, NTILE, ne]), float(P), place, ALU.mult, ALU.add))
            for k in range(kk):
                ch(v.tensor_tensor(work, chosen[:, k], place, ALU.mult))
                ch(v.tensor_reduce(slot[:, :, k], work, AX.X, ALU.add))
            v.tensor_copy(e.slot_u[:, :, 0:kk], slot)
            ch(v.tensor_copy(slot_i, slot))
            ch(v.tensor_scalar(part_i, slot_i, P - 1, None, ALU.bitwise_and))
            ch(v.tensor_scalar(tile_i, slot_i, 7, None, ALU.logical_shift_right))
            ch(v.tensor_copy(part, part_i))
            ch(v.tensor_copy(tile_f, tile_i))
            dve.wait_ge(first_raw, 1)
            ch(v.tensor_copy(e.expert[0:1, :], ps[0:1, 2, 0:P]))

            dve.wait_ge(pool_step, 1)
            pf, tf, kf = (z.rearrange("p i k -> p (i k)") for z in (part, tile_f, token))

            def pick(t, u, wait):
                q = t * W + u
                if wait:
                    dve.wait_ge(pick_used, q - (W - 1))
                v.tensor_scalar(row_is[:, u, :], e.iota[:], pf[:, bass.ds(q, 1)], None, ALU.is_equal)
                v.tensor_scalar(col_is[:, u, :], e.iota[:, 0:nt], tf[:, bass.ds(q, 1)], kf[:, bass.ds(q, 1)], ALU.is_equal, ALU.mult).then_inc(pick_ready, 1)

            for u in range(W):
                pick(0, u, False)
            with dve.Fori(1, NQ // W) as t:
                for u in range(W):
                    pick(t, u, True)
            dve.wait_ge(token_raw, 1)
            v.tensor_copy(e.token_u[:, 0:nt], ps[:, 3, 0:nt])

        @block.tensor
        def _(pe):
            pe.wait_ge(mask_ready, 1)
            m = maskb.rearrange("p i e -> p (i e)")
            nc.tensor.matmul(ps[:, 0, 0:N], e.earlier[:], m, start=True, stop=True).then_inc(rank_raw, 1)
            nc.tensor.matmul(ps[:, 1, 0:N], e.onesb[:], m, start=True, stop=True).then_inc(rank_raw, 1)
            pe.wait_ge(first_ready, 1)
            nc.tensor.transpose(ps[0:1, 2, 0:P], first, e.ident[:]).then_inc(first_raw, 1)

            def pick(q, u, begin, end):
                pe.wait_ge(pick_ready, q + 1)
                ins = nc.tensor.matmul(ps[:, 3, 0:nt], row_is[:, u, :], col_is[:, u, :], start=begin, stop=end)
                ins.then_inc(token_raw if end else pick_used, 1)

            for u in range(W):
                pick(u, u, u == 0, False)
            with pe.Fori(1, NQ // W - 1) as t:
                for u in range(W):
                    pick(t * W + u, u, False, False)
            for q in range(NQ - W, NQ):
                pick(q, q % W, False, q == NQ - 1)


def gather_tiles(e, layer, block, gathered, x_turned):
    nc = e.nc
    nt, ring = ((NT0, RING0), (NT1, RING1))[layer]
    icol_ready, carrier = e.sem(f"ga{layer}_icol_ready"), e.sem(f"ga{layer}_carrier")

    @block.gpsimd
    def _(pool):
        icol = e.icol[:].rearrange("p a b -> p (a b)")

        def body(j, r, turn, first, last):
            if not (isinstance(j, int) and j < ring):
                pool.wait_ge(x_turned, j + (1 - ring))
            nc.gpsimd.tensor_copy(icol[:, r:r + 1], e.token_u[:, bass.ds(j, 1)]).then_inc(icol_ready, 1)
            pool.wait_ge(icol_ready, j + 1)
            pool.sem_inc(carrier, 1)
            pool.indirect_dma_start(out=e.xg[:, r, :], out_offset=None, in_=e.xn[layer],
                                    in_offset=bass.IndirectOffsetOnAxis(ap=icol[:, r:r + 1], axis=0)).then_inc(gathered[r], 16)

        for j in range(ring):
            body(j, j, 0, j == 0, False)
        turns = (nt - ring) // ring
        with pool.Fori(1, 1 + turns) as t:
            for u in range(ring):
                body(t * ring + u, u, t, False, False)
        for j in range(ring * (1 + turns), nt):
            body(j, j % ring, j // ring, False, False)


def experts0(e):
    nc, ps, sem = e.nc, e.ps, e.sem
    gathered = [sem(f"e0_gathered{r}") for r in range(RING0)]
    x_turned, xT_ready = sem("e0_x_turned"), sem("e0_xT_ready")
    h_raw, h_copied, h_turned, hT_ready = sem("e0_h_raw"), sem("e0_h_copied"), sem("e0_h_turned"), sem("e0_hT_ready")
    y_raw, y_ready = sem("e0_y_raw"), sem("e0_y_ready")
    y_stored = [sem(f"e0_y_stored{r}") for r in range(RING0)]
    xT = e.carve(0, [DK, P], base=e.scr)
    h = e.carve(DK * P * 4, [H0], base=e.scr)
    hT = e.carve(DK * P * 4 + H0 * 4, [HK0, P], base=e.scr)
    HH = H0 // HB
    HALF = HK0 // HH
    XB, HB0, TB, YB = 0, 1, 3, 5

    with nc.Block() as block:
        gather_tiles(e, 0, block, gathered, x_turned)

        @block.tensor
        def _(pe):
            pe.wait_ge(e.w0_in, 16 * 2 * E0)

            def turn_x(j, r, turn):
                pe.wait_ge(gathered[r], turn * 16 + 16)
                for k in range(DK):
                    last = nc.tensor.transpose(ps[:, XB, k * P:(k + 1) * P], e.xg[:, r, k * P:(k + 1) * P], e.ident[:])
                last.then_inc(x_turned, 1)

            def down(j):
                ex = pe.value_load(e.expert[0:1, bass.ds(j, 1)], min_val=0, max_val=E0 - 1)
                if not (isinstance(j, int) and j == 0):
                    pe.wait_ge(y_ready, j)
                for k in range(HK0):
                    pe.wait_ge(hT_ready, j * HK0 + k + 1)
                    last = nc.tensor.matmul(ps[:, YB, 0:D], hT[:, k, :], e.w2[:, ex, k, :], start=(k == 0), stop=(k == HK0 - 1))
                last.then_inc(y_raw, 1)

            def body(j, r, turn, first, last):
                ex = pe.value_load(e.expert[0:1, bass.ds(j, 1)], min_val=0, max_val=E0 - 1)
                pe.wait_ge(xT_ready, j + 1)
                for n in range(HH):
                    for k in range(DK):
                        ins = nc.tensor.matmul(ps[:, HB0 + n, :], xT[:, k, :], e.w1[:, ex, k, n * HB:(n + 1) * HB], start=(k == 0), stop=(k == DK - 1))
                    ins.then_inc(h_raw, 1)
                if not last:
                    turn_x(j + 1, (r + 1) % RING0, turn + (r + 1) // RING0)
                if not first:
                    down(j - 1)
                for n in range(HH):
                    pe.wait_ge(h_copied, j * HH + n + 1)
                    for k in range(n * HALF, (n + 1) * HALF):
                        ins = nc.tensor.transpose(ps[:, TB + n, (k % HALF) * P:(k % HALF + 1) * P], h[:, k * P:(k + 1) * P], e.ident[:])
                    ins.then_inc(h_turned, 1)

            turn_x(0, 0, 0)
            tile_loop(pe, NT0, RING0, body)
            down(NT0 - 1)

        @block.scalar
        def _(act):
            def copy_x(j):
                act.wait_ge(x_turned, j + 1)
                nc.scalar.activation(xT.rearrange("p k t -> p (k t)"), ps[:, XB, 0:D], ACT.Copy).then_inc(xT_ready, 1)

            def body(j, r, turn, first, last):
                for n in range(HH):
                    act.wait_ge(h_raw, j * HH + n + 1)
                    nc.scalar.activation(h[:, n * HB:(n + 1) * HB], ps[:, HB0 + n, :], ACT.Copy).then_inc(h_copied, 1)
                if not last:
                    copy_x(j + 1)

            copy_x(0)
            tile_loop(act, NT0, RING0, body)

        @block.vector
        def _(dve):
            v = nc.vector

            def out(j, r, turn, fresh):
                ex = dve.value_load(e.expert[0:1, bass.ds(j, 1)], min_val=0, max_val=E0 - 1)
                if not fresh:
                    dve.wait_ge(y_stored[r], turn * 16)
                dve.wait_ge(y_raw, j + 1)
                v.tensor_tensor(e.ysb[:, r, :], ps[:, YB, 0:D], e.b2bc[:, ex, :], ALU.add).then_inc(y_ready, 1)

            def body(j, r, turn, first, last):
                if not first:
                    out(j - 1, (r - 1) % RING0, turn if r else turn - 1, isinstance(j, int) and j <= RING0)
                ex = dve.value_load(e.expert[0:1, bass.ds(j, 1)], min_val=0, max_val=E0 - 1)
                for k in range(HK0):
                    if k % HALF == 0:
                        dve.wait_ge(h_turned, j * HH + k // HALF + 1)
                    v.tensor_scalar(hT[:, k, :], ps[:, TB + k // HALF, (k % HALF) * P:(k % HALF + 1) * P],
                                    e.b1T[:, bass.ds(ex * HK0 + k, 1)], 0.0, ALU.add, ALU.max).then_inc(hT_ready, 1)

            tile_loop(dve, NT0, RING0, body)
            out(NT0 - 1, (NT0 - 1) % RING0, (NT0 - 1) // RING0, False)

        @block.sync
        def _(sp):
            def body(j, r, turn, first, last):
                sp.wait_ge(y_ready, j + 1)
                sp.dma_start(e.y[0][bass.ds(j * P, P), :], e.ysb[:, r, :]).then_inc(y_stored[r], 16)

            tile_loop(sp, NT0, RING0, body)
            for r in range(RING0):
                sp.wait_ge(y_stored[r], 16 * ((NT0 - 1 - r) // RING0 + 1))


def experts1(e):
    nc, ps, sem = e.nc, e.ps, e.sem
    gathered = [sem(f"e1_gathered{r}") for r in range(RING1)]
    x_turned, xT_ready = sem("e1_x_turned"), sem("e1_xT_ready")
    gu_raw, silu_ready, a_ready, a_turned, aT_ready = (sem("e1_" + n) for n in ("gu_raw", "silu_ready", "a_ready", "a_turned", "aT_ready"))
    y_raw, y_ready = sem("e1_y_raw"), sem("e1_y_ready")
    y_stored = [sem(f"e1_y_stored{r}") for r in range(RING1)]
    xT = e.carve(0, [DK, P], base=e.scr)
    silu = e.carve(DK * P * 4, [I1], base=e.scr)
    act_in = e.carve(DK * P * 4 + I1 * 4, [I1], base=e.scr)
    aT = e.carve(DK * P * 4 + 2 * I1 * 4, [2, P], base=e.scr)
    XB, GB, TB, YB = 0, 1, 2, 3

    with nc.Block() as block:
        gather_tiles(e, 1, block, gathered, x_turned)

        @block.tensor
        def _(pe):
            pe.wait_ge(e.w13_in, 32 * E1)
            pe.wait_ge(e.w2_in, 16 * E1)

            def turn_x(j, r, turn):
                pe.wait_ge(gathered[r], turn * 16 + 16)
                for k in range(DK):
                    last = nc.tensor.transpose(ps[:, XB, k * P:(k + 1) * P], e.xg[:, r, k * P:(k + 1) * P], e.ident[:])
                last.then_inc(x_turned, 1)

            def down(j):
                ex = pe.value_load(e.expert[0:1, bass.ds(j, 1)], min_val=0, max_val=E1 - 1)
                if not (isinstance(j, int) and j == 0):
                    pe.wait_ge(y_ready, j)
                pe.wait_ge(aT_ready, j + 1)
                for k in range(2):
                    last = nc.tensor.matmul(ps[:, YB, 0:D], aT[0:IH, k, :], e.w2b[0:IH, ex, k, :], start=(k == 0), stop=(k == 1))
                last.then_inc(y_raw, 1)

            def body(j, r, turn, first, last):
                ex = pe.value_load(e.expert[0:1, bass.ds(j, 1)], min_val=0, max_val=E1 - 1)
                pe.wait_ge(xT_ready, j + 1)
                for k in range(DK):
                    ins = nc.tensor.matmul(ps[:, GB, 0:2 * I1], xT[:, k, :], e.w13[:, ex, k, :], start=(k == 0), stop=(k == DK - 1))
                ins.then_inc(gu_raw, 1)
                if not last:
                    turn_x(j + 1, (r + 1) % RING1, turn + (r + 1) // RING1)
                if not first:
                    down(j - 1)
                pe.wait_ge(a_ready, j + 1)
                for k in range(2):
                    ins = nc.tensor.transpose(ps[0:IH, TB, k * P:(k + 1) * P], act_in[:, k * IH:(k + 1) * IH], e.ident[:])
                ins.then_inc(a_turned, 1)

            turn_x(0, 0, 0)
            tile_loop(pe, NT1, RING1, body)
            down(NT1 - 1)

        @block.scalar
        def _(act):
            def copy_x(j):
                act.wait_ge(x_turned, j + 1)
                nc.scalar.activation(xT.rearrange("p k t -> p (k t)"), ps[:, XB, 0:D], ACT.Copy).then_inc(xT_ready, 1)

            def body(j, r, turn, first, last):
                act.wait_ge(gu_raw, j + 1)
                if not first:
                    act.wait_ge(a_ready, j)
                nc.scalar.activation(silu, ps[:, GB, 0:I1], ACT.Silu).then_inc(silu_ready, 1)
                if not last:
                    copy_x(j + 1)
                act.wait_ge(a_turned, j + 1)
                nc.scalar.activation(aT[0:IH].rearrange("p k t -> p (k t)"), ps[0:IH, TB, 0:2 * P], ACT.Copy).then_inc(aT_ready, 1)

            copy_x(0)
            tile_loop(act, NT1, RING1, body)

        @block.vector
        def _(dve):
            v = nc.vector

            def out(j, r, turn, fresh):
                if not fresh:
                    dve.wait_ge(y_stored[r], turn * 16)
                dve.wait_ge(y_raw, j + 1)
                v.tensor_copy(e.ysb[:, r, :], ps[:, YB, 0:D]).then_inc(y_ready, 1)

            def body(j, r, turn, first, last):
                dve.wait_ge(silu_ready, j + 1)
                v.tensor_tensor(act_in, ps[:, GB, I1:2 * I1], silu, ALU.mult).then_inc(a_ready, 1)
                if not first:
                    out(j - 1, (r - 1) % RING1, turn if r else turn - 1, isinstance(j, int) and j <= RING1)

            tile_loop(dve, NT1, RING1, body)
            out(NT1 - 1, (NT1 - 1) % RING1, (NT1 - 1) // RING1, False)

        @block.sync
        def _(sp):
            def body(j, r, turn, first, last):
                sp.wait_ge(y_ready, j + 1)
                sp.dma_start(e.y[1][bass.ds(j * P, P), :], e.ysb[:, r, :]).then_inc(y_stored[r], 16)

            tile_loop(sp, NT1, RING1, body)
            for r in range(RING1):
                sp.wait_ge(y_stored[r], 16 * ((NT1 - 1 - r) // RING1 + 1))


def combine(e, layer):
    nc, sem = e.nc, e.sem
    kk = (K0, K1)[layer]
    nm = f"co{layer}_"
    U = 4
    got = [sem(nm + f"got{u}") for u in range(U)]
    icol_ready, carrier, added, step = sem(nm + "icol_ready"), sem(nm + "carrier"), sem(nm + "added"), sem(nm + "step")
    stored = sem(nm + "stored")
    yg = e.carve(0, [U, kk, D], base=e.scr)
    TURNS = NTILE // U
    last_layer = layer == 1

    with nc.Block() as block:
        @block.gpsimd
        def _(pool):
            def body(t, u, wait):
                i = t * U + u
                if wait:
                    pool.wait_ge(added, i - (U - 1))
                nc.gpsimd.tensor_copy(e.icol[:, u, 0:kk], e.slot_u[:, i, 0:kk]).then_inc(icol_ready, 1)
                pool.wait_ge(icol_ready, i + 1)
                pool.sem_inc(carrier, 1)
                for k in range(kk):
                    pool.indirect_dma_start(out=yg[:, u, k, :], out_offset=None, in_=e.y[layer],
                                            in_offset=bass.IndirectOffsetOnAxis(ap=e.icol[:, u, k:k + 1], axis=0)).then_inc(got[u], 16)

            for u in range(U):
                body(0, u, False)
            with pool.Fori(1, TURNS) as t:
                for u in range(U):
                    body(t, u, True)

        @block.vector
        def _(dve):
            v = nc.vector
            ch = Chain(dve, step)
            with dve.Fori(0, TURNS) as t:
                with ch.turns(t, U * kk, TURNS):
                    for u in range(U):
                        i = t * U + u
                        dve.wait_ge(got[u], t * (16 * kk) + 16 * kk)
                        ch(v.tensor_scalar(yg[:, u, 0, :], yg[:, u, 0, :], e.gate[:, i, 0:1], None, ALU.mult))
                        for k in range(1, kk):
                            ch(v.scalar_tensor_tensor(yg[:, u, 0, :], yg[:, u, k, :], e.gate[:, i, k:k + 1], yg[:, u, 0, :], ALU.mult, ALU.add))
                        v.scalar_tensor_tensor(e.x[:, i, :], yg[:, u, 0, :], e.tg[:, 2 + layer:3 + layer], e.x[:, i, :], ALU.mult, ALU.add).then_inc(added, 1)
                        if not last_layer:
                            dve.wait_ge(added, i + 1)
                            v.bn_stats(e.stats[:, i, :], e.x[:, i, :])

        @block.sync
        def _(sp):
            if last_layer:
                o = e.out.rearrange("b (t p) d -> p (b t) d", p=P)
                with sp.Fori(0, NTILE) as i:
                    sp.wait_ge(added, i + 1)
                    sp.dma_start(o[:, i, :], e.x[:, i, :]).then_inc(stored, 16)
                sp.wait_ge(stored, 16 * NTILE)


def attention_buffers(e):
    o = [ATT0]

    def buf(shape, dt=F32):
        got = e.carve(o[0], shape, dt)
        o[0] += int(np.prod(shape)) * (2 if dt == BF16 else 4)
        assert o[0] <= TOP, o[0]
        return got

    e.v_all = buf([B, MT, D])
    mark = o[0]
    e.xn_a = buf([4, D]); e.xT_a = buf([DK, HB]); e.parts = buf([4, 3, HB], BF16); e.left = buf([4, HB])
    o[0] = mark
    e.q_aug = [buf([2, GH, HB], BF16) for _ in range(2)]
    e.k_aug = [buf([GH, KEYS + 1], BF16) for _ in range(2)]
    e.v_g = [buf([MT, GH, HD + 1]) for _ in range(2)]
    e.prob = [buf([GH, HB]) for _ in range(2)]
    e.oT = buf([HB])
    e.mx = buf([2 * GH, TPB // 2, 3]).rearrange("p (c h) t k -> p c h t k", c=2); e.row_max = buf([GH, TPB // 2]); e.neg_all = buf([P], BF16); e.rest = buf([GH, TPB // 2]); e.negT = buf([P], BF16)
    e.neg = e.neg_all[:, 0:3 * GH * TPB // 2].rearrange("p (n h t) -> p n h t", n=3, h=GH)
    e.rec = buf([TPB // 2, GH])
    e.sums = buf([TPB // 2, GH, HD + 1])
    e.att = e.carve(0, [NTILE, D], base=e.scr)


def project_qkv(e):
    nc, ps, sem, a = e.nc, e.ps, e.sem, e.a
    step, var_ready, std_ready = sem("qkv_step"), sem("qkv_var"), sem("qkv_std")
    xn_ready, xT_raw, xT_ready, v_raw, v_done = (sem("qkv_" + n) for n in ("xn_ready", "xT_raw", "xT_ready", "v_raw", "v_done"))
    unit_raw, part0, left1, part1, unit_done = (sem("qkv_" + n) for n in ("unit_raw", "part0", "left1", "part1", "unit_done"))
    c_raw, stored = sem("qkv_c_raw"), [sem(f"qkv_stored{n}") for n in range(4)]
    U = 4
    CH = NTOK // HB
    qp = e.qp.rearrange("c (k p) t -> k p c t", p=P)
    kp = e.kp.rearrange("c (k p) b t -> k p b c t", p=P)
    SCALE = (float(HD) ** -0.5, 1.0)
    UB = 4

    with nc.Block() as block:
        def chunks(eng, body):
            with eng.Fori(0, B) as b, eng.Fori(0, CH // B) as h:
                body(b, h, b * (CH // B) + h)

        @block.sync
        def _(sp):
            for ex in range(EARLY):
                load_w13(e, sp, ex)
            for n in range(4):
                sp.wait_ge(unit_done, n + 1)
                sp.dma_start(kp[n % DK, :, n // DK, :, 0:CL], e.parts[:, n, :, 0:CL]).then_inc(stored[n], 16)

            def body(b, h, c):
                for n in range(4):
                    sp.wait_ge(unit_done, c * 4 + (5 + n))
                    if n < 2:
                        dst = qp[n, :, :, bass.ds(c * HB, HB)]
                    else:
                        dst = kp[n - 2, :, b, :, bass.ds(h * HB + CL, HB)]
                    sp.dma_start(dst, e.parts[:, n, :, :]).then_inc(stored[n], 16)

            chunks(sp, body)
            for n in range(4):
                sp.wait_ge(stored[n], 16 * (CH + 1))

        @block.tensor
        def _(pe):
            for n in range(4):
                nc.tensor.transpose(ps[:, UB + n, 0:CL], e.ctx[:, n // DK, (n % DK) * P:(n % DK + 1) * P], e.ident[0:CL, 0:CL]).then_inc(unit_raw, 1)

            def body(b, h, c):
                for u in range(U):
                    pe.wait_ge(xn_ready, c * U + u + 1)
                    for k in range(DK):
                        last = nc.tensor.transpose(ps[:, u % 2, k * P:(k + 1) * P], e.xn_a[:, u, k * P:(k + 1) * P], e.ident[:])
                    last.then_inc(xT_raw, 1)
                    pe.wait_ge(xT_ready, c * U + u + 1)
                    pe.wait_ge(v_done, c * U + u + 1)
                    for k in range(DK):
                        last = nc.tensor.matmul(ps[:, 2 + u % 2, 0:D], e.xT_a[:, k, u * P:(u + 1) * P], e.wqkvT[:, k, 2 * D:3 * D], start=(k == 0), stop=(k == DK - 1))
                    last.then_inc(v_raw, 1)
                for n in range(4):
                    pe.wait_ge(left1, c * 4 + (n + 1))
                    for k in range(DK):
                        last = nc.tensor.matmul(ps[:, UB + n, :], e.wqkvT[:, k, n * P:(n + 1) * P], e.xT_a[:, k, :], start=(k == 0), stop=(k == DK - 1))
                    last.then_inc(unit_raw, 1)

            chunks(pe, body)

        @block.scalar
        def _(act):
            act.wait_ge(var_ready, 1)
            nc.scalar.activation(e.std[:], e.ve[:], ACT.Sqrt).then_inc(std_ready, 1)

            def first_part(n, w, scale):
                nc.scalar.activation(e.parts[:, n, 0, 0:w], ps[:, UB + n, 0:w], ACT.Copy, scale=scale).then_inc(part0, 1)

            def second_part(n, w):
                nc.scalar.activation(e.parts[:, n, 1, 0:w], e.left[:, n, 0:w], ACT.Copy).then_inc(part1, 1)

            for n in range(4):
                act.wait_ge(unit_raw, n + 1)
                first_part(n, CL, 1.0)
            for n in range(4):
                act.wait_ge(left1, n + 1)
                second_part(n, CL)

            def body(b, h, c):
                for u in range(U):
                    act.wait_ge(xT_raw, c * U + u + 1)
                    nc.scalar.activation(e.xT_a[:, :, u * P:(u + 1) * P], ps[:, u % 2, 0:D].rearrange("p (k t) -> p k t", k=DK), ACT.Copy).then_inc(xT_ready, 1)
                for n in range(4):
                    act.wait_ge(unit_raw, c * 4 + (5 + n))
                    act.wait_ge(stored[n], c * 16 + 16)
                    first_part(n, HB, SCALE[n // 2])
                for n in range(4):
                    act.wait_ge(left1, c * 4 + (5 + n))
                    second_part(n, HB)

            chunks(act, body)

        @block.vector
        def _(dve):
            v = nc.vector
            ch = Chain(dve, step)
            moments(ch, nc, e.stats, D, e.mean[:], e.var[:], e.ve[:], [e.tmp[:, n, :] for n in range(4)], LN_EPS)
            v.engine_nop().then_inc(var_ready, 1)
            dve.wait_ge(std_ready, 1)
            ch(v.reciprocal(e.rstd[:], e.std[:]))
            for b in range(B):
                v.tensor_copy(e.v_all[0:CL, b, 0, :], e.ctx[:, b, D:2 * D])
            dve.sem_inc(v_done, 2)

            def split(n, at, w, scale):
                dve.wait_ge(part0, at)
                v.scalar_tensor_tensor(e.left[:, n, 0:w], ps[:, UB + n, 0:w], scale, e.parts[:, n, 0, 0:w], ALU.mult, ALU.subtract).then_inc(left1, 1)

            def third(n, at, w):
                dve.wait_ge(part1, at)
                v.tensor_tensor(e.parts[:, n, 2, 0:w], e.left[:, n, 0:w], e.parts[:, n, 1, 0:w], ALU.subtract).then_inc(unit_done, 1)

            for n in range(4):
                split(n, n + 1, CL, 1.0)
            for n in range(4):
                third(n, n + 1, CL)

            def body(b, h, c):
                for u in range(U):
                    i = c * U + u
                    v.tensor_scalar(e.xn_a[:, u, :], e.x[:, i, :], e.mean[:, bass.ds(i, 1)], e.rstd[:, bass.ds(i, 1)], ALU.subtract, ALU.mult).then_inc(xn_ready, 1)
                for u in range(U):
                    dve.wait_ge(v_raw, c * U + u + 1)
                    v.tensor_copy(e.v_all[:, b, h * U + (1 + u), :], ps[:, 2 + u % 2, 0:D]).then_inc(v_done, 1)
                for n in range(4):
                    split(n, c * 4 + (5 + n), HB, SCALE[n // 2])
                for n in range(4):
                    third(n, c * 4 + (5 + n), HB)

            chunks(dve, body)


def load_w13(e, eng, ex):
    eng.dma_start(e.w13[:, ex, :, 0:I1], e.a["L1_ffn_w1"][ex].rearrange("(k p) i -> p k i", p=P)).then_inc(e.w13_in, 16)
    eng.dma_start(e.w13[:, ex, :, I1:2 * I1], e.a["L1_ffn_w3"][ex].rearrange("(k p) i -> p k i", p=P)).then_inc(e.w13_in, 16)


STEPS = 2 * MT
HT = TPB // 2
MAXES = 2 * GH * HT
LATE, NEXT, AHEAD = 0, 1, 2
HALF_AT, PREV_AT = MT + 1, 1
INVERT = 3
SPREAD = (2, 3, 4, 4, 3, 4, 3, 4, 4, 3, 3, 4, 4, 3, 4, 4, 4, 4)
SPLIT_AT = {LATE: 5, NEXT: 14}
BEFORE = 3 * GH
SPREAD_FIRST = (3, 3, 3, 3, 4, 4) + (4,) * 12
SPLIT_AT_FIRST = {LATE: 6, NEXT: 14}


def attend(e):
    nc, ps, sem = e.nc, e.ps, e.sem
    loaded = [sem(f"at_loaded{u}") for u in range(2)]
    q2_loaded = [sem(f"at_q2_loaded{u}") for u in range(2)]
    max_in = [sem(f"at_max_in{c}") for c in range(2)]
    v_ready, ones_set, psum_set = sem("at_v_ready"), sem("at_ones_set"), sem("at_psum_set")
    max_raw, max_done, misc_raw, misc_done = (sem("at_" + n) for n in ("max_raw", "max_done", "misc_raw", "misc_done"))
    rows_max, neg_ready, negT_ready = sem("at_rows_max"), sem("at_neg_ready"), sem("at_negT_ready")
    step, carrier = sem("at_step"), sem("at_carrier")
    s_raw, p_ready, pv_done = sem("at_s_raw"), sem("at_p_ready"), sem("at_pv_done")
    half_out, half_inverted, half_done = (sem("at_half_" + n) for n in ("out", "inverted", "done"))
    MAXB, NMAXB, SB, NSB, AB, MB = 0, 3, 3, 3, 6, 7
    PARTS = len(QB)
    TURN_FIRST = MAXES + BEFORE // 2 - 1
    PROLOGUE, PER_GROUP = HT + BEFORE // (2 * GH) + 1, TPB + 4

    def misc_before(g):
        if isinstance(g, int) and g == 0:
            return PROLOGUE
        return g * PER_GROUP + (HT + HT // 2)

    def maxima_before(g):
        if isinstance(g, int) and g == 0:
            return MAXES + BEFORE
        return g * (2 * MAXES) + (MAXES + MAXES // 2)

    def groups(eng, body):
        body(0, 0, True, False)
        with eng.Fori(0, (NGRP - 2) // 2) as t:
            for u in range(2):
                body(t * 2 + (1 + u), (1 + u) % 2, False, False)
        body(NGRP - 1, (NGRP - 1) % 2, False, True)

    def batch_of(g):
        return g // (NGRP // B), g % (NGRP // B)

    def key_rows(mt):
        return (0, CL) if mt == 0 else (CL + (mt - 1) * P, P)

    def half(which, g, u):
        return (g, u, 1) if which == LATE else (g + 1, 1 - u, which - NEXT)

    def maxima_at(s, first, last):
        spread = SPREAD_FIRST if first else SPREAD
        late = MAXES - BEFORE if first else MAXES // 2
        for pos in range(sum(spread[:s]), sum(spread[:s + 1])):
            which = LATE if pos < late else NEXT if pos < late + MAXES else AHEAD
            if not (last and which != LATE):
                yield pos, which, pos + MAXES - late if which == LATE else pos - late - (which - NEXT) * MAXES

    def split_at(s, first, last):
        return [which for which, at in (SPLIT_AT_FIRST if first else SPLIT_AT).items() if at == s and not (last and which != LATE)]

    def odds_at(s, first, last):
        for which in split_at(s - 1, first, last):
            yield "turn", which, 0
        for pos, which, n in maxima_at(s, first, last):
            if n % (2 * GH) == 2 * GH - 1:
                yield "ctx", which, n // (2 * GH)
        if s == PREV_AT and not first:
            yield "half", 1, 0
        if s == HALF_AT:
            yield "half", 0, 0

    class Odds:

        def __init__(self):
            self.base, self.n = 0, 0

        def at(self, base):
            self.base, self.n = base, 0

        def next(self):
            self.n += 1
            return self.base + (self.n - 1)

    with nc.Block() as block:
        @block.sync
        def _(sp):
            qv = e.qp.rearrange("c (g h r) t -> c g r h t", h=GH, r=HD)
            kv = e.kp.rearrange("c (g h r) b t -> c g r h b t", h=GH, r=HD)

            def load(g, u):
                b, gg = batch_of(g)
                for n, (cq, ck) in enumerate(zip(QB, KB)):
                    rows = slice(n * HD, (n + 1) * HD)
                    sp.dma_start(e.q_aug[u][rows, 0, :, :], qv[cq, gg, :, :, bass.ds(b * S, HB)]).then_inc(loaded[u], 16)
                    sp.dma_start(e.k_aug[u][rows, :, 0:KEYS], kv[ck, gg, :, :, b, :]).then_inc(loaded[u], 16)
                for n, cq in enumerate(QB):
                    sp.dma_start(e.q_aug[u][n * HD:(n + 1) * HD, 1, :, :], qv[cq, gg, :, :, bass.ds(b * S + HB, HB)]).then_inc(q2_loaded[u], 16)

            def maxima(g, u, c):
                sp.wait_ge(negT_ready, g * 2 + (1 + c))
                for n in range(3):
                    sp.dma_start(e.q_aug[u][QROWS + n:QROWS + n + 1, c].rearrange("o h (t n) -> o (h t) n", n=P),
                                 e.negT[n * GH * HT:(n + 1) * GH * HT, :]).then_inc(max_in[c], 16)

            load(0, 0)
            maxima(0, 0, 0)

            def body(g, u, first, last):
                if not last:
                    if not first:
                        sp.wait_ge(s_raw, g * (GH * STEPS))
                    load(g + 1, 1 - u)
                maxima(g, u, 1)
                if not last:
                    maxima(g + 1, 1 - u, 0)

            groups(sp, body)

        @block.gpsimd
        def _(pool):
            g_ = nc.gpsimd
            ch = Chain(pool, step, carrier)
            for u in range(2):
                g_.memset(e.k_aug[u][QROWS:AROWS, :, :], 1.0).then_inc(ones_set, 1)
                pool.wait_ge(ones_set, 2 * u + 1)
                g_.memset(e.v_g[u][:, :, :, HD:HD + 1], 1.0).then_inc(ones_set, 1)
                pool.wait_ge(ones_set, 2 * u + 2)
            ch(g_.memset(e.neg_all, 0.0))

            def values(g, u):
                b, gg = batch_of(g)
                cols = e.v_all[:, b, :, bass.ds(gg * (GH * HD), GH * HD)]
                g_.tensor_copy(e.v_g[u][0:CL, 0, :, 0:HD], cols[0:CL, 0, :].rearrange("p (h r) -> p h r", h=GH)).then_inc(v_ready, 1)
                for mt in range(1, MT):
                    pool.wait_ge(v_ready, g * MT + mt)
                    pool.sem_inc(carrier, 1)
                    g_.tensor_copy(e.v_g[u][:, mt, :, 0:HD], cols[:, mt, :].rearrange("p (h r) -> p h r", h=GH)).then_inc(v_ready, 1)

            def negate(g, c):
                pool.wait_ge(rows_max, g * 2 + (1 + c))
                pool.sem_inc(carrier, 1)
                ch(g_.tensor_scalar(e.rest, e.row_max, -1.0, None, ALU.mult))
                ch(g_.tensor_scalar(e.neg[:, 0], e.rest, 1.0, None, ALU.mult))
                ch(g_.tensor_tensor(e.rest, e.rest, e.neg[:, 0], ALU.subtract))
                ch(g_.tensor_scalar(e.neg[:, 1], e.rest, 1.0, None, ALU.mult))
                g_.tensor_tensor(e.neg[:, 2], e.rest, e.neg[:, 1], ALU.subtract).then_inc(neg_ready, 1)

            def normalise(b, gg, c, count):
                pool.wait_ge(half_inverted, count)
                pool.sem_inc(carrier, 1)
                for t in range(HT):
                    ins = g_.tensor_tensor(e.att[:, b * TPB + (c * HT + t), bass.ds(gg * (GH * HD), GH * HD)].rearrange("p (h r) -> p h r", h=GH),
                                           e.sums[:, t, :, 0:HD], e.rec[:, t, :].unsqueeze(2).broadcast_to([P, GH, HD]), ALU.mult)
                    if t < HT - 1:
                        ch(ins)
                ins.then_inc(half_done, 1)

            values(0, 0)
            negate(0, 0)

            def body(g, u, first, last):
                if not last:
                    if not first:
                        pool.wait_ge(pv_done, g * STEPS)
                        pool.sem_inc(carrier, 1)
                    values(g + 1, 1 - u)
                if not first:
                    normalise(*batch_of(g - 1), 1, g * 2)
                negate(g, 1)
                normalise(*batch_of(g), 0, g * 2 + 1)
                if not last:
                    negate(g + 1, 0)

            body(0, 0, True, False)
            with pool.Fori(0, (NGRP - 2) // 2) as t:
                with ch.turns(t, 2 * (2 * 4 + 2 * (HT - 1)), (NGRP - 2) // 2):
                    for u in range(2):
                        body(t * 2 + (1 + u), (1 + u) % 2, False, False)
            body(NGRP - 1, (NGRP - 1) % 2, False, True)
            normalise(*batch_of(NGRP - 1), 1, NGRP * 2)

        @block.tensor
        def _(pe):
            odds = Odds()

            def odd():
                n = odds.next()
                if not (isinstance(n, int) and n == 0):
                    pe.wait_ge(misc_done, n)

            def maximum(g, u, c, n, pos, before):
                th, k = divmod(n, 2)
                t, h = divmod(th, GH)
                if pos >= NMAXB:
                    pe.wait_ge(max_done, before + (pos - NMAXB + 1))
                elif pos == 0 and not (isinstance(before, int) and before == 0):
                    pe.wait_ge(max_done, before)
                nc.tensor.matmul(ps[:, MAXB + pos % NMAXB, :], e.q_aug[u][0:QROWS, c, h, t * P:(t + 1) * P],
                                 e.k_aug[u][0:QROWS, h, CL + k * HB:CL + (k + 1) * HB], start=True, stop=True).then_inc(max_raw, 1)

            def context_max(u, c, t):
                odd()
                for h in range(GH):
                    ins = nc.tensor.matmul(ps[:, MB, h * CL:(h + 1) * CL], e.q_aug[u][0:QROWS, c, h, t * P:(t + 1) * P],
                                           e.k_aug[u][0:QROWS, h, 0:CL], start=True, stop=True)
                ins.then_inc(misc_raw, 1)

            def turn_maxima(g, c):
                pe.wait_ge(neg_ready, g * 2 + (1 + c))
                odd()
                nc.tensor.transpose(ps[:, MB, 0:P // 2].bitcast(BF16), e.neg_all, e.identb[:]).then_inc(misc_raw, 1)

            def turn_half(count):
                pe.wait_ge(half_out, count)
                odd()
                for t in range(HT):
                    ins = nc.tensor.transpose(ps[:, MB, t * P:(t + 1) * P], e.oT[:, t * P:(t + 1) * P], e.ident[:])
                ins.then_inc(misc_raw, 1)

            def weigh(g, u, s):
                mt = s % MT
                k0, rows = key_rows(mt)
                pe.wait_ge(p_ready, g * (GH * STEPS) + GH * (s + 1))
                if mt == 0 and not (isinstance(g, int) and g == 0 and s == 0):
                    pe.wait_ge(half_out, g * 2 + s // MT)
                for h in range(GH):
                    ins = nc.tensor.matmul(ps[h * 32:h * 32 + HD + 1, AB, :], e.v_g[u][0:rows, mt, h, :], e.prob[s % 2][0:rows, h, :],
                                           start=(mt == 0), stop=(mt == MT - 1))
                ins.then_inc(pv_done, 1)

            def score(g, u, s, h):
                c, mt = divmod(s, MT)
                k0, rows = key_rows(mt)
                n = s * GH + h
                if not (isinstance(g, int) and g == 0 and n < NSB):
                    pe.wait_ge(p_ready, g * (GH * STEPS) + (n - NSB + 1))
                nc.tensor.matmul(ps[0:rows, SB + n % NSB, :], e.k_aug[u][0:AROWS, h, k0:k0 + rows],
                                 e.q_aug[u][0:AROWS, c, h, :], start=True, stop=True).then_inc(s_raw, 1)

            pe.wait_ge(ones_set, 4)
            pe.wait_ge(psum_set, 1)
            odds.at(0)
            pe.wait_ge(loaded[0], 16 * PARTS * 2)
            for pos in range(MAXES + BEFORE):
                c, n = divmod(pos, MAXES)
                if pos == MAXES:
                    pe.wait_ge(q2_loaded[0], 16 * PARTS)
                maximum(0, 0, c, n, pos, 0)
                if n % (2 * GH) == 2 * GH - 1:
                    context_max(0, c, n // (2 * GH))
                if pos == TURN_FIRST:
                    turn_maxima(0, 0)

            def body(g, u, first, last):
                odds.at(misc_before(g))
                before = maxima_before(g)
                pe.wait_ge(v_ready, g * MT + MT)
                for s in range(STEPS):
                    if s % MT == 0:
                        pe.wait_ge(max_in[s // MT], g * (16 * 3) + 16 * 3)
                    todo = list(maxima_at(s, first, last))
                    skip = 2 if s == 0 and not first else 0

                    def maxima(slot):
                        at = slot - skip
                        for pos, which, n in todo[at:] if slot == GH - 1 else todo[at:at + 1] if at >= 0 else ():
                            hg, hu, c = half(which, g, u)
                            if which == NEXT and n == 0:
                                pe.wait_ge(loaded[hu], next_of(g, u) * (16 * PARTS * 2) + 16 * PARTS * 2)
                            if which == AHEAD and n == 0:
                                pe.wait_ge(q2_loaded[hu], next_of(g, u) * (16 * PARTS) + 16 * PARTS)
                            maximum(hg, hu, c, n, pos, before)

                    score(g, u, s, 0)
                    for what, which, n in odds_at(s, first, last):
                        if what == "turn":
                            hg, hu, c = half(which, g, u)
                            turn_maxima(hg, c)
                    maxima(0)
                    score(g, u, s, 1)
                    maxima(1)
                    if s > 0:
                        weigh(g, u, s - 1)
                    elif not first:
                        weigh(g - 1, 1 - u, STEPS - 1)
                    score(g, u, s, 2)
                    maxima(2)
                    score(g, u, s, 3)
                    maxima(3)
                    for what, which, n in odds_at(s, first, last):
                        if what == "ctx":
                            hg, hu, c = half(which, g, u)
                            context_max(hu, c, n)
                        if what == "half":
                            turn_half(g * 2 + 1 - which)

            groups(pe, body)
            weigh(NGRP - 1, (NGRP - 1) % 2, STEPS - 1)
            turn_half(NGRP * 2)

        @block.scalar
        def _(act):
            odds = Odds()

            def out(count):
                act.wait_ge(pv_done, count * MT)
                nc.scalar.activation(e.oT, ps[:, AB, :], ACT.Copy).then_inc(half_out, 1)

            def turned(count):
                act.wait_ge(misc_raw, odds.next() + 1)
                if not (isinstance(count, int) and count == 1):
                    act.wait_ge(half_done, count - 1)
                o = ps[:, MB, :].rearrange("p (t h c) -> p t h c", t=HT, h=GH)
                nc.scalar.activation(e.sums, o[:, :, :, 0:HD + 1], ACT.Copy).then_inc(misc_done, 1)

            def body(g, u, first, last):
                odds.at(misc_before(g))
                for s in range(STEPS):
                    rows = key_rows(s % MT)[1]
                    for h in range(GH):
                        act.wait_ge(s_raw, g * (GH * STEPS) + (s * GH + h + 1))
                        if h == 0 and not (isinstance(g, int) and g == 0 and s < 2):
                            act.wait_ge(pv_done, g * STEPS + (s - 1))
                        nc.scalar.activation(e.prob[s % 2][0:rows, h, :], ps[0:rows, SB + (s * GH + h) % NSB, :], ACT.Exp).then_inc(p_ready, 1)
                        if h == 1 and s == 0 and not first:
                            out(g * 2)
                        if h == 1 and s == MT:
                            out(g * 2 + 1)
                        if h == 1:
                            for what, which, n in odds_at(s - 1, first, last):
                                if what == "half":
                                    turned(g * 2 + 1 - which)
                                else:
                                    odds.next()

            groups(act, body)
            out(NGRP * 2)
            for what, which, n in odds_at(STEPS - 1, False, True):
                odds.next()
            turned(NGRP * 2)

        @block.vector
        def _(dve):
            v = nc.vector
            odds = Odds()
            v.memset(ps[:, AB, :], 0.0).then_inc(psum_set, 1)

            def maximum(c, n, pos, before):
                th, k = divmod(n, 2)
                t, h = divmod(th, GH)
                dve.wait_ge(max_raw, before + (pos + 1))
                v.tensor_reduce(e.mx[:, c, h, t, k:k + 1], ps[:, MAXB + pos % NMAXB, :], AX.X, ALU.max).then_inc(max_done, 1)

            def context_max(c, t):
                dve.wait_ge(misc_raw, odds.next() + 1)
                v.tensor_reduce(e.mx[:, c, :, t, 2], ps[:, MB, 0:GH * CL].rearrange("p (h c) -> p h c", h=GH), AX.X, ALU.max).then_inc(misc_done, 1)

            def row_max(g, c):
                dve.wait_ge(max_done, g * (2 * MAXES) + (c + 1) * MAXES)
                dve.wait_ge(misc_done, odds.base + odds.n)
                if not (isinstance(g, int) and g == 0 and c == 0):
                    dve.wait_ge(neg_ready, g * 2 + c)
                v.tensor_reduce(e.row_max, e.mx[:, c], AX.X, ALU.max).then_inc(rows_max, 1)

            def invert(count, use):
                dve.wait_ge(misc_done, use + 1)
                if not (isinstance(count, int) and count == 1):
                    dve.wait_ge(half_done, count - 1)
                v.reciprocal(e.rec, e.sums[:, :, :, HD]).then_inc(half_inverted, 1)

            def turned(g, c):
                dve.wait_ge(misc_raw, odds.next() + 1)
                if not (isinstance(g, int) and g == 0 and c == 0):
                    dve.wait_ge(max_in[1 - c], g * (16 * 3) + c * (16 * 3))
                v.tensor_copy(e.negT[0:3 * GH * HT, :], ps[0:3 * GH * HT, MB, 0:P // 2].bitcast(BF16)).then_inc(negT_ready, 1)
                v.engine_nop().then_inc(misc_done, 1)

            def body(g, u, first, last):
                odds.at(misc_before(g))
                before = maxima_before(g)
                for s in range(STEPS):
                    order = list(odds_at(s, first, last))
                    todo = list(maxima_at(s, first, last))
                    for which in split_at(s, first, last):
                        hg, _, c = half(which, g, u)
                        row_max(hg, c)
                    for what, which, n in odds_at(s - INVERT, first, last):
                        if what == "half":
                            invert(g * 2 + 1 - which, half_use)
                    for i, (pos, which, n) in enumerate(todo):
                        if i == 1 or len(todo) == 1:
                            for what, which_, n_ in order:
                                if what == "turn":
                                    hg, _, c = half(which_, g, u)
                                    turned(hg, c)
                        maximum(half(which, g, u)[2], n, pos, before)
                    for what, which, n in order:
                        if what == "turn" and not todo:
                            hg, _, c = half(which, g, u)
                            turned(hg, c)
                        if what == "ctx":
                            context_max(half(which, g, u)[2], n)
                        if what == "half":
                            half_use = odds.next()

            odds.at(0)
            for pos in range(MAXES + BEFORE):
                c, n = divmod(pos, MAXES)
                maximum(c, n, pos, 0)
                if n % (2 * GH) == 2 * GH - 1:
                    context_max(c, n // (2 * GH))
                if pos == MAXES - 1:
                    row_max(0, 0)
                if pos == TURN_FIRST:
                    turned(0, 0)
            groups(dve, body)
            invert(NGRP * 2, odds.next())


def next_of(g, u):
    return (g + 1 - (1 - u)) // 2


def project_out(e):
    nc, ps, sem, a = e.nc, e.ps, e.sem, e.a
    in_ready, aT_raw, aT_ready, o_raw, biased, x_new = (sem("pj_" + n) for n in ("in_ready", "aT_raw", "aT_ready", "o_raw", "biased", "x_new"))
    U = 4
    at = ATT0 + (E1 - EARLY) * W13_BYTES
    rows = e.carve(at, [U, D])
    aT = e.carve(at + U * D * 4, [U, DK, P])
    sums = e.carve(at + 2 * U * D * 4, [U, D])
    TURNS = NTILE // U

    with nc.Block() as block:
        @block.sync
        def _(sp):
            for ex in range(EARLY, E1):
                load_w13(e, sp, ex)

        @block.gpsimd
        def _(pool):
            with pool.Fori(0, TURNS) as t:
                for u in range(U):
                    i = t * U + u
                    pool.wait_ge(x_new, i + 1)
                    pool.sem_inc(biased, 1)
                    nc.gpsimd.tensor_copy(rows[:, u, :], e.att[:, i, :]).then_inc(in_ready, 1)

        @block.tensor
        def _(pe):
            with pe.Fori(0, TURNS) as t:
                for u in range(U):
                    pe.wait_ge(in_ready, t * U + u + 1)
                    for k in range(DK):
                        last = nc.tensor.transpose(ps[:, u, k * P:(k + 1) * P], rows[:, u, k * P:(k + 1) * P], e.ident[:])
                    last.then_inc(aT_raw, 1)
                for u in range(U):
                    pe.wait_ge(aT_ready, t * U + u + 1)
                    for k in range(DK):
                        last = nc.tensor.matmul(ps[:, 4 + u, 0:D], aT[:, u, k, :], e.wprojT[:, k, :], start=(k == 0), stop=(k == DK - 1))
                    last.then_inc(o_raw, 1)

        @block.scalar
        def _(act):
            with act.Fori(0, TURNS) as t:
                for u in range(U):
                    act.wait_ge(aT_raw, t * U + u + 1)
                    nc.scalar.activation(aT[:, u, :, :].rearrange("p k t -> p (k t)"), ps[:, u, 0:D], ACT.Copy).then_inc(aT_ready, 1)

        @block.vector
        def _(dve):
            v = nc.vector
            step = sem("pj_step")
            ch = Chain(dve, step)
            dve.sem_inc(x_new, U)
            with dve.Fori(0, TURNS) as t:
                with ch.turns(t, U, TURNS):
                    for u in range(U):
                        i = t * U + u
                        dve.wait_ge(o_raw, i + 1)
                        ch(v.tensor_tensor(sums[:, u, :], ps[:, 4 + u, 0:D], e.bproj, ALU.add))
                        v.scalar_tensor_tensor(e.x[:, i, :], sums[:, u, :], e.tg[:, 1:2], e.x[:, i, :], ALU.mult, ALU.add).then_inc(x_new, 1)
                        dve.wait_ge(x_new, i + (U + 1))
                        v.bn_stats(e.stats[:, i, :], e.x[:, i, :])


def load_w2(e):
    nc, a = e.nc, e.a
    with nc.Block() as block:
        @block.sync
        def _(sp):
            for ex in range(E1):
                sp.dma_start(e.w2b[0:IH, ex, :, :], a["L1_ffn_w2"][ex].rearrange("(k p) d -> p k d", p=IH)).then_inc(e.w2_in, 16)


def flamingo_block(nc, out, **inputs):
    with ExitStack() as ctx:
        e = make_env(nc, ctx, inputs, out)
        attention_buffers(e)
        for stage, *args in ((prepare,), (depool_mixer,), (router, 0), (route, 0), (experts0,), (combine, 0)):
            stage(e, *args)
        nc.clear_and_free_semaphores(e.used)
        nc.all_engine_barrier()
        e.used = []
        for stage, *args in ((project_qkv,), (attend,), (project_out,), (router, 1), (route, 1), (load_w2,), (experts1,), (combine, 1)):
            stage(e, *args)


NAMES = ("x", "ctx_2048", "mask_BxS2_if0", "g_xattn", "g_ffn", "L0_xattn_W_in", "L0_xattn_b_in", "L0_xattn_g_res", "L0_xattn_g_init",
         "L0_ffn_Wr", "L0_ffn_br", "L0_ffn_W1", "L0_ffn_b1", "L0_ffn_W2", "L0_ffn_b2", "L1_xattn_w_qkv", "L1_xattn_w_proj",
         "L1_xattn_b_proj", "L1_ffn_gate_w", "L1_ffn_w1", "L1_ffn_w3", "L1_ffn_w2", "L1_ffn_e_bias")


def kernel(**inputs):
    import concourse.bacc as bacc
    from concourse.bass_utils import run_bass_kernel_spmd

    nc = bacc.Bacc("TRN2", target_bir_lowering=False, num_devices=1)
    arrays = {"in_" + n: np.ascontiguousarray(inputs[n]) for n in NAMES}
    aps = {n: nc.dram_tensor("in_" + n, arrays["in_" + n].shape, mybir.dt.from_np(arrays["in_" + n].dtype), kind="ExternalInput").ap() for n in NAMES}
    out = nc.dram_tensor("out", (B, S, D), F32, kind="ExternalOutput").ap()
    flamingo_block(nc, out, **aps)
    return run_bass_kernel_spmd(nc, [arrays], core_ids=[0]).results[0]["out"]
```

```python
from contextlib import ExitStack, contextmanager

import numpy as np
import concourse.bass as bass
from concourse import mybir

F32 = mybir.dt.float32
BF16 = mybir.dt.bfloat16
F16 = mybir.dt.float16
U32 = mybir.dt.uint32
I32 = mybir.dt.int32
ALU = mybir.AluOpType
ACT = mybir.ActivationFunctionType
AX = mybir.AxisListType

P = 128
B, S, D = 2, 1024, 256
DK = D // P
NTOK = B * S
NTILE = NTOK // P
TPB = S // P
CL, CD = 77, 512
HB = 512

E0, K0, H0 = 8, 2, 1024
HK0 = H0 // P
E1, K1, I1 = 32, 4, 192
IH = I1 // 2
NT0 = (NTOK * K0 - E0) // P + E0
NT1 = (NTOK * K1 - E1) // P + E1
RING0, RING1 = 3, 4

HEADS, HD = 16, D // 16
GH = 4
NGRP = B * HEADS // GH
KEYS = CL + S
MT = 1 + TPB
QB = (0, 0, 1, 1, 0, 2)
KB = (0, 1, 0, 1, 2, 0)
XCH = 4
CNTB, DEPB = 4, 3
QROWS = len(QB) * HD
AROWS = QROWS + 3

LN_EPS = 1e-5
RMS_EPS = 1e-5
PATCH_EPS = 1e-3

W1_0, W2_0 = 0, E0 * DK * H0 * 4
ARENA0_END = W2_0 + E0 * HK0 * D * 4
W13_BYTES = DK * 2 * I1 * 4
W2_1 = E1 * W13_BYTES
ARENA = W2_1 + E1 * 2 * D * 4
E1_SCRATCH = 2 * 4 * D * 4
LOGITS_AT = 3 * 4 * D * 4
TOP = ARENA - (DK * D + D + DK * E1) * 4
W2_TOP = (TOP - W2_1) // (2 * D * 4)
EARLY = 26
ATT0 = EARLY * W13_BYTES


class Memory:
    pass


class Chain:

    def __init__(self, eng, sem, carrier=None):
        self.eng, self.sem, self.base, self.k, self.it, self.per, self.carrier = eng, sem, 0, 0, None, 0, carrier

    def __call__(self, ins):
        self.k += 1
        ins.then_inc(self.sem, 1)
        at = self.base + self.k
        self.eng.wait_ge(self.sem, at if self.it is None else self.it * self.per + at)
        if self.carrier is not None:
            self.eng.sem_inc(self.carrier, 1)

    @contextmanager
    def turns(self, it, per, times):
        self.base, self.k, self.it, self.per = self.base + self.k, 0, it, per
        yield
        assert self.k == per, (self.k, per)
        self.base, self.k, self.it = self.base + per * times, 0, None


def tile_loop(eng, n, ring, body):
    for j in range(ring + 1):
        body(j, j % ring, j // ring, j == 0, False)
    turns = (n - 2 - ring) // ring
    with eng.Fori(1, 1 + turns) as t:
        for u in range(ring):
            body(t * ring + (1 + u), (1 + u) % ring, t + (1 + u) // ring, False, False)
    for j in range(1 + ring + turns * ring, n):
        body(j, j % ring, j // ring, False, j == n - 1)


def moments(ch, nc, stats, n, mean, var, ve, tmp, eps):
    v = nc.vector
    v.tensor_tensor(tmp[0], stats[:, :, 1], stats[:, :, 4], ALU.add)
    v.tensor_tensor(tmp[1], stats[:, :, 1], stats[:, :, 4], ALU.subtract)
    ch(v.tensor_tensor(tmp[2], stats[:, :, 2], stats[:, :, 5], ALU.add))
    v.tensor_scalar(mean, tmp[0], 0.5, None, ALU.mult)
    ch(v.tensor_tensor(tmp[3], tmp[1], tmp[1], ALU.mult))
    ch(v.tensor_scalar(tmp[2], tmp[2], 1.0 / n, None, ALU.mult))
    ch(v.scalar_tensor_tensor(var, tmp[3], 0.25, tmp[2], ALU.mult, ALU.add))
    ch(v.tensor_scalar(ve, var, eps, None, ALU.add))


def make_env(nc, ctx, a, out):
    e = Memory()
    e.nc, e.a, e.out = nc, a, out

    def sb(name, shape, dt=F32):
        return ctx.enter_context(nc.sbuf_tensor(name, shape, dt))

    e.used = []

    def new_semaphore(name):
        e.used.append(nc.alloc_semaphore(name=name))
        return e.used[-1]

    e.sem = new_semaphore
    e.w0_in, e.w13_early, e.w13_in, e.w2_in = (ctx.enter_context(nc.semaphore(n)) for n in ("w0_in", "w13_early", "w13_in", "w2_in"))
    e.x = sb("x_resident", [P, NTILE, D])
    e.arena = sb("arena", [P, ARENA // 4])
    e.scr = sb("scratch", [P, NTILE * D])
    e.ident = sb("ident", [P, P])
    e.identb = sb("identb", [P, P], BF16)
    e.not_earlier = sb("not_earlier", [P, P], BF16)
    e.onesb = sb("onesb", [P, P], BF16)
    e.iota = sb("iota", [P, P])
    e.iota_p = sb("iota_p", [P, 1])
    e.stats = sb("stats", [P, NTILE, 6])
    e.mean = sb("mean", [P, NTILE])
    e.rstd = sb("rstd", [P, NTILE])
    e.shift = sb("shift", [P, NTILE])
    e.var = sb("var", [P, NTILE])
    e.ve = sb("ve", [P, NTILE])
    e.std = sb("std", [P, NTILE])
    e.tmp = sb("ln_tmp", [P, 4, NTILE])
    e.tg = sb("tanh_gates", [P, 4])
    e.ebias = sb("ebias", [P, E1])
    e.expert = sb("expert", [1, P], I32)
    e.token_u = sb("token_u", [P, NT1 + RING1], U32)
    e.row_u = sb("row_u", [P, NT0], U32)
    e.slot_u = sb("slot_u", [P, NTILE, K1], U32)
    e.gate = sb("gate", [P, NTILE, K1])
    e.xg = sb("xg", [P, RING1, D])
    e.ysb = sb("ysb", [P, RING1, D])
    e.tcol = sb("tcol", [P, RING1], U32)
    e.rcol = sb("rcol", [P, RING1], U32)
    e.bin = sb("b_in", [P, D])
    e.small = sb("small", [P, P])
    e.ps = ctx.enter_context(nc.psum_tensor("ps", [P, 8, HB], F32))

    def dram(name, shape, dt=F32):
        return nc.dram_tensor(name, shape, dt, kind="Internal").ap()

    e.xn = [dram("xn0", [NTOK, D]), dram("xn1", [NTOK, D])]
    e.y = [dram("y0", [NTOK * K0 + P, D]), dram("y1", [NT1 * P, D])]
    e.qp = dram("q_parts", [3, D, NTOK], BF16)
    e.kp = dram("k_parts", [3, D, B, KEYS], BF16)

    def carve(off, shape, dt=F32, base=e.arena):
        n = int(np.prod(shape))
        words = n * (2 if dt in (BF16, F16) else 4) // 4
        v = base[:].rearrange("p a b -> p (a b)") if len(base.shape) == 3 else base[:]
        v = v[:, off // 4: off // 4 + words]
        if dt != F32:
            v = v.bitcast(dt)
        if len(shape) == 2:
            v = v.rearrange("p (a b) -> p a b", b=shape[1])
        if len(shape) == 3:
            v = v.rearrange("p (a b c) -> p a b c", b=shape[1], c=shape[2])
        if len(shape) == 4:
            v = v.rearrange("p (a b c d) -> p a b c d", b=shape[1], c=shape[2], d=shape[3])
        return v

    e.carve = carve
    e.w1 = carve(W1_0, [E0, DK, H0])
    e.w2 = carve(W2_0, [E0, HK0, D])
    e.w13 = carve(0, [E1, DK, 2 * I1])
    e.w2b = carve(W2_1, [E1, 2, D])
    o = e.b2_at = ARENA0_END
    e.b2bc = carve(o, [E0, D]); o += E0 * D * 4
    e.wqkv_at = o
    e.wqkvT = carve(o, [DK, 3 * D]); o += DK * 3 * D * 4
    e.ctx = carve(o, [B, CD])[0:CL]; o += B * CD * 4
    e.b1T = carve(o, [E0 * HK0]); o += E0 * HK0 * 4
    e.wr = carve(o, [DK, E0]); o += DK * E0 * 4
    e.br = carve(o, [E0]); o += E0 * 4
    e.free0 = o
    e.dep = carve(o, [B, D]); o += B * D * 4
    e.plug = carve(o, [NTOK], BF16); o += NTOK * 2
    e.winT = carve(o, [DK, D]); o += DK * D * 4
    e.free1 = o
    o = TOP
    e.wprojT = carve(o, [DK, D]); o += DK * D * 4
    e.bproj = carve(o, [D]); o += D * 4
    e.gateT = carve(o, [DK, E1])
    return e


def prepare(e):
    nc, a, ps = e.nc, e.a, e.ps
    sem = e.sem
    ctx_in, win_in, wqkv_in, small_in = sem("ctx_in"), sem("win_in"), sem("wqkv_in"), sem("small_in")
    x_in = [sem(f"x_in{c}") for c in range(XCH)]
    patch_consts, ident_set, decay_set = sem("patch_consts"), sem("ident_set"), sem("decay_set")
    tr_raw, tr_done = sem("prep_tr_raw"), sem("prep_tr_done")
    pool_step, dve_step = sem("prep_pool_step"), sem("prep_dve_step")
    var_ready, std_ready = sem("prep_var"), sem("prep_std")
    u_ready, lens_ready, bidx_raw = sem("u_ready"), sem("lens_ready"), sem("bidx_raw")
    begun_ready = sem("begun_ready")

    room = [[e.arena, e.free1, TOP], [e.scr, 0, NTILE * D * 4], [e.small, 0, P * 4]]

    def buf(shape, dt=F32):
        size = int(np.prod(shape)) * (2 if dt == BF16 else 4)
        for part in room:
            if part[1] + size <= part[2]:
                part[1] += size
                return e.carve(part[1] - size, shape, dt, base=part[0])
        raise ValueError("no room for " + str(shape))

    u = buf([B, D])[0:CL]
    wqkv = buf([6, D]); wproj = buf([DK, D]); gatew = buf([D]); b1r = buf([P]); win = buf([DK, D])
    ginit = buf([D])[0:CL]; gres = buf([DK]); g4 = buf([4])
    tri = buf([CL])[0:CL]
    earlier = buf([CL])[0:CL]
    ones = buf([CL])[0:CL]
    tdec = buf([CL])[0:CL]
    lens_i = buf([B]).bitcast(I32)[0:CL]; lens = buf([B])[0:CL]; lens_bc = buf([B, CL])[0:CL]
    BC = B * CL
    bidx = buf([BC + B])[0:CL]
    copies = buf([B])[0:CL]; inside = buf([B])[0:CL]; counts = buf([B])[0:CL]
    counts_bc = buf([B, CL], BF16)[0:CL]
    cs = buf([B, 6])[0:CL]; cm = buf([8, B])[0:CL]
    begun = e.ysb[:].rearrange("p a b -> p (a b)").bitcast(BF16).rearrange("p (b t) -> p b t", b=B)[0:CL]
    iota_t = e.xg[:].rearrange("p a b -> p (a b)")[0:CL, 0:S]
    NTR, BIB, TRB = 3, CNTB, 0
    N_CTX, N_WIN, N_SMALL = 3, 4, 8
    wrap = ps[0:CL, BIB + 1, 0:BC + B]
    same = ps[0:CL, TRB, 0:BC].rearrange("p (b q) -> p b q", b=B)

    TURNS_BEFORE_ROOT = (4, 4)
    turn = []
    for dk in range(DK):
        for et in range(DK):
            turn.append((win[:, et, dk * P:(dk + 1) * P], P, e.winT[:, dk, et * P:(et + 1) * P], gres[:, dk:dk + 1]))
    MIXER_TURNS = len(turn)
    for dk in range(DK):
        for et in range(6):
            turn.append((wqkv[:, et, dk * P:(dk + 1) * P], P, e.wqkvT[:, dk, et * P:(et + 1) * P], None))
    QKV_TURNS = len(turn)
    for dk in range(DK):
        for et in range(DK):
            turn.append((wproj[:, et, dk * P:(dk + 1) * P], P, e.wprojT[:, dk, et * P:(et + 1) * P], None))
        turn.append((gatew[0:E1, dk * P:(dk + 1) * P], E1, e.gateT[:, dk, :], None))
    turn.append((b1r[0:E0 * HK0, :], E0 * HK0, e.b1T, None))

    dt = float(-np.log(-np.expm1(np.float32(-PATCH_EPS)).astype(np.float32)).astype(np.float32))
    bcoef = float(np.exp(np.float32(-PATCH_EPS)))
    decay = [bcoef * float(np.exp(-dt * k)) for k in range(CL)]
    decay = [w for w in decay if np.float32(w) > 0]

    with nc.Block() as block:
        @block.sync
        def _(sp):
            def load(dst, src, loaded):
                sp.dma_start(dst, src, allow_slow_non_contiguous=True).then_inc(loaded, 16)

            load(lens_i, a["mask_BxS2_if0"].rearrange("b s -> s b"), ctx_in)
            load(e.ctx, a["ctx_2048"].rearrange("b s d -> s b d"), ctx_in)
            load(ginit, a["L0_xattn_g_init"][0:D].partition_broadcast(CL), ctx_in)
            x = a["x"].rearrange("b (t p) d -> p (b t) d", p=P)
            for c in range(XCH):
                tiles = slice(c * NTILE // XCH, (c + 1) * NTILE // XCH)
                load(e.x[:, tiles], x[:, tiles], x_in[c])
            for dst, src in (
                (win, a["L0_xattn_W_in"].rearrange("(k p) d -> p k d", p=P)),
                (gres, a["L0_xattn_g_res"].rearrange("(k p) -> p k", p=P)),
                (e.bin[0:CL, :], a["L0_xattn_b_in"].partition_broadcast(CL)),
                (g4[:, 0:2], a["g_xattn"].partition_broadcast(P)),
            ):
                load(dst, src, win_in)
            load(wqkv, a["L1_xattn_w_qkv"].rearrange("(k p) d -> p k d", p=P), wqkv_in)
            for dst, src in (
                (g4[:, 2:4], a["g_ffn"].partition_broadcast(P)),
                (wproj, a["L1_xattn_w_proj"].rearrange("(k p) d -> p k d", p=P)),
                (gatew[0:E1, :], a["L1_ffn_gate_w"]),
                (b1r[0:E0 * HK0, :], a["L0_ffn_b1"].rearrange("e (k p) -> (e k) p", p=P)),
                (e.wr, a["L0_ffn_Wr"].rearrange("(k p) e -> p k e", p=P)),
                (e.br, a["L0_ffn_br"].partition_broadcast(P)),
                (e.ebias[:], a["L1_ffn_e_bias"].partition_broadcast(P)),
                (e.bproj, a["L1_xattn_b_proj"].partition_broadcast(P)),
            ):
                load(dst, src, small_in)
            sp.dma_start(e.b2bc, a["L0_ffn_b2"].rearrange("e d -> (e d)").partition_broadcast(P).rearrange("p (e d) -> p e d", d=D)).then_inc(e.w0_in, 16)
            for ex in range(E0):
                sp.dma_start(e.w1[:, ex], a["L0_ffn_W1"][ex].rearrange("(k p) h -> p k h", p=P)).then_inc(e.w0_in, 16)
                sp.dma_start(e.w2[:, ex], a["L0_ffn_W2"][ex].rearrange("(k p) d -> p k d", p=P)).then_inc(e.w0_in, 16)

        @block.gpsimd
        def _(pool):
            ch = Chain(pool, pool_step)
            g = nc.gpsimd
            g.memset(ones, 1.0)
            g.memset(tri, 1.0)
            ch(g.memset(earlier, 1.0))
            g.affine_select(out=tri, in_=tri, compare_op=ALU.is_ge, fill=0.0, base=0, pattern=[[1, CL]], channel_multiplier=-1)
            g.affine_select(out=earlier, in_=earlier, compare_op=ALU.is_gt, fill=0.0, base=0, pattern=[[-1, CL]], channel_multiplier=1)
            g.iota(iota_t, pattern=[[1, S]], base=0, channel_multiplier=0, allow_small_or_imprecise_dtypes=True)
            g.drain().then_inc(patch_consts, 1)
            g.memset(e.ident[:], 0.0)
            ch(g.memset(tdec, 0.0))
            g.affine_select(out=e.ident[:], in_=e.ident[:], compare_op=ALU.not_equal, fill=1.0, base=0, pattern=[[-1, P]], channel_multiplier=1).then_inc(ident_set, 1)
            for k, w in enumerate(decay):
                ch(g.affine_select(out=tdec, in_=tdec, compare_op=ALU.not_equal, fill=w, base=-k, pattern=[[1, CL]], channel_multiplier=-1))
            pool.sem_inc(decay_set, 1)
            g.memset(e.identb[:], 0.0)
            g.memset(e.not_earlier[:], 0.0)
            g.memset(e.token_u[:], 0)
            ch(g.memset(e.onesb[:], 1.0))
            g.affine_select(out=e.identb[:], in_=e.identb[:], compare_op=ALU.not_equal, fill=1.0, base=0, pattern=[[-1, P]], channel_multiplier=1)
            g.affine_select(out=e.not_earlier[:], in_=e.not_earlier[:], compare_op=ALU.is_gt, fill=-1.0, base=0, pattern=[[1, P]], channel_multiplier=-1)
            g.iota(e.iota[:], pattern=[[1, P]], base=0, channel_multiplier=0, allow_small_or_imprecise_dtypes=True)
            g.iota(e.iota_p[:], pattern=[[0, 1]], base=0, channel_multiplier=1, allow_small_or_imprecise_dtypes=True)

        @block.tensor
        def _(pe):
            def turns(first, end):
                for n in range(first, end):
                    src, rows = turn[n][0:2]
                    if n >= NTR:
                        pe.wait_ge(tr_done, n - NTR + 1)
                    nc.tensor.transpose(ps[:, TRB + n % NTR, 0:rows], src, e.ident[0:rows, 0:rows]).then_inc(tr_raw, 1)

            pe.wait_ge(lens_ready, B)
            for b in range(B):
                nc.tensor.matmul(ps[0:CL, BIB, b * CL:(b + 1) * CL], lens_bc[:, b, :], tri, start=True, stop=True)
            nc.tensor.matmul(ps[0:CL, BIB, BC:BC + B], tri, lens, start=True, stop=True).then_inc(bidx_raw, 1)
            pe.wait_ge(decay_set, 1)
            pe.wait_ge(u_ready, B)
            nc.tensor.matmul(ps[0:CL, DEPB, :], tdec, u.rearrange("p b d -> p (b d)"), start=True, stop=True)
            pe.wait_ge(ident_set, 1)
            pe.wait_ge(win_in, 16 * N_WIN)
            turns(0, MIXER_TURNS)
            pe.wait_ge(wqkv_in, 16)
            turns(MIXER_TURNS, QKV_TURNS)
            for b in range(B):
                pe.wait_ge(begun_ready, b + 1)
                for h in range(S // HB):
                    nc.tensor.matmul(ps[0:CL, CNTB + 2 * b + h, :], counts_bc[:, b, :], begun[:, b, h * HB:(h + 1) * HB], start=True, stop=True)
            pe.wait_ge(small_in, 16 * N_SMALL)
            turns(QKV_TURNS, len(turn))

        @block.scalar
        def _(act):
            def copies(first, end):
                for n in range(first, end):
                    rows, dst, scale = turn[n][1:]
                    act.wait_ge(tr_raw, n + 1)
                    if scale is None:
                        nc.scalar.activation(dst, ps[:, TRB + n % NTR, 0:rows], ACT.Copy).then_inc(tr_done, 1)
                    else:
                        nc.scalar.activation(dst, ps[:, TRB + n % NTR, 0:rows], ACT.Copy, scale=scale).then_inc(tr_done, 1)

            act.wait_ge(var_ready, 1)
            nc.scalar.activation(cm[:, 6, :], cm[:, 5, :], ACT.Sqrt).then_inc(std_ready, 1)
            act.wait_ge(win_in, 16 * N_WIN)
            copies(0, MIXER_TURNS)
            at = MIXER_TURNS
            for n in range(2):
                copies(at, at + TURNS_BEFORE_ROOT[n])
                at += TURNS_BEFORE_ROOT[n]
                act.wait_ge(var_ready, 2 + n)
                nc.scalar.activation(e.std[:], e.ve[:], ACT.Sqrt).then_inc(std_ready, 1)
            copies(at, QKV_TURNS)
            act.wait_ge(small_in, 16 * N_SMALL)
            nc.scalar.activation(e.tg[:], g4, ACT.Tanh)
            copies(QKV_TURNS, len(turn))

        @block.vector
        def _(dve):
            ch = Chain(dve, dve_step)
            v = nc.vector
            dve.wait_ge(ctx_in, 16 * N_CTX)
            ch(v.tensor_copy(lens, lens_i))
            dve.wait_ge(patch_consts, 1)
            for b in range(B):
                v.tensor_scalar(lens_bc[:, b, :], ones, lens[:, b:b + 1], None, ALU.mult).then_inc(lens_ready, 1)

            for b in range(B):
                ch(v.bn_stats(cs[:, b, :], e.ctx[:, b, :]))
            c = [cm[:, n, :] for n in range(8)]
            moments(ch, nc, cs, CD, c[4], c[5], c[6], c[0:4], RMS_EPS)
            ch(v.tensor_tensor(c[0], c[4], c[4], ALU.mult))
            v.tensor_tensor(c[5], c[0], c[6], ALU.add).then_inc(var_ready, 1)

            dve.wait_ge(bidx_raw, 1)
            ch(v.tensor_scalar(bidx, ps[0:CL, BIB, 0:BC + B], -1.0, None, ALU.add))
            ch(v.tensor_scalar(wrap, bidx, 0.0, float(S), ALU.is_lt, ALU.mult))
            ch(v.tensor_tensor(bidx, bidx, wrap, ALU.add))
            for b in range(B):
                v.scalar_tensor_tensor(same[:, b, :], bidx[:, b * CL:(b + 1) * CL], bidx[:, BC + b:BC + b + 1], earlier, ALU.is_equal, ALU.mult)
            ch(v.tensor_scalar(inside, bidx[:, BC:BC + B], 0.0, None, ALU.is_ge))
            ch(v.tensor_reduce(copies, same, AX.X, ALU.add))
            ch(v.scalar_tensor_tensor(counts, copies, 0.0, inside, ALU.is_equal, ALU.mult))
            for b in range(B):
                v.tensor_scalar(counts_bc[:, b, :], ones, counts[:, b:b + 1], None, ALU.mult)

            dve.wait_ge(std_ready, 1)
            ch(v.reciprocal(c[7], c[6]))
            for b in range(B):
                v.scalar_tensor_tensor(u[:, b, :], e.ctx[:, b, 0:D], cm[:, 7, b:b + 1], ginit, ALU.mult, ALU.mult).then_inc(u_ready, 1)

            def begin(b):
                v.tensor_scalar(begun[:, b, :], iota_t, bidx[:, BC + b:BC + b + 1], None, ALU.is_ge).then_inc(begun_ready, 1)

            for i in range(NTILE):
                if i % (NTILE // XCH) == 0:
                    dve.wait_ge(x_in[i // (NTILE // XCH)], 16)
                v.bn_stats(e.stats[:, i, :], e.x[:, i, :])
            ch(v.memset(e.tmp[:, 0, :], 0.0))
            t = [e.tmp[:, n, :] for n in range(4)]
            moments(ch, nc, e.stats, D, e.mean[:], e.var[:], e.ve[:], t, LN_EPS)
            v.engine_nop().then_inc(var_ready, 1)
            begin(0)
            dve.wait_ge(std_ready, 2)
            ch(v.reciprocal(e.rstd[:], e.std[:]))
            ch(v.tensor_tensor(e.tmp[:, 0, :], e.rstd[:], e.rstd[:], ALU.mult))
            ch(v.tensor_tensor(e.tmp[:, 1, :], e.tmp[:, 0, :], e.var[:], ALU.mult))
            v.tensor_scalar(e.ve[:], e.tmp[:, 1, :], RMS_EPS, None, ALU.add).then_inc(var_ready, 1)
            begin(1)
            dve.wait_ge(std_ready, 3)
            ch(v.reciprocal(e.tmp[:, 2, :], e.std[:]))
            ch(v.tensor_tensor(e.rstd[:], e.rstd[:], e.tmp[:, 2, :], ALU.mult))
            ch(v.scalar_tensor_tensor(e.shift[:], e.mean[:], -1.0, e.rstd[:], ALU.mult, ALU.mult))


def depool_mixer(e):
    nc, ps, sem = e.nc, e.ps, e.sem
    xn_ready, xT_raw, xT_ready = sem("mix_xn_ready"), sem("mix_xT_raw"), sem("mix_xT_ready")
    mixed_raw, x_new = sem("mix_raw"), sem("mix_x_new")
    oh_ready, step, dep_taken = sem("mix_oh_ready"), sem("mix_step"), sem("mix_dep_taken")
    U = 4
    LAG = 3
    xn = e.carve(0, [U, D], base=e.scr)
    xT = e.carve(U * D * 4, [U, DK, P], base=e.scr)
    oh = e.carve(2 * U * D * 4, [U, P], base=e.scr)

    with nc.Block() as block:
        @block.vector
        def _(dve):
            v = nc.vector
            ch = Chain(dve, step)
            v.tensor_tensor(e.dep[0:CL], ps[0:CL, DEPB, :].rearrange("p (b d) -> p b d", b=B), e.bin[0:CL].unsqueeze(1).broadcast_to([CL, B, D]), ALU.add).then_inc(dep_taken, 1)
            for b in range(B):
                ch(v.tensor_scalar(e.plug[0:CL, b * S:(b + 1) * S], ps[0:CL, CNTB + 2 * b:CNTB + 2 * b + 2, :].rearrange("p a b -> p (a b)"), -1.0, 0.0, ALU.add, ALU.max))

            def patch(i):
                v.tensor_scalar(oh[0:CL, i % U, :], e.plug[0:CL, i * P:(i + 1) * P], e.iota_p[0:CL, :], None, ALU.is_equal).then_inc(oh_ready, 1)

            for i in range(U):
                patch(i)
            for i in range(NTILE + 1):
                if i < NTILE:
                    dve.wait_ge(mixed_raw, i + 1)
                    v.scalar_tensor_tensor(e.x[:, i, :], ps[:, U + i % U, 0:D], e.tg[:, 0:1], e.x[:, i, :], ALU.mult, ALU.add).then_inc(x_new, 1)
                if i + U < NTILE:
                    patch(i + U)
                if i >= 1:
                    dve.wait_ge(x_new, i)
                    v.bn_stats(e.stats[:, i - 1, :], e.x[:, i - 1, :])

        @block.tensor
        def _(pe):
            for i in range(NTILE + LAG):
                if i < NTILE:
                    pe.wait_ge(xn_ready, i + 1)
                    if i == DEPB:
                        pe.wait_ge(dep_taken, 1)
                    if i >= U:
                        pe.wait_ge(xT_ready, i - U + 1)
                    for k in range(DK):
                        last = nc.tensor.transpose(ps[:, i % U, k * P:(k + 1) * P], xn[:, i % U, k * P:(k + 1) * P], e.ident[:])
                    last.then_inc(xT_raw, 1)
                if i >= LAG:
                    j = i - LAG
                    pe.wait_ge(xT_ready, j + 1)
                    pe.wait_ge(oh_ready, j + 1)
                    if j >= U:
                        pe.wait_ge(x_new, j - U + 1)
                    for k in range(DK):
                        nc.tensor.matmul(ps[:, U + j % U, 0:D], xT[:, j % U, k, :], e.winT[:, k, :], start=(k == 0), stop=False)
                    nc.tensor.matmul(ps[:, U + j % U, 0:D], oh[0:CL, j % U, :], e.dep[0:CL, j // TPB, :], start=False, stop=True).then_inc(mixed_raw, 1)

        @block.scalar
        def _(act):
            for i in range(NTILE + 2):
                if i < NTILE:
                    if i >= U:
                        act.wait_ge(xT_raw, i - U + 1)
                    nc.scalar.activation(xn[:, i % U, :], e.x[:, i, :], ACT.Identity, scale=e.rstd[:, i:i + 1], bias=e.shift[:, i:i + 1]).then_inc(xn_ready, 1)
                if i >= 2:
                    j = i - 2
                    act.wait_ge(xT_raw, j + 1)
                    if j >= U:
                        act.wait_ge(mixed_raw, j - U + 1)
                    nc.scalar.activation(xT[:, j % U, :, :].rearrange("p k t -> p (k t)"), ps[:, j % U, 0:D], ACT.Copy).then_inc(xT_ready, 1)


def router(e, layer):
    nc, ps, sem = e.nc, e.ps, e.sem
    ne = (E0, E1)[layer]
    wr = (e.wr, e.gateT)[layer]
    nm = f"rt{layer}_"
    xn_ready, xT_raw, xT_ready = sem(nm + "xn_ready"), sem(nm + "xT_raw"), sem(nm + "xT_ready")
    lg_raw, lg_done, step = sem(nm + "lg_raw"), sem(nm + "lg_done"), sem(nm + "step")
    var_ready, std_ready, rstd_ready = (sem(nm + n) for n in ("var", "std", "rstd"))
    U, R = 4, 8
    stored = [sem(nm + f"xn_stored{r}") for r in range(R)]
    xn = e.carve(0, [R, D], base=e.scr)
    xT = e.carve(R * D * 4, [U, DK, P], base=e.scr)
    e.logits = e.carve(LOGITS_AT, [NTILE, ne], base=e.scr)

    with nc.Block() as block:
        @block.vector
        def _(dve):
            v = nc.vector
            ch = Chain(dve, step)
            moments(ch, nc, e.stats, D, e.mean[:], e.var[:], e.ve[:], [e.tmp[:, n, :] for n in range(4)], LN_EPS)
            v.engine_nop().then_inc(var_ready, 1)
            dve.wait_ge(std_ready, 1)
            ch(v.reciprocal(e.rstd[:], e.std[:]))
            v.scalar_tensor_tensor(e.shift[:], e.mean[:], -1.0, e.rstd[:], ALU.mult, ALU.mult).then_inc(rstd_ready, 1)
            for i in range(NTILE):
                dve.wait_ge(lg_raw, i + 1)
                if layer == 0:
                    v.tensor_tensor(e.logits[:, i, :], ps[:, U + i % U, 0:ne], e.br, ALU.add).then_inc(lg_done, 1)
                else:
                    v.tensor_copy(e.logits[:, i, :], ps[:, U + i % U, 0:ne]).then_inc(lg_done, 1)

        @block.scalar
        def _(act):
            def norm(i):
                if i >= R:
                    act.wait_ge(stored[i % R], 16)
                    act.wait_ge(xT_raw, i - R + 1)
                nc.scalar.activation(xn[:, i % R, :], e.x[:, i, :], ACT.Identity, scale=e.rstd[:, i:i + 1], bias=e.shift[:, i:i + 1]).then_inc(xn_ready, 1)

            act.wait_ge(var_ready, 1)
            nc.scalar.activation(e.std[:], e.ve[:], ACT.Sqrt).then_inc(std_ready, 1)
            act.wait_ge(rstd_ready, 1)
            for i in range(NTILE + 2):
                if i < NTILE:
                    norm(i)
                if i >= 2:
                    act.wait_ge(xT_raw, i - 1)
                    if i - 2 >= U:
                        act.wait_ge(lg_raw, i - 1 - U)
                    nc.scalar.activation(xT[:, (i - 2) % U, :, :].rearrange("p k t -> p (k t)"), ps[:, (i - 2) % U, 0:D], ACT.Copy).then_inc(xT_ready, 1)

        @block.sync
        def _(sp):
            for i in range(NTILE):
                sp.wait_ge(xn_ready, i + 1)
                sp.dma_start(e.xn[layer][i * P:(i + 1) * P, :], xn[:, i % R, :]).then_inc(stored[i % R], 16)
            for r in range(R):
                sp.wait_ge(stored[r], 16 * (NTILE // R))

        @block.tensor
        def _(pe):
            for i in range(NTILE + 3):
                if i < NTILE:
                    pe.wait_ge(xn_ready, i + 1)
                    if i >= U:
                        pe.wait_ge(xT_ready, i - U + 1)
                    for k in range(DK):
                        last = nc.tensor.transpose(ps[:, i % U, k * P:(k + 1) * P], xn[:, i % R, k * P:(k + 1) * P], e.ident[:])
                    last.then_inc(xT_raw, 1)
                if i >= 3:
                    j = i - 3
                    pe.wait_ge(xT_ready, j + 1)
                    if j >= U:
                        pe.wait_ge(lg_done, j - U + 1)
                    for k in range(DK):
                        last = nc.tensor.matmul(ps[:, U + j % U, 0:ne], xT[:, j % U, k, :], wr[:, k, :], start=(k == 0), stop=(k == DK - 1))
                    last.then_inc(lg_raw, 1)


def route(e, layer):
    nc, ps, sem = e.nc, e.ps, e.sem
    ne, kk, nt = ((E0, K0, NT0), (E1, K1, NT1))[layer]
    nm = f"ro{layer}_"
    step, act_in, act_out, pool_step = (sem(nm + n) for n in ("step", "act_in", "act_out", "pool_step"))
    mask_ready, rank_raw, first_ready, first_raw, parts_ready = (sem(nm + n) for n in ("mask", "rank_raw", "first", "first_raw", "parts"))
    off_ready, row_ready, col_ready, pick_used, token_raw = (sem(nm + n) for n in ("off_ready", "row_ready", "col_ready", "pick_used", "token_raw"))
    ring = RING1 * D * 4
    free = [[e.scr, 0, LOGITS_AT], [e.scr, LOGITS_AT + NTILE * ne * 4, NTILE * D * 4], [e.xg, 0, ring], [e.ysb, 0, ring]]

    def buf(shape, dt=F32):
        size = int(np.prod(shape)) * (2 if dt in (BF16, F16) else 4)
        for part in free:
            if part[1] + size <= part[2]:
                part[1] += size
                return e.carve(part[1] - size, shape, dt, base=part[0])
        raise ValueError("no room for " + str(shape))

    def flat(ap):
        return ap.rearrange("p a b -> p (a b)")

    N, NQ = NTILE * ne, NTILE * kk
    W, WA = 4, (1, 2)
    TURNS = NQ // W
    place = buf([NTILE, ne]); work = buf([NTILE, ne])
    upto_i = buf([ne, NTILE]); carry = buf([ne, NTILE])
    assert layer == 0 or free[0][1] >= E1_SCRATCH
    chosen = buf([kk, NTILE, ne], BF16)
    sel, sig = (e.logits, None) if layer == 0 else (place, e.logits)
    e.chosen, e.sig = chosen, sig
    maskb = buf([NTILE, ne], BF16)
    top = buf([NTILE, 8]); topi = buf([NTILE, 8]).bitcast(U32); topf = top
    tiles_i = buf([ne]).bitcast(I32); tiles = buf([ne]); upto = buf([ne]); start = buf([ne]); below = buf([ne])
    first = buf([1])
    slot = buf([NTILE, kk]); slot_i = buf([NTILE, kk]).bitcast(I32)
    part_i = buf([NTILE, kk]).bitcast(I32); part = buf([NTILE, kk]); minus_part = buf([NTILE, kk])
    tile_i = part_i; tile_f = buf([NTILE, kk])
    row1 = buf([NTILE, kk]); minus_row1 = buf([NTILE, kk])
    choice_rows = NTOK if layer == 0 else 0
    spare = buf([1])
    w = buf([NTILE, kk]); tot = buf([NTILE])
    row_i = buf([nt]).bitcast(I32); none = buf([nt]) if layer == 0 else None
    if layer == 0:
        row_is, col_is, off = ([buf([W, n]) for _ in range(2)] for n in (P, nt, P))
    else:
        row_is = [flat(place).bitcast(F16)[:, n * W * P:(n + 1) * W * P].rearrange("p (w c) -> p w c", c=P) for n in range(2)]
        col_is = [flat(upto_i).bitcast(F16)[:, n * W * nt:(n + 1) * W * nt].rearrange("p (w c) -> p w c", c=nt) for n in range(2)]
        off = [flat(work)[:, n * 2 * P:(n + 1) * 2 * P].rearrange("p (w c) -> p w c", c=P) for n in range(2)]

    def rows_before(t):
        return t // 2 * sum(WA) + t % 2 * WA[0]

    def bc(ap, n):
        return ap.unsqueeze(2).broadcast_to([P, ap.shape[1], n])

    with nc.Block() as block:
        if layer == 1:
            @block.sync
            def _(sp):
                for x in range(W2_TOP, E1):
                    load_w2(e, sp, x)

        @block.gpsimd
        def _(pool):
            g_ = nc.gpsimd
            g_.iota(row1, pattern=[[P, NTILE], [choice_rows, kk]], base=1, channel_multiplier=1, allow_small_or_imprecise_dtypes=True)
            g_.iota(minus_row1, pattern=[[-P, NTILE], [-choice_rows, kk]], base=-1, channel_multiplier=-1, allow_small_or_imprecise_dtypes=True)
            g_.iota(spare, pattern=[[0, 1]], base=NTOK * kk + 1, channel_multiplier=1, allow_small_or_imprecise_dtypes=True).then_inc(pool_step, 1)

        @block.scalar
        def _(act):
            act.wait_ge(act_in, 1)
            if layer == 0:
                nc.scalar.activation(w, w, ACT.Exp).then_inc(act_out, 1)
            else:
                nc.scalar.activation(sig, e.logits, ACT.Exp, scale=-1.0).then_inc(act_out, 1)
            act.wait_ge(parts_ready, 1)
            mf = minus_part.rearrange("p i k -> p (i k)")

            act.wait_ge(pool_step, 1)
            rf, mrf = flat(row1), flat(minus_row1)
            for t in range(TURNS):
                for u in range(WA[t % 2]):
                    if t >= 2:
                        act.wait_ge(row_ready, rows_before(t - 2) + u + 1)
                    q = t * W + u
                    nc.scalar.activation(off[t % 2][:, u, :], e.iota[:], ACT.Abs, bias=mf[:, q:q + 1]).then_inc(off_ready, 1)
                for u in range(WA[t % 2]):
                    act.wait_ge(off_ready, rows_before(t) + u + 1)
                    if t >= 2:
                        act.wait_ge(pick_used, (t - 2) * W + u + 1)
                    q = t * W + u
                    nc.scalar.activation(row_is[t % 2][:, u, :], off[t % 2][:, u, :], ACT.Relu, bias=rf[:, q:q + 1], scale=mrf[:, q:q + 1]).then_inc(row_ready, 1)

        @block.vector
        def _(dve):
            v = nc.vector
            ch = Chain(dve, step)
            if layer == 1:
                v.engine_nop().then_inc(act_in, 1)
                dve.wait_ge(act_out, 1)
                ch(v.tensor_scalar(sig, sig, 1.0, None, ALU.add))
                ch(v.reciprocal(sig, sig))
                ch(v.tensor_tensor(sel, sig, e.ebias[:].unsqueeze(1).broadcast_to([P, NTILE, ne]), ALU.add))
            for i in range(NTILE):
                v.max(top[:, i, :], sel[:, i, :])
            ch(v.memset(tot, 0.0))
            for i in range(NTILE):
                v.max_index(topi[:, i, :], top[:, i, :], sel[:, i, :])
            ch(v.memset(below, 0.0))
            if layer == 0:
                ch(v.tensor_tensor(w, top[:, :, 0:kk], bc(top[:, :, 0], kk), ALU.subtract))
                v.engine_nop().then_inc(act_in, 1)
            ch(v.tensor_copy(topf, topi))
            for k in range(kk):
                v.tensor_tensor(chosen[:, k], e.iota[:, 0:ne].unsqueeze(1).broadcast_to([P, NTILE, ne]), bc(topf[:, :, k], ne), ALU.is_equal)
            ch(v.memset(tot, 0.0))
            for k in range(1, kk - 1):
                ch(v.tensor_tensor(maskb, maskb if k > 1 else chosen[:, 0], chosen[:, k], ALU.add))
            v.tensor_tensor(maskb, maskb if kk > 2 else chosen[:, 0], chosen[:, kk - 1], ALU.add).then_inc(mask_ready, 1)

            if layer == 0:
                dve.wait_ge(act_out, 1)
                ch(v.tensor_reduce(tot, w, AX.X, ALU.add))
                ch(v.reciprocal(tot, tot))
                ch(v.scalar_tensor_tensor(e.gate[:, :, 0:kk], w, e.tg[:, 2:3], bc(tot, kk), ALU.mult, ALU.mult))

            ch(v.memset(carry, 1.0))
            ch(v.memset(carry[:, :, 0:1], 0.0))
            dve.wait_ge(rank_raw, 2)
            ch(v.tensor_copy(flat(place).rearrange("p (e i) -> p e i", e=ne), ps[:, 1, 0:N].rearrange("p (i e) -> p e i", e=ne)))
            ch(v.tensor_tensor_scan(flat(upto_i), flat(carry), flat(place), 0.0, ALU.mult, ALU.add))
            ch(v.tensor_scalar(tiles_i, upto_i[:, :, NTILE - 1], float(P - 1), None, ALU.add))
            ch(v.tensor_scalar(tiles_i, tiles_i, 7, None, ALU.logical_shift_right))
            v.memset(below, 1.0)
            ch(v.tensor_copy(tiles, tiles_i))
            ch(v.tensor_tensor_scan(upto, below, tiles, 0.0, ALU.mult, ALU.add))
            ch(v.tensor_tensor(start, upto, tiles, ALU.subtract))

            ch(v.tensor_tensor(place, ps[:, 0, 0:N].rearrange("p (i e) -> p i e", e=ne), upto_i.rearrange("p e i -> p i e"), ALU.add))
            ch(v.scalar_tensor_tensor(place, start.unsqueeze(1).broadcast_to([P, NTILE, ne]), float(P), place, ALU.mult, ALU.add))
            for k in range(kk):
                ch(v.tensor_tensor(work, chosen[:, k], place, ALU.mult))
                ch(v.tensor_reduce(slot[:, :, k], work, AX.X, ALU.add))
            ch(v.tensor_copy(slot_i, slot))
            if layer == 1:
                v.tensor_copy(e.slot_u[:], slot)
            ch(v.tensor_scalar(part_i, slot_i, P - 1, None, ALU.bitwise_and))
            v.tensor_copy(part, part_i)
            ch(v.tensor_scalar(minus_part, part_i, -1.0, None, ALU.mult))
            v.engine_nop().then_inc(parts_ready, 1)
            ch(v.tensor_scalar(tile_i, slot_i, 7, None, ALU.logical_shift_right))
            ch(v.tensor_copy(tile_f, tile_i))

            dve.wait_ge(pool_step, 1)
            pf, tf, rf = (z.rearrange("p i k -> p (i k)") for z in (part, tile_f, row1))

            for t in range(TURNS):
                q = t * W
                if t >= 2:
                    dve.wait_ge(pick_used, q - W)
                v.tensor_tensor(col_is[t % 2], e.iota[:, 0:nt].unsqueeze(1).broadcast_to([P, W, nt]), bc(tf[:, q:q + W], nt), ALU.is_equal).then_inc(col_ready, 1)
                for u in range(WA[t % 2], W):
                    v.tensor_scalar(row_is[t % 2][:, u, :], e.iota[:], pf[:, q + u:q + u + 1], rf[:, q + u:q + u + 1], ALU.is_equal, ALU.mult).then_inc(col_ready, 1)

            ch(v.tensor_scalar(below, upto, e.iota_p[:], None, ALU.is_le))
            ch(v.tensor_reduce(first, below, AX.X, ALU.add))
            v.tensor_scalar(first, first, float(ne - 1), None, ALU.min).then_inc(first_ready, 1)

            dve.wait_ge(token_raw, 1)
            row = ps[:, 3, 0:nt]
            if layer == 0:
                v.tensor_scalar(none, row, 0.0, spare, ALU.is_equal, ALU.mult)
            ch(v.tensor_scalar(row_i, row, -1.0, None, ALU.add))
            if layer == 0:
                v.scalar_tensor_tensor(e.row_u[:], none, -1.0, row, ALU.add, ALU.add)
            v.tensor_scalar(e.token_u[:, 0:nt].bitcast(I32), row_i, NTOK - 1, None, ALU.bitwise_and)
            dve.wait_ge(first_raw, 1)
            v.tensor_copy(e.expert[0:1, :], ps[0:1, 2, 0:P])

        @block.tensor
        def _(pe):
            pe.wait_ge(mask_ready, 1)
            m = maskb.rearrange("p i e -> p (i e)")
            nc.tensor.matmul(ps[:, 0, 0:N], e.not_earlier[:], m, start=True, stop=True).then_inc(rank_raw, 1)
            nc.tensor.matmul(ps[:, 1, 0:N], e.onesb[:], m, start=True, stop=True).then_inc(rank_raw, 1)

            for t in range(TURNS):
                for u in range(W):
                    made = t * W - rows_before(t) + t
                    if u < WA[t % 2]:
                        pe.wait_ge(row_ready, rows_before(t) + u + 1)
                        pe.wait_ge(col_ready, made + 1)
                    else:
                        pe.wait_ge(col_ready, made + 1 + u - WA[t % 2] + 1)
                    end = t == TURNS - 1 and u == W - 1
                    ins = nc.tensor.matmul(ps[:, 3, 0:nt], row_is[t % 2][:, u, :], col_is[t % 2][:, u, :], start=t == 0 and u == 0, stop=end)
                    ins.then_inc(token_raw if end else pick_used, 1)
            pe.wait_ge(first_ready, 1)
            nc.tensor.transpose(ps[0:1, 2, 0:P], first, e.ident[:]).then_inc(first_raw, 1)


def move_tiles(e, layer, block, gathered, tcol_ready, y_ready=None, y_stored=None):
    nt, ring = ((NT0, RING0), (NT1, RING1))[layer]
    carrier = e.sem(f"ga{layer}_carrier")
    LAG = 2 + ring

    @block.gpsimd
    def _(pool):
        def gather(j, r):
            pool.wait_ge(tcol_ready, j + 1)
            pool.sem_inc(carrier, 1)
            pool.indirect_dma_start(out=e.xg[:, r, :], out_offset=None, in_=e.xn[layer],
                                    in_offset=bass.IndirectOffsetOnAxis(ap=e.tcol[:, r:r + 1], axis=0)).then_inc(gathered[r], 16)

        def scatter(j, r):
            if layer == 1 or (isinstance(j, int) and j < 0):
                return
            pool.wait_ge(y_ready, j + 1)
            pool.sem_inc(carrier, 1)
            if not (isinstance(j, int) and j == 0):
                pool.wait_ge(y_stored, j * 16)
                pool.sem_inc(carrier, 1)
            pool.indirect_dma_start(out=e.y[layer], out_offset=bass.IndirectOffsetOnAxis(ap=e.rcol[:, r:r + 1], axis=0),
                                    in_=e.ysb[:, r, :], in_offset=None).then_inc(y_stored, 16)

        head = LAG + 1 + ring - (LAG + 1) % ring
        for j in range(head):
            gather(j, j % ring)
            scatter(j - LAG, (j - LAG) % ring)
        turns = (nt - head) // ring
        with pool.Fori(0, turns) as t:
            for u in range(ring):
                gather(t * ring + (head + u), u)
                scatter(t * ring + (head + u - LAG), (u - LAG) % ring)
        for j in range(head + turns * ring, nt + LAG):
            if j < nt:
                gather(j, j % ring)
            scatter(j - LAG, (j - LAG) % ring)
        if layer == 0:
            pool.wait_ge(y_stored, 16 * nt)


def token_column(e, dve, j, r, ready):
    e.nc.vector.tensor_copy(e.tcol[:, r:r + 1], e.token_u[:, bass.ds(j, 1)]).then_inc(ready, 1)


def experts0(e):
    nc, ps, sem = e.nc, e.ps, e.sem
    gathered = [sem(f"e0_gathered{r}") for r in range(RING0)]
    x_turned, xT_ready = sem("e0_x_turned"), sem("e0_xT_ready")
    h_raw, h_copied, h_turned, hT_ready = sem("e0_h_raw"), sem("e0_h_copied"), sem("e0_h_turned"), sem("e0_hT_ready")
    y_raw, y_ready, tcol_ready = sem("e0_y_raw"), sem("e0_y_ready"), sem("e0_tcol_ready")
    y_stored = sem("e0_y_stored")
    xT = e.carve(0, [DK, P], base=e.scr)
    h = e.carve(DK * P * 4, [H0], base=e.scr)
    hT = e.carve(DK * P * 4 + H0 * 4, [HK0, P], base=e.scr)
    HH = H0 // HB
    HALF = HK0 // HH
    XB, HB0, TB, YB = 0, 1, 3, 5

    with nc.Block() as block:
        move_tiles(e, 0, block, gathered, tcol_ready, y_ready, y_stored)

        @block.tensor
        def _(pe):
            pe.wait_ge(e.w0_in, 16 * (2 * E0 + 1))

            def turn_x(j, r, turn):
                pe.wait_ge(gathered[r], turn * 16 + 16)
                for k in range(DK):
                    last = nc.tensor.transpose(ps[:, XB, k * P:(k + 1) * P], e.xg[:, r, k * P:(k + 1) * P], e.ident[:])
                last.then_inc(x_turned, 1)

            def down(j):
                ex = pe.value_load(e.expert[0:1, bass.ds(j, 1)], min_val=0, max_val=E0 - 1)
                if not (isinstance(j, int) and j == 0):
                    pe.wait_ge(y_ready, j)
                for k in range(HK0):
                    pe.wait_ge(hT_ready, j * HK0 + k + 1)
                    last = nc.tensor.matmul(ps[:, YB, 0:D], hT[:, k, :], e.w2[:, ex, k, :], start=(k == 0), stop=(k == HK0 - 1))
                last.then_inc(y_raw, 1)

            def body(j, r, turn, first, last):
                ex = pe.value_load(e.expert[0:1, bass.ds(j, 1)], min_val=0, max_val=E0 - 1)
                pe.wait_ge(xT_ready, j + 1)
                for n in range(HH):
                    for k in range(DK):
                        ins = nc.tensor.matmul(ps[:, HB0 + n, :], xT[:, k, :], e.w1[:, ex, k, n * HB:(n + 1) * HB], start=(k == 0), stop=(k == DK - 1))
                    ins.then_inc(h_raw, 1)
                if not last:
                    turn_x(j + 1, (r + 1) % RING0, turn + (r + 1) // RING0)
                if not first:
                    down(j - 1)
                for n in range(HH):
                    pe.wait_ge(h_copied, j * HH + n + 1)
                    for k in range(n * HALF, (n + 1) * HALF):
                        ins = nc.tensor.transpose(ps[:, TB + n, (k % HALF) * P:(k % HALF + 1) * P], h[:, k * P:(k + 1) * P], e.ident[:])
                    ins.then_inc(h_turned, 1)

            turn_x(0, 0, 0)
            tile_loop(pe, NT0, RING0, body)
            down(NT0 - 1)

        @block.scalar
        def _(act):
            def copy_x(j):
                act.wait_ge(x_turned, j + 1)
                nc.scalar.activation(xT.rearrange("p k t -> p (k t)"), ps[:, XB, 0:D], ACT.Copy).then_inc(xT_ready, 1)

            def body(j, r, turn, first, last):
                for n in range(HH):
                    act.wait_ge(h_raw, j * HH + n + 1)
                    nc.scalar.activation(h[:, n * HB:(n + 1) * HB], ps[:, HB0 + n, :], ACT.Copy).then_inc(h_copied, 1)
                if not last:
                    copy_x(j + 1)

            copy_x(0)
            tile_loop(act, NT0, RING0, body)

        @block.vector
        def _(dve):
            v = nc.vector

            def out(j, r, turn, fresh):
                ex = dve.value_load(e.expert[0:1, bass.ds(j, 1)], min_val=0, max_val=E0 - 1)
                if not fresh:
                    dve.wait_ge(y_stored, j * 16 - (RING0 - 1) * 16)
                v.tensor_copy(e.rcol[:, r:r + 1], e.row_u[:, bass.ds(j, 1)])
                dve.wait_ge(y_raw, j + 1)
                v.tensor_tensor(e.ysb[:, r, :], ps[:, YB, 0:D], e.b2bc[:, ex, :], ALU.add).then_inc(y_ready, 1)

            def next_column(j, r):
                if not isinstance(j, int) or j + RING0 < NT0:
                    dve.wait_ge(x_turned, j + 1)
                    token_column(e, dve, j + RING0, r, tcol_ready)

            def body(j, r, turn, first, last):
                if not first:
                    out(j - 1, (r - 1) % RING0, turn if r else turn - 1, isinstance(j, int) and j <= RING0)
                ex = dve.value_load(e.expert[0:1, bass.ds(j, 1)], min_val=0, max_val=E0 - 1)
                for k in range(HK0):
                    if k % HALF == 0:
                        dve.wait_ge(h_turned, j * HH + k // HALF + 1)
                    v.tensor_scalar(hT[:, k, :], ps[:, TB + k // HALF, (k % HALF) * P:(k % HALF + 1) * P],
                                    e.b1T[:, bass.ds(ex * HK0 + k, 1)], 0.0, ALU.add, ALU.max).then_inc(hT_ready, 1)
                if not last:
                    next_column(j + 1, (r + 1) % RING0)

            for j in range(RING0):
                token_column(e, dve, j, j, tcol_ready)
            next_column(0, 0)
            tile_loop(dve, NT0, RING0, body)
            out(NT0 - 1, (NT0 - 1) % RING0, (NT0 - 1) // RING0, False)


def experts1(e):
    nc, ps, sem = e.nc, e.ps, e.sem
    gathered = [sem(f"e1_gathered{r}") for r in range(RING1)]
    x_turned, xT_ready = sem("e1_x_turned"), sem("e1_xT_ready")
    gu_raw, silu_ready, a_ready, a_turned, aT_ready = (sem("e1_" + n) for n in ("gu_raw", "silu_ready", "a_ready", "a_turned", "aT_ready"))
    y_raw, y_ready, tcol_ready = sem("e1_y_raw"), sem("e1_y_ready"), sem("e1_tcol_ready")
    y_stored = [sem(f"e1_y_stored{r}") for r in range(RING1)]
    o = 0
    xT = e.carve(o, [2, DK, P], base=e.scr); o += 2 * DK * P * 4
    silu = e.carve(o, [2, I1], base=e.scr); o += 2 * I1 * 4
    act_in = e.carve(o, [2, I1], base=e.scr); o += 2 * I1 * 4
    aT = e.carve(o, [2, 2, P], base=e.scr); o += 2 * 2 * P * 4
    assert o <= E1_SCRATCH
    XB, GB, TB, YB = 0, 2, 4, 6

    def at_least(j, n):
        return not isinstance(j, int) or j >= n

    def before(j, n):
        return not isinstance(j, int) or j < n

    with nc.Block() as block:
        move_tiles(e, 1, block, gathered, tcol_ready)

        @block.tensor
        def _(pe):
            def turn_x(j, r, turn):
                pe.wait_ge(gathered[r], turn * 16 + 16)
                for k in range(DK):
                    last = nc.tensor.transpose(ps[:, XB + r % 2, k * P:(k + 1) * P], e.xg[:, r, k * P:(k + 1) * P], e.ident[:])
                last.then_inc(x_turned, 1)

            def gate_up(j, r, ex):
                pe.wait_ge(xT_ready, j + 1)
                for k in range(DK):
                    ins = nc.tensor.matmul(ps[:, GB + r % 2, 0:2 * I1], xT[:, r % 2, k, :], e.w13[:, ex, k, :], start=(k == 0), stop=(k == DK - 1))
                ins.then_inc(gu_raw, 1)

            def turn_hidden(j, r):
                pe.wait_ge(a_ready, j + 1)
                for k in range(2):
                    ins = nc.tensor.transpose(ps[0:IH, TB + r % 2, k * P:(k + 1) * P], act_in[:, r % 2, k * IH:(k + 1) * IH], e.ident[:])
                ins.then_inc(a_turned, 1)

            def down(j, r):
                ex = expert(j)
                if at_least(j, 2):
                    pe.wait_ge(y_ready, j - 1)
                pe.wait_ge(aT_ready, j + 1)
                for k in range(2):
                    last = nc.tensor.matmul(ps[:, YB + r % 2, 0:D], aT[0:IH, r % 2, k, :], e.w2b[0:IH, ex, k, :], start=(k == 0), stop=(k == 1))
                last.then_inc(y_raw, 1)

            def expert(j):
                return pe.value_load(e.expert[0:1, bass.ds(j, 1)], min_val=0, max_val=E1 - 1)

            def body(j, r, turn, first, last):
                gate_up(j, r, expert(j))
                if at_least(j, 1):
                    turn_hidden(j - 1, (r - 1) % RING1)
                if isinstance(j, int) and j == 2:
                    pe.wait_ge(e.w2_in, 16 * E1)
                if at_least(j, 2):
                    down(j - 2, (r - 2) % RING1)
                if before(j, NT1 - 2):
                    turn_x(j + 2, (r + 2) % RING1, turn + (r + 2) // RING1)

            for j in range(2):
                turn_x(j, j, 0)
            pe.wait_ge(e.w13_early, 32 * EARLY // 2)
            pe.wait_ge(e.w13_in, 32 * (E1 - EARLY))
            tile_loop(pe, NT1, RING1, body)
            turn_hidden(NT1 - 1, (NT1 - 1) % RING1)
            for j in (NT1 - 2, NT1 - 1):
                down(j, j % RING1)

        @block.scalar
        def _(act):
            def copy_x(j, r):
                act.wait_ge(x_turned, j + 1)
                nc.scalar.activation(xT[:, r % 2].rearrange("p k t -> p (k t)"), ps[:, XB + r % 2, 0:D], ACT.Copy).then_inc(xT_ready, 1)

            def copy_hidden(j, r):
                act.wait_ge(a_turned, j + 1)
                if at_least(j, 2):
                    act.wait_ge(y_raw, j - 1)
                nc.scalar.activation(aT[0:IH, r % 2].rearrange("p k t -> p (k t)"), ps[0:IH, TB + r % 2, 0:2 * P], ACT.Copy).then_inc(aT_ready, 1)

            def body(j, r, turn, first, last):
                act.wait_ge(gu_raw, j + 1)
                if at_least(j, 2):
                    act.wait_ge(a_ready, j - 1)
                nc.scalar.activation(silu[:, r % 2], ps[:, GB + r % 2, 0:I1], ACT.Silu).then_inc(silu_ready, 1)
                if at_least(j, 1):
                    copy_hidden(j - 1, (r - 1) % RING1)
                if before(j, NT1 - 2):
                    copy_x(j + 2, (r + 2) % RING1)

            for j in range(2):
                copy_x(j, j)
            tile_loop(act, NT1, RING1, body)
            copy_hidden(NT1 - 1, (NT1 - 1) % RING1)

        @block.vector
        def _(dve):
            v = nc.vector

            def out(j, r, turn):
                if at_least(j, RING1):
                    dve.wait_ge(y_stored[r], turn * 16)
                dve.wait_ge(y_raw, j + 1)
                v.tensor_copy(e.ysb[:, r, :], ps[:, YB + r % 2, 0:D]).then_inc(y_ready, 1)

            def next_column(j, r):
                if not isinstance(j, int) or j + RING1 < NT1:
                    dve.wait_ge(x_turned, j + 1)
                    token_column(e, dve, j + RING1, r, tcol_ready)

            def body(j, r, turn, first, last):
                dve.wait_ge(silu_ready, j + 1)
                if at_least(j, 2):
                    dve.wait_ge(a_turned, j - 1)
                v.tensor_tensor(act_in[:, r % 2], ps[:, GB + r % 2, I1:2 * I1], silu[:, r % 2], ALU.mult).then_inc(a_ready, 1)
                if at_least(j, 2):
                    out(j - 2, (r - 2) % RING1, turn if r >= 2 else turn - 1)
                if not last:
                    next_column(j + 1, (r + 1) % RING1)

            for j in range(RING1):
                token_column(e, dve, j, j, tcol_ready)
            next_column(0, 0)
            tile_loop(dve, NT1, RING1, body)
            for j in (NT1 - 2, NT1 - 1):
                out(j, j % RING1, j // RING1)

        @block.sync
        def _(sp):
            def body(j, r, turn, first, last):
                sp.wait_ge(y_ready, j + 1)
                sp.dma_start(e.y[1][bass.ds(j * P, P), :], e.ysb[:, r, :]).then_inc(y_stored[r], 16)

            tile_loop(sp, NT1, RING1, body)
            for r in range(RING1):
                sp.wait_ge(y_stored[r], 16 * ((NT1 - 1 - r) // RING1 + 1))


def combine(e, layer):
    nc, sem = e.nc, e.sem
    kk = (K0, K1)[layer]
    nm = f"co{layer}_"
    U = 4
    got = [sem(nm + f"got{u}") for u in range(U)]
    step, added, stored = sem(nm + "step"), sem(nm + "added"), sem(nm + "stored")
    yg = e.carve(0, [U, kk, D], base=(e.scr, e.arena)[layer])
    TURNS = NTILE // U
    loads = 16 if layer == 0 else 16 * kk
    last_layer = layer == 1

    with nc.Block() as block:
        if layer == 0:
            @block.sync
            def _(sp):
                y = e.y[0][0:NTOK * kk, :].rearrange("(k i p) d -> p i k d", k=kk, p=P)

                def load(t):
                    for u in range(U):
                        i = t * U + u
                        if not isinstance(t, int):
                            sp.wait_ge(added, i - (U - 1))
                        sp.dma_start(yg[:, u, :, :], y[:, i, :, :]).then_inc(got[u], 16)

                load(0)
                with sp.Fori(1, TURNS) as t:
                    load(t)
        else:
            @block.gpsimd
            def _(pool):
                for i in range(NTILE):
                    u = i % U
                    if i >= U:
                        pool.wait_ge(added, i - (U - 1))
                    for k in range(kk):
                        pool.indirect_dma_start(out=yg[:, u, k, :], out_offset=None, in_=e.y[1],
                                                in_offset=bass.IndirectOffsetOnAxis(ap=e.slot_u[:, i, k:k + 1], axis=0)).then_inc(got[u], 16)

        @block.vector
        def _(dve):
            v = nc.vector
            if last_layer:
                ch = Chain(dve, sem(nm + "weight_step"))
                o = U * kk * D * 4
                scores = e.carve(o, [kk, NTILE * E1]); o += kk * NTILE * E1 * 4
                w = e.carve(o, [NTILE, kk]); o += NTILE * kk * 4
                tot = e.carve(o, [NTILE])
                for k in range(kk):
                    ins = v.tensor_tensor(scores[:, k].rearrange("p (i e) -> p i e", e=E1), e.chosen[:, k], e.sig, ALU.mult)
                ch(ins)
                for k in range(kk):
                    ins = v.tensor_reduce(w[:, :, k], scores[:, k].rearrange("p (i e) -> p i e", e=E1), AX.X, ALU.add)
                ch(ins)
                ch(v.tensor_reduce(tot, w, AX.X, ALU.add))
                ch(v.reciprocal(tot, tot))
                ch(v.scalar_tensor_tensor(e.gate[:], w, e.tg[:, 3:4], tot.unsqueeze(2).broadcast_to([P, NTILE, kk]), ALU.mult, ALU.mult))
            with dve.Fori(0, TURNS) as t:
                for pair in range(0, U, 2):
                    for k in range(kk):
                        for u in (pair, pair + 1):
                            i = t * U + u
                            if k == 0:
                                dve.wait_ge(got[u], t * loads + loads)
                            else:
                                dve.wait_ge(step, t * (U * (kk - 1)) + (pair * (kk - 1) + (k - 1) * 2 + (u - pair) + 1))
                            v.scalar_tensor_tensor(e.x[:, i, :], yg[:, u, k, :], e.gate[:, i, k:k + 1], e.x[:, i, :],
                                                   ALU.mult, ALU.add).then_inc(step if k < kk - 1 else added, 1)
                    if not last_layer:
                        for u in (pair, pair + 1):
                            i = t * U + u
                            dve.wait_ge(added, i + 1)
                            v.bn_stats(e.stats[:, i, :], e.x[:, i, :])

        if last_layer:
            @block.scalar
            def _(act):
                o = e.out.rearrange("b (t p) d -> p (b t) d", p=P)
                with act.Fori(0, NTILE) as i:
                    act.wait_ge(added, i + 1)
                    act.dma_start(o[:, i, :], e.x[:, i, :]).then_inc(stored, 16)
                act.wait_ge(stored, 16 * NTILE)


def attention_buffers(e):
    def place(start, end):
        at = [start]

        def buf(shape, dt=F32):
            got = e.carve(at[0], shape, dt)
            at[0] += int(np.prod(shape)) * (2 if dt in (BF16, F16) else 4)
            assert at[0] <= end, (at[0], end)
            return got

        return buf

    k_at = TOP - GH * (KEYS + 1) * 2
    assert k_at >= e.free0
    q_aug0 = place(e.b2_at, e.wqkv_at)([2, GH, HB], BF16)
    k_aug0 = place(k_at, TOP)([GH, KEYS + 1], BF16)
    v_at = ATT0 + B * MT * D * 4
    e.v_all = place(ATT0, v_at)([B, MT, D])
    buf = place(v_at, e.b2_at)
    e.xn_a = buf([4, D]); e.xT_a = buf([2, DK, HB]); e.parts = [buf([4, 3, HB], BF16), e.carve(0, [4, 3, HB], BF16, base=e.scr)]; e.left = buf([4, HB])
    buf = place(v_at, e.b2_at)
    e.q_aug = [q_aug0, buf([2, GH, HB], BF16)]
    e.k_aug = [k_aug0, buf([GH, KEYS + 1], BF16)]
    prob1 = buf([GH, HB])
    e.v_g = [buf([MT, GH, HD + 1]) for _ in range(2)]
    e.oT = buf([HB])
    buf = place(e.wqkv_at, k_at)
    e.prob = [buf([GH, HB]), prob1]
    e.mx = buf([2 * GH, TPB // 2, 3]).rearrange("p (c h) t k -> p c h t k", c=2); e.row_max = buf([GH, TPB // 2]); e.neg_all = buf([P], BF16); e.rest = buf([GH, TPB // 2]); e.negT = buf([P], BF16)
    e.neg = e.neg_all[:, 0:3 * GH * TPB // 2].rearrange("p (n h t) -> p n h t", n=3, h=GH)
    e.rec = buf([TPB // 2, GH])
    e.sums = buf([TPB // 2, GH, HD + 1])
    e.att = e.carve(0, [NTILE, D], base=e.scr)


def project_qkv(e):
    nc, ps, sem, a = e.nc, e.ps, e.sem, e.a
    step, var_ready, std_ready, shift_ready = (sem("qkv_" + n) for n in ("step", "var", "std", "shift"))
    xn_ready, xT_raw, xT_ready, v_raw, v_done = (sem("qkv_" + n) for n in ("xn_ready", "xT_raw", "xT_ready", "v_raw", "v_done"))
    unit_raw, part0, left1, part1, unit_done = (sem("qkv_" + n) for n in ("unit_raw", "part0", "left1", "part1", "unit_done"))
    stored = e.qkv_stored = [[sem(f"qkv_stored{n}_{u}") for u in range(4)] for n in range(2)]
    e.loaded = [sem(f"at_loaded{u}") for u in range(2)]
    e.q2_loaded = [sem(f"at_q2_loaded{u}") for u in range(2)]
    ones_set = sem("qkv_ones_set")
    e.unit_done = unit_done
    U = 4
    CH = NTOK // HB
    kp = e.kp.rearrange("c (k p) b t -> k p b c t", p=P)
    SCALE = (float(HD) ** -0.5, 1.0)
    XB, VB, UB = 0, 2, 4

    with nc.Block() as block:
        @block.gpsimd
        def _(pool):
            nc.gpsimd.memset(e.k_aug[0][QROWS:AROWS, :, :], 1.0).then_inc(ones_set, 1)
            pool.wait_ge(ones_set, 1)
            for ex in range(0, EARLY, 2):
                load_w13(e, pool, ex, e.w13_early, 2)

        @block.sync
        def _(sp):
            for n in range(4):
                sp.wait_ge(unit_done, n + 1)
                sp.dma_start(kp[n % DK, :, n // DK, :, 0:CL], e.parts[1][:, n, :, 0:CL]).then_inc(stored[1][n], 16)
            for c in range(CH - 1):
                store_chunk(e, sp, c)
                if c * HB == S:
                    for n in range(4):
                        sp.wait_ge(stored[(c - 1) % 2][n], 16 * ((c + 1) // 2 + 1))
                    load_group(e, sp, 0, 0)

        @block.tensor
        def _(pe):
            for n in range(4):
                nc.tensor.transpose(ps[:, UB + n, 0:CL], e.ctx[:, n // DK, (n % DK) * P:(n % DK + 1) * P], e.ident[0:CL, 0:CL]).then_inc(unit_raw, 1)

            def turn(c):
                for u in range(U):
                    i = c * U + u
                    pe.wait_ge(xn_ready, i + 1)
                    if i >= 2:
                        pe.wait_ge(xT_ready, i - 1)
                    for k in range(DK):
                        last = nc.tensor.transpose(ps[:, XB + i % 2, k * P:(k + 1) * P], e.xn_a[:, u, k * P:(k + 1) * P], e.ident[:])
                    last.then_inc(xT_raw, 1)

            turn(0)
            for c in range(CH):
                if 0 < c < CH - 1:
                    turn(c + 1)
                for u in range(U):
                    i = c * U + u
                    pe.wait_ge(xT_ready, i + 1)
                    if i >= 2:
                        pe.wait_ge(v_done, i - 1)
                    for k in range(DK):
                        last = nc.tensor.matmul(ps[:, VB + i % 2, 0:D], e.xT_a[:, c % 2, k, u * P:(u + 1) * P], e.wqkvT[:, k, 2 * D:3 * D], start=(k == 0), stop=(k == DK - 1))
                    last.then_inc(v_raw, 1)
                if c == 0:
                    turn(1)
                for n in range(4):
                    pe.wait_ge(left1, c * 4 + n + 1)
                    for k in range(DK):
                        last = nc.tensor.matmul(ps[:, UB + n, :], e.wqkvT[:, k, n * P:(n + 1) * P], e.xT_a[:, c % 2, k, :], start=(k == 0), stop=(k == DK - 1))
                    last.then_inc(unit_raw, 1)

        @block.scalar
        def _(act):
            act.wait_ge(var_ready, 1)
            nc.scalar.activation(e.std[:], e.ve[:], ACT.Sqrt).then_inc(std_ready, 1)

            def norm(c):
                for u in range(U):
                    i = c * U + u
                    if c > 0:
                        act.wait_ge(xT_raw, i - U + 1)
                    nc.scalar.activation(e.xn_a[:, u, :], e.x[:, i, :], ACT.Identity, scale=e.rstd[:, i:i + 1], bias=e.shift[:, i:i + 1]).then_inc(xn_ready, 1)

            def copy(c):
                for u in range(U):
                    i = c * U + u
                    act.wait_ge(xT_raw, i + 1)
                    nc.scalar.activation(e.xT_a[:, c % 2, :, u * P:(u + 1) * P], ps[:, XB + i % 2, 0:D].rearrange("p (k t) -> p k t", k=DK), ACT.Copy).then_inc(xT_ready, 1)

            def first_parts(c, w):
                for n in range(4):
                    i = (c + 1) * 4 + n
                    act.wait_ge(unit_raw, i + 1)
                    if c > 0:
                        act.wait_ge(stored[c % 2][n], (c + 1) // 2 * 16)
                    nc.scalar.activation(e.parts[c % 2][:, n, 0, 0:w], ps[:, UB + n, 0:w], ACT.Copy, scale=SCALE[n // DK] if c >= 0 else 1.0).then_inc(part0, 1)

            def second_parts(c, w):
                for n in range(4):
                    act.wait_ge(left1, (c + 1) * 4 + n + 1)
                    nc.scalar.activation(e.parts[c % 2][:, n, 1, 0:w], e.left[:, n, 0:w], ACT.Copy).then_inc(part1, 1)

            act.wait_ge(shift_ready, 1)
            norm(0)
            copy(0)
            first_parts(-1, CL)
            second_parts(-1, CL)
            norm(1)
            copy(1)
            for c in range(CH):
                if c + 2 < CH:
                    norm(c + 2)
                first_parts(c, HB)
                if c + 2 < CH:
                    copy(c + 2)
                second_parts(c, HB)

        @block.vector
        def _(dve):
            v = nc.vector
            ch = Chain(dve, step)
            moments(ch, nc, e.stats, D, e.mean[:], e.var[:], e.ve[:], [e.tmp[:, n, :] for n in range(4)], LN_EPS)
            v.engine_nop().then_inc(var_ready, 1)
            dve.wait_ge(std_ready, 1)
            ch(v.reciprocal(e.rstd[:], e.std[:]))
            v.scalar_tensor_tensor(e.shift[:], e.mean[:], -1.0, e.rstd[:], ALU.mult, ALU.mult).then_inc(shift_ready, 1)
            for b in range(B):
                v.tensor_copy(e.v_all[0:CL, b, 0, :], e.ctx[:, b, D:2 * D])

            def left(c, w):
                for n in range(4):
                    dve.wait_ge(part0, (c + 1) * 4 + n + 1)
                    if c >= 0:
                        dve.wait_ge(unit_done, c * 4 + n + 1)
                    v.scalar_tensor_tensor(e.left[:, n, 0:w], ps[:, UB + n, 0:w], SCALE[n // DK] if c >= 0 else 1.0, e.parts[c % 2][:, n, 0, 0:w],
                                           ALU.mult, ALU.subtract).then_inc(left1, 1)

            def third_parts(c, w):
                for n in range(4):
                    dve.wait_ge(part1, (c + 1) * 4 + n + 1)
                    v.tensor_tensor(e.parts[c % 2][:, n, 2, 0:w], e.left[:, n, 0:w], e.parts[c % 2][:, n, 1, 0:w], ALU.subtract).then_inc(unit_done, 1)

            def values(c):
                for u in range(U):
                    i = c * U + u
                    dve.wait_ge(v_raw, i + 1)
                    v.tensor_copy(e.v_all[:, i // TPB, 1 + i % TPB, :], ps[:, VB + i % 2, 0:D]).then_inc(v_done, 1)

            values(0)
            left(-1, CL)
            third_parts(-1, CL)
            for c in range(CH):
                left(c, HB)
                if c + 1 < CH:
                    values(c + 1)
                third_parts(c, HB)


def store_chunk(e, sp, c):
    qp = e.qp.rearrange("c (k p) t -> k p c t", p=P)
    kp = e.kp.rearrange("c (k p) b t -> k p b c t", p=P)
    b, t0 = divmod(c * HB, S)
    for n in range(4):
        sp.wait_ge(e.unit_done, (c + 1) * 4 + n + 1)
        dst = qp[n, :, :, c * HB:(c + 1) * HB] if n < DK else kp[n - DK, :, b, :, CL + t0:CL + t0 + HB]
        sp.dma_start(dst, e.parts[c % 2][:, n, :, :]).then_inc(e.qkv_stored[c % 2][n], 16)


def batch_of(g):
    return g // (NGRP // B), g % (NGRP // B)


def load_group(e, sp, g, u):
    qv = e.qp.rearrange("c (g h r) t -> c g r h t", h=GH, r=HD)
    kv = e.kp.rearrange("c (g h r) b t -> c g r h b t", h=GH, r=HD)
    b, gg = batch_of(g)
    for n, (cq, ck) in enumerate(zip(QB, KB)):
        rows = slice(n * HD, (n + 1) * HD)
        sp.dma_start(e.q_aug[u][rows, 0, :, :], qv[cq, gg, :, :, bass.ds(b * S, HB)]).then_inc(e.loaded[u], 16)
        sp.dma_start(e.k_aug[u][rows, :, 0:KEYS], kv[ck, gg, :, :, b, :]).then_inc(e.loaded[u], 16)
    for n, cq in enumerate(QB):
        sp.dma_start(e.q_aug[u][n * HD:(n + 1) * HD, 1, :, :], qv[cq, gg, :, :, bass.ds(b * S + HB, HB)]).then_inc(e.q2_loaded[u], 16)


def load_w2(e, eng, ex):
    eng.dma_start(e.w2b[0:IH, ex, :, :], e.a["L1_ffn_w2"][ex].rearrange("(k p) d -> p k d", p=IH)).then_inc(e.w2_in, 16)


def load_w13(e, eng, ex, loaded, n=1):
    for at, name in ((0, "L1_ffn_w1"), (I1, "L1_ffn_w3")):
        eng.dma_start(e.w13[:, ex:ex + n, :, at:at + I1], e.a[name][ex:ex + n].rearrange("e (k p) i -> p e k i", p=P)).then_inc(loaded, 16)


STEPS = 2 * MT
HT = TPB // 2
MAXES = 2 * GH * HT
LATE, NEXT, AHEAD = 0, 1, 2
HALF_AT, PREV_AT = MT + 1, 1
INVERT = 3
SPREAD = (2, 3, 4, 4, 3, 4, 3, 4, 4, 3, 3, 4, 4, 3, 4, 4, 4, 4)
SPLIT_AT = {LATE: 5, NEXT: 14}
BEFORE = 3 * GH
SPREAD_FIRST = (3, 3, 3, 3, 4, 4) + (4,) * 12
SPLIT_AT_FIRST = {LATE: 6, NEXT: 14}


def attend(e):
    nc, ps, sem = e.nc, e.ps, e.sem
    loaded, q2_loaded = e.loaded, e.q2_loaded
    max_in = [sem(f"at_max_in{c}") for c in range(2)]
    v_ready, ones_set, psum_set = sem("at_v_ready"), sem("at_ones_set"), sem("at_psum_set")
    max_raw, max_done, misc_raw, misc_done = (sem("at_" + n) for n in ("max_raw", "max_done", "misc_raw", "misc_done"))
    rows_max, neg_ready, negT_ready = sem("at_rows_max"), sem("at_neg_ready"), sem("at_negT_ready")
    step, carrier = sem("at_step"), sem("at_carrier")
    s_raw, p_ready, pv_done = sem("at_s_raw"), sem("at_p_ready"), sem("at_pv_done")
    half_out, half_inverted, half_done = (sem("at_half_" + n) for n in ("out", "inverted", "done"))
    MAXB, NMAXB, SB, NSB, AB, MB = 0, 3, 3, 3, 6, 7
    PARTS = len(QB)
    TURN_FIRST = MAXES + BEFORE // 2 - 1
    PROLOGUE, PER_GROUP = HT + BEFORE // (2 * GH) + 1, TPB + 4

    def misc_before(g):
        if isinstance(g, int) and g == 0:
            return PROLOGUE
        return g * PER_GROUP + (HT + HT // 2)

    def maxima_before(g):
        if isinstance(g, int) and g == 0:
            return MAXES + BEFORE
        return g * (2 * MAXES) + (MAXES + MAXES // 2)

    def groups(eng, body):
        body(0, 0, True, False)
        with eng.Fori(0, (NGRP - 2) // 2) as t:
            for u in range(2):
                body(t * 2 + (1 + u), (1 + u) % 2, False, False)
        body(NGRP - 1, (NGRP - 1) % 2, False, True)

    def key_rows(mt):
        return (0, CL) if mt == 0 else (CL + (mt - 1) * P, P)

    def half(which, g, u):
        return (g, u, 1) if which == LATE else (g + 1, 1 - u, which - NEXT)

    def maxima_at(s, first, last):
        spread = SPREAD_FIRST if first else SPREAD
        late = MAXES - BEFORE if first else MAXES // 2
        for pos in range(sum(spread[:s]), sum(spread[:s + 1])):
            which = LATE if pos < late else NEXT if pos < late + MAXES else AHEAD
            if not (last and which != LATE):
                yield pos, which, pos + MAXES - late if which == LATE else pos - late - (which - NEXT) * MAXES

    def split_at(s, first, last):
        return [which for which, at in (SPLIT_AT_FIRST if first else SPLIT_AT).items() if at == s and not (last and which != LATE)]

    def odds_at(s, first, last):
        for which in split_at(s - 1, first, last):
            yield "turn", which, 0
        for pos, which, n in maxima_at(s, first, last):
            if n % (2 * GH) == 2 * GH - 1:
                yield "ctx", which, n // (2 * GH)
        if s == PREV_AT and not first:
            yield "half", 1, 0
        if s == HALF_AT:
            yield "half", 0, 0

    class Odds:

        def __init__(self):
            self.base, self.n = 0, 0

        def at(self, base):
            self.base, self.n = base, 0

        def next(self):
            self.n += 1
            return self.base + (self.n - 1)

    def projections_stored(eng):
        for n in range(2):
            for unit in range(4):
                eng.wait_ge(e.qkv_stored[n][unit], 16 * (NTOK // HB // 2 + n))

    with nc.Block() as block:
        @block.sync
        def _(sp):
            def maxima(g, u, c):
                sp.wait_ge(negT_ready, g * 2 + (1 + c))
                for n in range(3):
                    sp.dma_start(e.q_aug[u][QROWS + n:QROWS + n + 1, c].rearrange("o h (t n) -> o (h t) n", n=P),
                                 e.negT[n * GH * HT:(n + 1) * GH * HT, :]).then_inc(max_in[c], 16)

            store_chunk(e, sp, NTOK // HB - 1)
            projections_stored(sp)
            maxima(0, 0, 0)

            def body(g, u, first, last):
                if not last:
                    if not first:
                        sp.wait_ge(s_raw, g * (GH * STEPS))
                    load_group(e, sp, g + 1, 1 - u)
                maxima(g, u, 1)
                if not last:
                    maxima(g + 1, 1 - u, 0)

            groups(sp, body)

        @block.gpsimd
        def _(pool):
            g_ = nc.gpsimd
            ch = Chain(pool, step, carrier)
            for u in range(2):
                ch(g_.memset(e.v_g[u][:, :, :, HD:HD + 1], 1.0))
            ch(g_.memset(e.neg_all, 0.0))

            def values(g, u):
                b, gg = batch_of(g)
                cols = e.v_all[:, b, :, bass.ds(gg * (GH * HD), GH * HD)]
                g_.tensor_copy(e.v_g[u][0:CL, 0, :, 0:HD], cols[0:CL, 0, :].rearrange("p (h r) -> p h r", h=GH)).then_inc(v_ready, 1)
                for mt in range(1, MT):
                    pool.wait_ge(v_ready, g * MT + mt)
                    pool.sem_inc(carrier, 1)
                    g_.tensor_copy(e.v_g[u][:, mt, :, 0:HD], cols[:, mt, :].rearrange("p (h r) -> p h r", h=GH)).then_inc(v_ready, 1)

            def negate(g, c):
                pool.wait_ge(rows_max, g * 2 + (1 + c))
                pool.sem_inc(carrier, 1)
                ch(g_.tensor_scalar(e.rest, e.row_max, -1.0, None, ALU.mult))
                ch(g_.tensor_scalar(e.neg[:, 0], e.rest, 1.0, None, ALU.mult))
                ch(g_.tensor_tensor(e.rest, e.rest, e.neg[:, 0], ALU.subtract))
                ch(g_.tensor_scalar(e.neg[:, 1], e.rest, 1.0, None, ALU.mult))
                g_.tensor_tensor(e.neg[:, 2], e.rest, e.neg[:, 1], ALU.subtract).then_inc(neg_ready, 1)

            def normalise(b, gg, c, count):
                pool.wait_ge(half_inverted, count)
                pool.sem_inc(carrier, 1)
                for t in range(HT):
                    ins = g_.tensor_tensor(e.att[:, b * TPB + (c * HT + t), bass.ds(gg * (GH * HD), GH * HD)].rearrange("p (h r) -> p h r", h=GH),
                                           e.sums[:, t, :, 0:HD], e.rec[:, t, :].unsqueeze(2).broadcast_to([P, GH, HD]), ALU.mult)
                    if t < HT - 1:
                        ch(ins)
                ins.then_inc(half_done, 1)

            values(0, 0)
            projections_stored(pool)
            pool.wait_ge(v_ready, MT)
            g_.memset(e.k_aug[1][QROWS:AROWS, :, :], 1.0).then_inc(ones_set, 1)
            pool.wait_ge(ones_set, 1)
            negate(0, 0)

            def body(g, u, first, last):
                if not last:
                    if not first:
                        pool.wait_ge(pv_done, g * STEPS)
                        pool.sem_inc(carrier, 1)
                    values(g + 1, 1 - u)
                if not first:
                    normalise(*batch_of(g - 1), 1, g * 2)
                negate(g, 1)
                normalise(*batch_of(g), 0, g * 2 + 1)
                if not last:
                    negate(g + 1, 0)

            body(0, 0, True, False)
            with pool.Fori(0, (NGRP - 2) // 2) as t:
                with ch.turns(t, 2 * (2 * 4 + 2 * (HT - 1)), (NGRP - 2) // 2):
                    for u in range(2):
                        body(t * 2 + (1 + u), (1 + u) % 2, False, False)
            body(NGRP - 1, (NGRP - 1) % 2, False, True)
            normalise(*batch_of(NGRP - 1), 1, NGRP * 2)

        @block.tensor
        def _(pe):
            odds = Odds()

            def odd():
                n = odds.next()
                if not (isinstance(n, int) and n == 0):
                    pe.wait_ge(misc_done, n)

            def maximum(g, u, c, n, pos, before):
                th, k = divmod(n, 2)
                t, h = divmod(th, GH)
                if pos >= NMAXB:
                    pe.wait_ge(max_done, before + (pos - NMAXB + 1))
                elif pos == 0 and not (isinstance(before, int) and before == 0):
                    pe.wait_ge(max_done, before)
                nc.tensor.matmul(ps[:, MAXB + pos % NMAXB, :], e.q_aug[u][0:QROWS, c, h, t * P:(t + 1) * P],
                                 e.k_aug[u][0:QROWS, h, CL + k * HB:CL + (k + 1) * HB], start=True, stop=True).then_inc(max_raw, 1)

            def context_max(u, c, t):
                odd()
                for h in range(GH):
                    ins = nc.tensor.matmul(ps[:, MB, h * CL:(h + 1) * CL], e.q_aug[u][0:QROWS, c, h, t * P:(t + 1) * P],
                                           e.k_aug[u][0:QROWS, h, 0:CL], start=True, stop=True)
                ins.then_inc(misc_raw, 1)

            def turn_maxima(g, c):
                pe.wait_ge(neg_ready, g * 2 + (1 + c))
                odd()
                nc.tensor.transpose(ps[:, MB, 0:P // 2].bitcast(BF16), e.neg_all, e.identb[:]).then_inc(misc_raw, 1)

            def turn_half(count):
                pe.wait_ge(half_out, count)
                odd()
                for t in range(HT):
                    ins = nc.tensor.transpose(ps[:, MB, t * P:(t + 1) * P], e.oT[:, t * P:(t + 1) * P], e.ident[:])
                ins.then_inc(misc_raw, 1)

            def weigh(g, u, s):
                mt = s % MT
                k0, rows = key_rows(mt)
                pe.wait_ge(p_ready, g * (GH * STEPS) + GH * (s + 1))
                if mt == 0 and not (isinstance(g, int) and g == 0 and s == 0):
                    pe.wait_ge(half_out, g * 2 + s // MT)
                for h in range(GH):
                    ins = nc.tensor.matmul(ps[h * 32:h * 32 + HD + 1, AB, :], e.v_g[u][0:rows, mt, h, :], e.prob[s % 2][0:rows, h, :],
                                           start=(mt == 0), stop=(mt == MT - 1))
                ins.then_inc(pv_done, 1)

            def score(g, u, s, h):
                c, mt = divmod(s, MT)
                k0, rows = key_rows(mt)
                n = s * GH + h
                if not (isinstance(g, int) and g == 0 and n < NSB):
                    pe.wait_ge(p_ready, g * (GH * STEPS) + (n - NSB + 1))
                nc.tensor.matmul(ps[0:rows, SB + n % NSB, :], e.k_aug[u][0:AROWS, h, k0:k0 + rows],
                                 e.q_aug[u][0:AROWS, c, h, :], start=True, stop=True).then_inc(s_raw, 1)

            odds.at(0)
            pe.wait_ge(loaded[0], 16 * PARTS * 2)
            for pos in range(MAXES + BEFORE):
                c, n = divmod(pos, MAXES)
                if pos == MAXES:
                    pe.wait_ge(q2_loaded[0], 16 * PARTS)
                maximum(0, 0, c, n, pos, 0)
                if n % (2 * GH) == 2 * GH - 1:
                    context_max(0, c, n // (2 * GH))
                if pos == TURN_FIRST:
                    turn_maxima(0, 0)

            def body(g, u, first, last):
                odds.at(misc_before(g))
                before = maxima_before(g)
                pe.wait_ge(v_ready, g * MT + MT)
                for s in range(STEPS):
                    if s % MT == 0:
                        pe.wait_ge(max_in[s // MT], g * (16 * 3) + 16 * 3)
                    todo = list(maxima_at(s, first, last))
                    skip = 2 if s == 0 and not first else 0

                    def maxima(slot):
                        at = slot - skip
                        for pos, which, n in todo[at:] if slot == GH - 1 else todo[at:at + 1] if at >= 0 else ():
                            hg, hu, c = half(which, g, u)
                            if which == NEXT and n == 0:
                                pe.wait_ge(loaded[hu], next_of(g, u) * (16 * PARTS * 2) + 16 * PARTS * 2)
                            if which == AHEAD and n == 0:
                                pe.wait_ge(q2_loaded[hu], next_of(g, u) * (16 * PARTS) + 16 * PARTS)
                            maximum(hg, hu, c, n, pos, before)

                    score(g, u, s, 0)
                    for what, which, n in odds_at(s, first, last):
                        if what == "turn":
                            hg, hu, c = half(which, g, u)
                            turn_maxima(hg, c)
                    maxima(0)
                    score(g, u, s, 1)
                    maxima(1)
                    if s > 0:
                        weigh(g, u, s - 1)
                    elif not first:
                        weigh(g - 1, 1 - u, STEPS - 1)
                    score(g, u, s, 2)
                    maxima(2)
                    score(g, u, s, 3)
                    maxima(3)
                    for what, which, n in odds_at(s, first, last):
                        if what == "ctx":
                            hg, hu, c = half(which, g, u)
                            context_max(hu, c, n)
                        if what == "half":
                            turn_half(g * 2 + 1 - which)

            pe.wait_ge(ones_set, 1)
            pe.wait_ge(psum_set, 1)
            groups(pe, body)
            weigh(NGRP - 1, (NGRP - 1) % 2, STEPS - 1)
            turn_half(NGRP * 2)

        @block.scalar
        def _(act):
            odds = Odds()

            def out(count):
                act.wait_ge(pv_done, count * MT)
                nc.scalar.activation(e.oT, ps[:, AB, :], ACT.Copy).then_inc(half_out, 1)

            def turned(count):
                act.wait_ge(misc_raw, odds.next() + 1)
                if not (isinstance(count, int) and count == 1):
                    act.wait_ge(half_done, count - 1)
                o = ps[:, MB, :].rearrange("p (t h c) -> p t h c", t=HT, h=GH)
                nc.scalar.activation(e.sums, o[:, :, :, 0:HD + 1], ACT.Copy).then_inc(misc_done, 1)

            def body(g, u, first, last):
                odds.at(misc_before(g))
                for s in range(STEPS):
                    rows = key_rows(s % MT)[1]
                    for h in range(GH):
                        act.wait_ge(s_raw, g * (GH * STEPS) + (s * GH + h + 1))
                        if h == 0 and not (isinstance(g, int) and g == 0 and s < 2):
                            act.wait_ge(pv_done, g * STEPS + (s - 1))
                        nc.scalar.activation(e.prob[s % 2][0:rows, h, :], ps[0:rows, SB + (s * GH + h) % NSB, :], ACT.Exp).then_inc(p_ready, 1)
                        if h == 1 and s == 0 and not first:
                            out(g * 2)
                        if h == 1 and s == MT:
                            out(g * 2 + 1)
                        if h == 1:
                            for what, which, n in odds_at(s - 1, first, last):
                                if what == "half":
                                    turned(g * 2 + 1 - which)
                                else:
                                    odds.next()

            groups(act, body)
            out(NGRP * 2)
            for what, which, n in odds_at(STEPS - 1, False, True):
                odds.next()
            turned(NGRP * 2)

        @block.vector
        def _(dve):
            v = nc.vector
            odds = Odds()
            v.memset(ps[:, AB, :], 0.0).then_inc(psum_set, 1)

            def maximum(c, n, pos, before):
                th, k = divmod(n, 2)
                t, h = divmod(th, GH)
                dve.wait_ge(max_raw, before + (pos + 1))
                v.tensor_reduce(e.mx[:, c, h, t, k:k + 1], ps[:, MAXB + pos % NMAXB, :], AX.X, ALU.max).then_inc(max_done, 1)

            def context_max(c, t):
                dve.wait_ge(misc_raw, odds.next() + 1)
                v.tensor_reduce(e.mx[:, c, :, t, 2], ps[:, MB, 0:GH * CL].rearrange("p (h c) -> p h c", h=GH), AX.X, ALU.max).then_inc(misc_done, 1)

            def row_max(g, c):
                dve.wait_ge(max_done, g * (2 * MAXES) + (c + 1) * MAXES)
                dve.wait_ge(misc_done, odds.base + odds.n)
                if not (isinstance(g, int) and g == 0 and c == 0):
                    dve.wait_ge(neg_ready, g * 2 + c)
                v.tensor_reduce(e.row_max, e.mx[:, c], AX.X, ALU.max).then_inc(rows_max, 1)

            def invert(count, use):
                dve.wait_ge(misc_done, use + 1)
                if not (isinstance(count, int) and count == 1):
                    dve.wait_ge(half_done, count - 1)
                v.reciprocal(e.rec, e.sums[:, :, :, HD]).then_inc(half_inverted, 1)

            def turned(g, c):
                dve.wait_ge(misc_raw, odds.next() + 1)
                if not (isinstance(g, int) and g == 0 and c == 0):
                    dve.wait_ge(max_in[1 - c], g * (16 * 3) + c * (16 * 3))
                v.tensor_copy(e.negT[0:3 * GH * HT, :], ps[0:3 * GH * HT, MB, 0:P // 2].bitcast(BF16)).then_inc(negT_ready, 1)
                v.engine_nop().then_inc(misc_done, 1)

            def body(g, u, first, last):
                odds.at(misc_before(g))
                before = maxima_before(g)
                for s in range(STEPS):
                    order = list(odds_at(s, first, last))
                    todo = list(maxima_at(s, first, last))
                    for which in split_at(s, first, last):
                        hg, _, c = half(which, g, u)
                        row_max(hg, c)
                    for what, which, n in odds_at(s - INVERT, first, last):
                        if what == "half":
                            invert(g * 2 + 1 - which, half_use)
                    for i, (pos, which, n) in enumerate(todo):
                        if i == 1 or len(todo) == 1:
                            for what, which_, n_ in order:
                                if what == "turn":
                                    hg, _, c = half(which_, g, u)
                                    turned(hg, c)
                        maximum(half(which, g, u)[2], n, pos, before)
                    for what, which, n in order:
                        if what == "turn" and not todo:
                            hg, _, c = half(which, g, u)
                            turned(hg, c)
                        if what == "ctx":
                            context_max(half(which, g, u)[2], n)
                        if what == "half":
                            half_use = odds.next()

            odds.at(0)
            for pos in range(MAXES + BEFORE):
                c, n = divmod(pos, MAXES)
                maximum(c, n, pos, 0)
                if n % (2 * GH) == 2 * GH - 1:
                    context_max(c, n // (2 * GH))
                if pos == MAXES - 1:
                    row_max(0, 0)
                if pos == TURN_FIRST:
                    turned(0, 0)
            groups(dve, body)
            invert(NGRP * 2, odds.next())


def next_of(g, u):
    return (g + 1 - (1 - u)) // 2


def project_out(e):
    nc, ps, sem, a = e.nc, e.ps, e.sem, e.a
    aT_raw, aT_ready, o_raw, biased, x_new = (sem("pj_" + n) for n in ("aT_raw", "aT_ready", "o_raw", "biased", "x_new"))
    U = 4
    sums = e.att
    aT = e.ysb[:].rearrange("p u (k t) -> p u k t", k=DK)

    with nc.Block() as block:
        @block.sync
        def _(sp):
            for ex in range(EARLY, E1):
                load_w13(e, sp, ex, e.w13_in)
            for ex in range(W2_TOP):
                load_w2(e, sp, ex)

        @block.tensor
        def _(pe):
            for i in range(NTILE + 2):
                if i < NTILE:
                    if i >= U:
                        pe.wait_ge(aT_ready, i - U + 1)
                    for k in range(DK):
                        last = nc.tensor.transpose(ps[:, i % U, k * P:(k + 1) * P], e.att[:, i, k * P:(k + 1) * P], e.ident[:])
                    last.then_inc(aT_raw, 1)
                if i >= 2:
                    j = i - 2
                    pe.wait_ge(aT_ready, j + 1)
                    if j >= U:
                        pe.wait_ge(biased, j - U + 1)
                    for k in range(DK):
                        last = nc.tensor.matmul(ps[:, U + j % U, 0:D], aT[:, j % U, k, :], e.wprojT[:, k, :], start=(k == 0), stop=(k == DK - 1))
                    last.then_inc(o_raw, 1)

        @block.scalar
        def _(act):
            for i in range(NTILE):
                act.wait_ge(aT_raw, i + 1)
                if i >= U:
                    act.wait_ge(o_raw, i - U + 1)
                nc.scalar.activation(aT[:, i % U, :, :].rearrange("p k t -> p (k t)"), ps[:, i % U, 0:D], ACT.Copy).then_inc(aT_ready, 1)

        @block.vector
        def _(dve):
            v = nc.vector
            for i in range(NTILE + 2):
                if i < NTILE:
                    dve.wait_ge(o_raw, i + 1)
                    v.tensor_tensor(sums[:, i, :], ps[:, U + i % U, 0:D], e.bproj, ALU.add).then_inc(biased, 1)
                if 0 < i <= NTILE:
                    dve.wait_ge(biased, i)
                    v.scalar_tensor_tensor(e.x[:, i - 1, :], sums[:, i - 1, :], e.tg[:, 1:2], e.x[:, i - 1, :], ALU.mult, ALU.add).then_inc(x_new, 1)
                if i >= 2:
                    dve.wait_ge(x_new, i - 1)
                    v.bn_stats(e.stats[:, i - 2, :], e.x[:, i - 2, :])


def flamingo_block(nc, out, **inputs):
    with ExitStack() as ctx:
        e = make_env(nc, ctx, inputs, out)
        attention_buffers(e)
        for stage, *args in ((prepare,), (depool_mixer,), (router, 0), (route, 0), (experts0,), (combine, 0)):
            stage(e, *args)
        nc.clear_and_free_semaphores(e.used)
        nc.all_engine_barrier()
        e.used = []
        for stage, *args in ((project_qkv,), (attend,), (project_out,), (router, 1), (route, 1), (experts1,), (combine, 1)):
            stage(e, *args)


NAMES = ("x", "ctx_2048", "mask_BxS2_if0", "g_xattn", "g_ffn", "L0_xattn_W_in", "L0_xattn_b_in", "L0_xattn_g_res", "L0_xattn_g_init",
         "L0_ffn_Wr", "L0_ffn_br", "L0_ffn_W1", "L0_ffn_b1", "L0_ffn_W2", "L0_ffn_b2", "L1_xattn_w_qkv", "L1_xattn_w_proj",
         "L1_xattn_b_proj", "L1_ffn_gate_w", "L1_ffn_w1", "L1_ffn_w3", "L1_ffn_w2", "L1_ffn_e_bias")


def kernel(**inputs):
    import concourse.bacc as bacc
    from concourse.bass_utils import run_bass_kernel_spmd

    nc = bacc.Bacc("TRN2", target_bir_lowering=False, num_devices=1)
    arrays = {"in_" + n: np.ascontiguousarray(inputs[n]) for n in NAMES}
    aps = {n: nc.dram_tensor("in_" + n, arrays["in_" + n].shape, mybir.dt.from_np(arrays["in_" + n].dtype), kind="ExternalInput").ap() for n in NAMES}
    out = nc.dram_tensor("out", (B, S, D), F32, kind="ExternalOutput").ap()
    flamingo_block(nc, out, **aps)
    return run_bass_kernel_spmd(nc, [arrays], core_ids=[0]).results[0]["out"]
```
